# Optimizing a Trainium2 kernel written in Bass

```python
import numpy as np
import jax
import jax.numpy as jnp

def _softmax(x, axis=-1):
    return jax.nn.softmax(x, axis=axis)

def _gelu(x):
    return jax.nn.gelu(x, approximate=True)

def _silu(x):
    return jax.nn.silu(x)

def _sigmoid(x):
    return jax.nn.sigmoid(x)

def _layernorm(x, axis=-1, eps=1e-05):
    m = jnp.mean(x, axis=axis, keepdims=True)
    v = jnp.var(x, axis=axis, keepdims=True)
    return (x - m) / jnp.sqrt(v + eps)

def _scatter_add(tgt, idx, src, axis=0):
    return tgt.at[idx].add(src)

def _segment_sum(src, seg, n):
    return jax.ops.segment_sum(src, seg, n)
kernel_name = 'mk_metaformer_d4_conv_nchw256_r4_1cf09a'

def setup_inputs(seed: int=0):
    np.random.seed(seed)
    _w = jnp.asarray

    def _rec_inputs():
        import jax
        import jax.numpy as jnp
        _gk = jax.random.key(seed)
        x = -0.0003929 + 0.9999 * jax.random.normal(jax.random.fold_in(_gk, 1), (16, 64, 16, 16), jnp.float32)
        return x
    x = _rec_inputs()

    def _L0_conv_setup():
        import jax, jax.numpy as jnp
        import numpy as np
        EPS = 1e-12

        def l2norm(x, axis):
            n = jnp.sqrt(jnp.sum(x * x, axis=axis, keepdims=True))
            return x / jnp.maximum(n, EPS)

        def conv2d(x, w, b, pad):
            y = jax.lax.conv_general_dilated(x, w, (1, 1), [(pad, pad), (pad, pad)], dimension_numbers=('NCHW', 'OIHW', 'NCHW'))
            return y + b[None, :, None, None]
        key = jax.random.key(seed)
        ks = jax.random.split(key, 12)
        N, C, H, W, K = (16, 64, 16, 16, 32)
        s = 0.05
        return {'feature': jax.random.normal(ks[0], (N, C, H, W), jnp.float32), 'conv_up_w': jax.random.normal(ks[1], (K, C, 3, 3), jnp.float32) * s, 'conv_up_b': jax.random.normal(ks[2], (K,), jnp.float32) * s, 'centroids': jax.random.uniform(ks[3], (K, C), jnp.float32), 'upfc_w': jax.random.normal(ks[4], (C, K * C), jnp.float32) * s, 'upfc_b': jax.random.normal(ks[5], (C,), jnp.float32) * s, 't1_w': jax.random.normal(ks[6], (C, 2 * C, 1, 1), jnp.float32) * s, 't1_b': jax.random.normal(ks[7], (C,), jnp.float32) * s, 't2_w': jax.random.normal(ks[8], (C, C, 1, 1), jnp.float32) * s, 't2_b': jax.random.normal(ks[9], (C,), jnp.float32) * s}
    _L0_conv_all = _L0_conv_setup()
    _L0_conv_in = {k: v for k, v in _L0_conv_all.items() if k in ('conv_up_w', 'conv_up_b', 'centroids', 'upfc_w', 'upfc_b', 't1_w', 't1_b', 't2_w', 't2_b')}
    del _L0_conv_all

    def _L0_ffn_setup():
        import jax, jax.numpy as jnp
        import numpy as np
        B, S, D = (8, 1024, 64)
        H = 4 * D
        CAPACITY = 0.5
        key = jax.random.key(seed)
        ks = jax.random.split(key, 6)
        x = jax.random.normal(ks[0], (B, S, D), dtype=jnp.float32)
        attention_mask = jnp.zeros((B, 1, 1, S), dtype=jnp.float32)
        wr = jax.random.normal(ks[1], (D, 1), dtype=jnp.float32) * 0.02
        br = jnp.zeros((1,), dtype=jnp.float32)
        w1 = jax.random.normal(ks[2], (D, H), dtype=jnp.float32) * 0.02
        b1 = jnp.zeros((H,), dtype=jnp.float32)
        w2 = jax.random.normal(ks[3], (H, D), dtype=jnp.float32) * 0.02
        b2 = jnp.zeros((D,), dtype=jnp.float32)
        return {'x': x, 'attention_mask': attention_mask, 'wr': wr, 'br': br, 'w1': w1, 'b1': b1, 'w2': w2, 'b2': b2}
    _L0_ffn_all = _L0_ffn_setup()
    _L0_ffn_in = {k: v for k, v in _L0_ffn_all.items() if k in ('attention_mask', 'wr', 'br', 'w1', 'b1', 'w2', 'b2')}
    del _L0_ffn_all

    def _L1_conv_setup():
        import jax, jax.numpy as jnp
        import numpy as np
        IN_PLANES = 64
        B, C, H, W = (16, 64, 56, 56)
        key = jax.random.key(seed)
        k_x, k1, k2, k3, k4 = jax.random.split(key, 5)
        x = jax.random.normal(k_x, (B, C, H, W), dtype=jnp.float32)
        w1 = jax.random.normal(k1, (C // 2, C), dtype=jnp.float32) * (1.0 / np.sqrt(C))
        w2 = jax.random.normal(k2, (C, C // 2), dtype=jnp.float32) * (1.0 / np.sqrt(C // 2))
        w_enc = jax.random.normal(k3, (1, C), dtype=jnp.float32) * (1.0 / np.sqrt(C))
        b_enc = jax.random.normal(k4, (1,), dtype=jnp.float32) * 0.01
        return {'x': x, 'w1': w1, 'w2': w2, 'w_enc': w_enc, 'b_enc': b_enc}
    _L1_conv_all = _L1_conv_setup()
    _L1_conv_in = {k: v for k, v in _L1_conv_all.items() if k in ('w1', 'w2', 'w_enc', 'b_enc')}
    del _L1_conv_all

    def _L1_ffn_setup():
        import jax, jax.numpy as jnp
        import numpy as np
        D_MODEL = 64
        N_EXPERTS = 16
        HIDDEN = 128
        SCALE = 0.02
        key = jax.random.key(seed)
        ks = jax.random.split(key, 5)
        x = jax.random.normal(ks[0], (4, 2048, D_MODEL), dtype=jnp.float32)
        gate_w = jax.random.normal(ks[1], (D_MODEL, N_EXPERTS), dtype=jnp.float32) * SCALE
        gate_b = jnp.zeros((N_EXPERTS,), dtype=jnp.float32)
        w1 = jax.random.normal(ks[2], (N_EXPERTS, D_MODEL, HIDDEN), dtype=jnp.float32) * SCALE
        w2 = jax.random.normal(ks[3], (N_EXPERTS, D_MODEL, HIDDEN), dtype=jnp.float32) * SCALE
        w3 = jax.random.normal(ks[4], (N_EXPERTS, HIDDEN, D_MODEL), dtype=jnp.float32) * SCALE
        return {'x': x, 'gate_w': gate_w, 'gate_b': gate_b, 'w1': w1, 'w2': w2, 'w3': w3}
    _L1_ffn_all = _L1_ffn_setup()
    _L1_ffn_in = {k: v for k, v in _L1_ffn_all.items() if k in ('gate_w', 'gate_b', 'w1', 'w2', 'w3')}
    del _L1_ffn_all

    def _L2_conv_setup():
        import jax, jax.numpy as jnp
        import numpy as np
        from jax import lax
        HEADS = 8
        DIM_HEAD = 16
        SCALE = DIM_HEAD ** (-0.5)

        def _to_heads(t, B, h, dh, HW):
            return t.reshape(B, h, dh, HW).transpose(0, 1, 3, 2).reshape(B * h, HW, dh)
        key = jax.random.key(seed)
        ks = jax.random.split(key, 6)
        B, C, H, W = (8, 64, 16, 16)
        inner = HEADS * DIM_HEAD
        fmap = jax.random.normal(ks[0], (B, C, H, W), dtype=jnp.float32)
        wq = jax.random.normal(ks[1], (inner, C), dtype=jnp.float32) * (1.0 / np.sqrt(C))
        wdw = jax.random.normal(ks[2], (C, 1, 3, 3), dtype=jnp.float32) * (1.0 / 3.0)
        wpw = jax.random.normal(ks[3], (2 * inner, C), dtype=jnp.float32) * (1.0 / np.sqrt(C))
        wout = jax.random.normal(ks[4], (C, inner), dtype=jnp.float32) * (1.0 / np.sqrt(inner))
        bout = jnp.zeros((C,), dtype=jnp.float32)
        return {'fmap': fmap, 'wq': wq, 'wdw': wdw, 'wpw': wpw, 'wout': wout, 'bout': bout}
    _L2_conv_all = _L2_conv_setup()
    _L2_conv_in = {k: v for k, v in _L2_conv_all.items() if k in ('wq', 'wdw', 'wpw', 'wout', 'bout')}
    del _L2_conv_all

    def _L2_ffn_setup():
        import jax, jax.numpy as jnp
        import numpy as np
        TOP_K = 2
        LN_EPS = 1e-05
        key = jax.random.key(seed)
        ks = jax.random.split(key, 8)
        B, S, D, E, H = (16, 256, 64, 8, 256)
        x = jax.random.normal(ks[0], (B, S, D), dtype=jnp.float32)
        Wr = jax.random.normal(ks[1], (D, E), dtype=jnp.float32) * 0.1
        br = jnp.zeros((E,), dtype=jnp.float32)
        ln_g = jnp.ones((E, D), dtype=jnp.float32)
        ln_b = jnp.zeros((E, D), dtype=jnp.float32)
        W1 = jax.random.normal(ks[2], (E, D, H), dtype=jnp.float32) * (1.0 / np.sqrt(D))
        b1 = jnp.zeros((E, H), dtype=jnp.float32)
        W2 = jax.random.normal(ks[3], (E, H, D), dtype=jnp.float32) * (1.0 / np.sqrt(H))
        b2 = jnp.zeros((E, D), dtype=jnp.float32)
        return {'x': x, 'Wr': Wr, 'br': br, 'ln_g': ln_g, 'ln_b': ln_b, 'W1': W1, 'b1': b1, 'W2': W2, 'b2': b2}
    _L2_ffn_all = _L2_ffn_setup()
    _L2_ffn_in = {k: v for k, v in _L2_ffn_all.items() if k in ('Wr', 'br', 'ln_g', 'ln_b', 'W1', 'b1', 'W2', 'b2')}
    del _L2_ffn_all

    def _L3_conv_setup():
        import jax, jax.numpy as jnp
        import numpy as np
        QMAX = 7.0
        SCALING_MIN_VAL = 2e-16

        def fake_quant_weight_per_channel(w):
            amax = jnp.max(jnp.abs(w), axis=(1, 2, 3), keepdims=True)
            scale = jnp.maximum(amax / QMAX, SCALING_MIN_VAL)
            wq = jnp.clip(jnp.round(w / scale), -QMAX, QMAX) * scale
            return w + jax.lax.stop_gradient(wq - w)
        key = jax.random.key(seed)
        kx, kw = jax.random.split(key)
        x = jax.random.normal(kx, (32, 64, 56, 56), dtype=jnp.float32)
        w = jax.random.normal(kw, (64, 64, 3, 3), dtype=jnp.float32) * 0.05
        return {'x': x, 'w': w}
    _L3_conv_all = _L3_conv_setup()
    _L3_conv_in = {k: v for k, v in _L3_conv_all.items() if k in ('w',)}
    del _L3_conv_all

    def _L3_ffn_setup():
        import math
        import jax, jax.numpy as jnp
        import numpy as np
        CAPACITY_FACTOR = 1.25
        TOP_K = 2
        LN_EPS = 1e-05

        def _layer_norm(x, gamma, beta):
            mu = jnp.mean(x, axis=-1, keepdims=True)
            var = jnp.var(x, axis=-1, keepdims=True)
            return (x - mu) * jax.lax.rsqrt(var + LN_EPS) * gamma + beta
        key = jax.random.key(seed)
        ks = jax.random.split(key, 4)
        B, S, D, F, E = (8, 1024, 64, 128, 8)
        x = jax.random.normal(ks[0], (B, S, D), dtype=jnp.float32)
        Wr = jax.random.normal(ks[1], (D, E), dtype=jnp.float32) / np.sqrt(D)
        br = jnp.zeros((E,), jnp.float32)
        W1 = jax.random.normal(ks[2], (E, D, F), dtype=jnp.float32) / np.sqrt(D)
        b1 = jnp.zeros((E, F), jnp.float32)
        W2 = jax.random.normal(ks[3], (E, F, D), dtype=jnp.float32) / np.sqrt(F)
        b2 = jnp.zeros((E, D), jnp.float32)
        gamma = jnp.ones((D,), jnp.float32)
        beta = jnp.zeros((D,), jnp.float32)
        return {'x': x, 'Wr': Wr, 'br': br, 'W1': W1, 'b1': b1, 'W2': W2, 'b2': b2, 'gamma': gamma, 'beta': beta}
    _L3_ffn_all = _L3_ffn_setup()
    _L3_ffn_in = {k: v for k, v in _L3_ffn_all.items() if k in ('Wr', 'br', 'W1', 'b1', 'W2', 'b2', 'gamma', 'beta')}
    del _L3_ffn_all
    return {'x': x, 'L0_conv_conv_up_w': _L0_conv_in['conv_up_w'], 'L0_conv_conv_up_b': _L0_conv_in['conv_up_b'], 'L0_conv_centroids': _L0_conv_in['centroids'], 'L0_conv_upfc_w': _L0_conv_in['upfc_w'], 'L0_conv_upfc_b': _L0_conv_in['upfc_b'], 'L0_conv_t1_w': _L0_conv_in['t1_w'], 'L0_conv_t1_b': _L0_conv_in['t1_b'], 'L0_conv_t2_w': _L0_conv_in['t2_w'], 'L0_conv_t2_b': _L0_conv_in['t2_b'], 'L0_ffn_attention_mask': _L0_ffn_in['attention_mask'], 'L0_ffn_wr': _L0_ffn_in['wr'], 'L0_ffn_br': _L0_ffn_in['br'], 'L0_ffn_w1': _L0_ffn_in['w1'], 'L0_ffn_b1': _L0_ffn_in['b1'], 'L0_ffn_w2': _L0_ffn_in['w2'], 'L0_ffn_b2': _L0_ffn_in['b2'], 'L1_conv_w1': _L1_conv_in['w1'], 'L1_conv_w2': _L1_conv_in['w2'], 'L1_conv_w_enc': _L1_conv_in['w_enc'], 'L1_conv_b_enc': _L1_conv_in['b_enc'], 'L1_ffn_gate_w': _L1_ffn_in['gate_w'], 'L1_ffn_gate_b': _L1_ffn_in['gate_b'], 'L1_ffn_w1': _L1_ffn_in['w1'], 'L1_ffn_w2': _L1_ffn_in['w2'], 'L1_ffn_w3': _L1_ffn_in['w3'], 'L2_conv_wq': _L2_conv_in['wq'], 'L2_conv_wdw': _L2_conv_in['wdw'], 'L2_conv_wpw': _L2_conv_in['wpw'], 'L2_conv_wout': _L2_conv_in['wout'], 'L2_conv_bout': _L2_conv_in['bout'], 'L2_ffn_Wr': _L2_ffn_in['Wr'], 'L2_ffn_br': _L2_ffn_in['br'], 'L2_ffn_ln_g': _L2_ffn_in['ln_g'], 'L2_ffn_ln_b': _L2_ffn_in['ln_b'], 'L2_ffn_W1': _L2_ffn_in['W1'], 'L2_ffn_b1': _L2_ffn_in['b1'], 'L2_ffn_W2': _L2_ffn_in['W2'], 'L2_ffn_b2': _L2_ffn_in['b2'], 'L3_conv_w': _L3_conv_in['w'], 'L3_ffn_Wr': _L3_ffn_in['Wr'], 'L3_ffn_br': _L3_ffn_in['br'], 'L3_ffn_W1': _L3_ffn_in['W1'], 'L3_ffn_b1': _L3_ffn_in['b1'], 'L3_ffn_W2': _L3_ffn_in['W2'], 'L3_ffn_b2': _L3_ffn_in['b2'], 'L3_ffn_gamma': _L3_ffn_in['gamma'], 'L3_ffn_beta': _L3_ffn_in['beta']}

def reference(x, L0_conv_conv_up_w, L0_conv_conv_up_b, L0_conv_centroids, L0_conv_upfc_w, L0_conv_upfc_b, L0_conv_t1_w, L0_conv_t1_b, L0_conv_t2_w, L0_conv_t2_b, L0_ffn_attention_mask, L0_ffn_wr, L0_ffn_br, L0_ffn_w1, L0_ffn_b1, L0_ffn_w2, L0_ffn_b2, L1_conv_w1, L1_conv_w2, L1_conv_w_enc, L1_conv_b_enc, L1_ffn_gate_w, L1_ffn_gate_b, L1_ffn_w1, L1_ffn_w2, L1_ffn_w3, L2_conv_wq, L2_conv_wdw, L2_conv_wpw, L2_conv_wout, L2_conv_bout, L2_ffn_Wr, L2_ffn_br, L2_ffn_ln_g, L2_ffn_ln_b, L2_ffn_W1, L2_ffn_b1, L2_ffn_W2, L2_ffn_b2, L3_conv_w, L3_ffn_Wr, L3_ffn_br, L3_ffn_W1, L3_ffn_b1, L3_ffn_W2, L3_ffn_b2, L3_ffn_gamma, L3_ffn_beta):
    import jax
    import jax.numpy as jnp

    def _L0_conv_ref(feature, conv_up_w, conv_up_b, centroids, upfc_w, upfc_b, t1_w, t1_b, t2_w, t2_b):
        import jax, jax.numpy as jnp
        import numpy as np
        EPS = 1e-12

        def l2norm(x, axis):
            n = jnp.sqrt(jnp.sum(x * x, axis=axis, keepdims=True))
            return x / jnp.maximum(n, EPS)

        def conv2d(x, w, b, pad):
            y = jax.lax.conv_general_dilated(x, w, (1, 1), [(pad, pad), (pad, pad)], dimension_numbers=('NCHW', 'OIHW', 'NCHW'))
            return y + b[None, :, None, None]
        N, C, H, W = feature.shape
        K = centroids.shape[0]
        xn = l2norm(feature, axis=1)
        sa = jax.nn.softmax(conv2d(xn, conv_up_w, conv_up_b, 1), axis=1)
        sa_flat = sa.reshape(N, K, H * W)
        x_flat = xn.reshape(N, C, H * W)
        up = jnp.einsum('nkl,ncl->nkc', sa_flat, x_flat) - jnp.sum(sa_flat, axis=-1)[:, :, None] * centroids[None]
        up = l2norm(up, axis=2).reshape(N, K * C)
        up = l2norm(up, axis=1)
        up = up @ upfc_w.T + upfc_b
        up_map = jnp.broadcast_to(up[:, :, None, None], (N, C, H, W))
        nf = jnp.concatenate([feature, up_map], axis=1)
        h = jax.nn.relu(conv2d(nf, t1_w, t1_b, 0))
        return jax.nn.relu(conv2d(h, t2_w, t2_b, 0))

    def _L0_ffn_ref(x, attention_mask, wr, br, w1, b1, w2, b2):
        import jax, jax.numpy as jnp
        import numpy as np
        B, S, D = (8, 1024, 64)
        H = 4 * D
        CAPACITY = 0.5
        b, s, d = x.shape
        weights = (jnp.einsum('bsd,do->bso', x, wr) + br)[..., 0]
        k = max(1, int(CAPACITY * s))
        kk = k - 1 if k > 1 else 1
        _, idx = jax.lax.top_k(weights, k)
        sel_idx = idx[:, :kk]
        sel = jnp.take_along_axis(x, sel_idx[:, :, None], axis=1)
        h = jax.nn.gelu(jnp.einsum('bkd,dh->bkh', sel, w1) + b1)
        y = jnp.einsum('bkh,hd->bkd', h, w2) + b2
        w_sel = jnp.take_along_axis(weights, sel_idx, axis=1)
        y = y * w_sel[..., None]
        batch_idx = jnp.arange(b)[:, None]
        processed = jnp.zeros_like(x).at[batch_idx, sel_idx].set(y)
        return processed + x

    def _L1_conv_ref(x, w1, w2, w_enc, b_enc):
        import jax, jax.numpy as jnp
        import numpy as np
        IN_PLANES = 64
        B, C, H, W = (16, 64, 56, 56)
        x01 = x[:, :, 0::2, :] * 0.5
        x02 = x[:, :, 1::2, :] * 0.5
        x1 = x01[:, :, :, 0::2]
        x2 = x02[:, :, :, 0::2]
        x3 = x01[:, :, :, 1::2]
        x4 = x02[:, :, :, 1::2]
        x_LL = x1 + x2 + x3 + x4
        x_HL = -x1 - x2 + x3 + x4
        x_LH = -x1 + x2 - x3 + x4
        x_HH = x1 - x2 - x3 + x4
        bands = jnp.stack([x_LL, x_HL, x_LH, x_HH], axis=1)
        ori_y = bands.mean(axis=(3, 4))
        a1 = jax.nn.sigmoid(jnp.einsum('bkc,oc->bko', ori_y, w_enc) + b_enc)
        top_idx = jnp.argmax(a1[..., 0], axis=1)
        Q = jnp.take_along_axis(ori_y, top_idx[:, None, None], axis=1)
        y = jnp.maximum(ori_y - Q, 0.0).sum(axis=1)
        h = jnp.maximum(y @ w1.T, 0.0)
        s = jax.nn.sigmoid(h @ w2.T)
        return x * s[:, :, None, None]

    def _L1_ffn_ref(x, gate_w, gate_b, w1, w2, w3):
        import jax, jax.numpy as jnp
        import numpy as np
        D_MODEL = 64
        N_EXPERTS = 16
        HIDDEN = 128
        SCALE = 0.02
        n_experts = w1.shape[0]
        logits = jnp.einsum('bsd,de->bse', x, gate_w) + gate_b
        probs = jax.nn.softmax(logits, axis=-1)
        top_probs, top_idx = jax.lax.top_k(probs, 2)
        top_probs = top_probs / jnp.sum(top_probs, axis=-1, keepdims=True)
        dispatch = jnp.sum(jax.nn.one_hot(top_idx, n_experts, dtype=x.dtype) * top_probs[..., None], axis=-2)
        h1 = jnp.einsum('bsd,edh->bseh', x, w1)
        h2 = jnp.einsum('bsd,edh->bseh', x, w2)
        hidden = jax.nn.silu(h1) * h2
        expert_out = jnp.einsum('bseh,eho->bseo', hidden, w3)
        return jnp.einsum('bseo,bse->bso', expert_out, dispatch)

    def _L2_conv_ref(fmap, wq, wdw, wpw, wout, bout):
        import jax, jax.numpy as jnp
        import numpy as np
        from jax import lax
        HEADS = 8
        DIM_HEAD = 16
        SCALE = DIM_HEAD ** (-0.5)

        def _to_heads(t, B, h, dh, HW):
            return t.reshape(B, h, dh, HW).transpose(0, 1, 3, 2).reshape(B * h, HW, dh)
        B, C, H, W = fmap.shape
        h, dh = (HEADS, DIM_HEAD)
        HW = H * W
        q = jnp.einsum('oc,bchw->bohw', wq, fmap)
        kdw = lax.conv_general_dilated(fmap, wdw, window_strides=(1, 1), padding=[(1, 1), (1, 1)], dimension_numbers=('NCHW', 'OIHW', 'NCHW'), feature_group_count=C)
        kv = jnp.einsum('oc,bchw->bohw', wpw, kdw)
        k, v = jnp.split(kv, 2, axis=1)
        q = _to_heads(q, B, h, dh, HW)
        k = _to_heads(k, B, h, dh, HW)
        v = _to_heads(v, B, h, dh, HW)
        q = jax.nn.softmax(q, axis=-1) * SCALE
        k = jax.nn.softmax(k, axis=-2)
        context = jnp.einsum('bnd,bne->bde', k, v)
        out = jnp.einsum('bnd,bde->bne', q, context)
        out = out.reshape(B, h, HW, dh).transpose(0, 1, 3, 2).reshape(B, h * dh, H, W)
        out = jax.nn.gelu(out, approximate=False)
        return jnp.einsum('oc,bchw->bohw', wout, out) + bout[None, :, None, None]

    def _L2_ffn_ref(x, Wr, br, ln_g, ln_b, W1, b1, W2, b2):
        import jax, jax.numpy as jnp
        import numpy as np
        TOP_K = 2
        LN_EPS = 1e-05
        B, S, D = x.shape
        N = B * S
        xt = x.reshape(N, D)
        logits = xt @ Wr + br
        probs = jax.nn.softmax(logits, axis=-1)
        top_p, top_idx = jax.lax.top_k(probs, TOP_K)
        weights = top_p / top_p.sum(axis=-1, keepdims=True)
        mu = xt.mean(axis=-1, keepdims=True)
        var = ((xt - mu) ** 2).mean(axis=-1, keepdims=True)
        xn = (xt - mu) * jax.lax.rsqrt(var + LN_EPS)
        xe = xn[None, :, :] * ln_g[:, None, :] + ln_b[:, None, :]
        h = jax.nn.gelu(jnp.einsum('end,edh->enh', xe, W1) + b1[:, None, :], approximate=False)
        y = jnp.einsum('enh,ehd->end', h, W2) + b2[:, None, :]
        y_tok = jnp.transpose(y, (1, 0, 2))
        sel = jnp.take_along_axis(y_tok, top_idx[:, :, None], axis=1)
        out = (weights[:, :, None] * sel).sum(axis=1)
        return out.reshape(B, S, D)

    def _L3_conv_ref(x, w):
        import jax, jax.numpy as jnp
        import numpy as np
        QMAX = 7.0
        SCALING_MIN_VAL = 2e-16

        def fake_quant_weight_per_channel(w):
            amax = jnp.max(jnp.abs(w), axis=(1, 2, 3), keepdims=True)
            scale = jnp.maximum(amax / QMAX, SCALING_MIN_VAL)
            wq = jnp.clip(jnp.round(w / scale), -QMAX, QMAX) * scale
            return w + jax.lax.stop_gradient(wq - w)
        wq = fake_quant_weight_per_channel(w)
        return jax.lax.conv_general_dilated(x, wq, window_strides=(1, 1), padding=((1, 1), (1, 1)), dimension_numbers=('NCHW', 'OIHW', 'NCHW'))

    def _L3_ffn_ref(x, Wr, br, W1, b1, W2, b2, gamma, beta):
        import math
        import jax, jax.numpy as jnp
        import numpy as np
        CAPACITY_FACTOR = 1.25
        TOP_K = 2
        LN_EPS = 1e-05

        def _layer_norm(x, gamma, beta):
            mu = jnp.mean(x, axis=-1, keepdims=True)
            var = jnp.var(x, axis=-1, keepdims=True)
            return (x - mu) * jax.lax.rsqrt(var + LN_EPS) * gamma + beta
        B, S, D = x.shape
        E = Wr.shape[1]
        N = B * S
        K = TOP_K
        logits = jnp.mean(x, axis=1) @ Wr + br
        routing_weights = jax.nn.softmax(logits, axis=-1)
        capacity = float(math.ceil(N * CAPACITY_FACTOR / E))
        expected_loads = routing_weights.sum(axis=0) * (N / B)
        scale = jnp.where(expected_loads > capacity, capacity / expected_loads, 1.0)
        routing_weights = jax.nn.softmax(routing_weights * scale, axis=-1)
        rw_tok = jnp.broadcast_to(routing_weights[:, None, :], (B, S, E)).reshape(N, E)
        top_w, top_i = jax.lax.top_k(rw_tok, K)
        top_w = jax.nn.softmax(top_w, axis=-1)
        xf = x.reshape(N, D)
        h = jax.nn.gelu(jnp.einsum('nd,edf->enf', xf, W1) + b1[:, None, :], approximate=False)
        y = jnp.einsum('enf,efd->end', h, W2) + b2[:, None, :]
        w_dense = jnp.zeros((N, E), x.dtype).at[jnp.arange(N)[:, None], top_i].add(top_w)
        out = jnp.einsum('ne,end->nd', w_dense, y).reshape(B, S, D)
        out = _layer_norm(out + x, gamma, beta)
        return out

    def _gn(v, G=32, eps=1e-05):
        B_, C_, H_, W_ = v.shape
        g = v.reshape(B_, G, C_ // G, H_, W_)
        m = jnp.mean(g, axis=(2, 3, 4), keepdims=True)
        s = jnp.var(g, axis=(2, 3, 4), keepdims=True)
        return ((g - m) / jnp.sqrt(s + eps)).reshape(v.shape)

    def _ln_c(v, eps=1e-06):
        m = jnp.mean(v, axis=1, keepdims=True)
        s = jnp.var(v, axis=1, keepdims=True)
        return (v - m) / jnp.sqrt(s + eps)

    def _ln_t(v, eps=1e-05):
        m = jnp.mean(v, axis=-1, keepdims=True)
        s = jnp.var(v, axis=-1, keepdims=True)
        return (v - m) / jnp.sqrt(s + eps)

    def _to_tokens(v):
        B_, C_, H_, W_ = v.shape
        return v.reshape(B_, C_, H_ * W_).transpose(0, 2, 1)

    def _from_tokens(t, like):
        B_, C_, H_, W_ = like.shape
        return t.transpose(0, 2, 1).reshape(B_, C_, H_, W_)
    x = x + _L0_conv_ref(_ln_c(x), L0_conv_conv_up_w, L0_conv_conv_up_b, L0_conv_centroids, L0_conv_upfc_w, L0_conv_upfc_b, L0_conv_t1_w, L0_conv_t1_b, L0_conv_t2_w, L0_conv_t2_b)
    t = _to_tokens(x)
    t = t + _L0_ffn_ref(_ln_t(t), L0_ffn_attention_mask, L0_ffn_wr, L0_ffn_br, L0_ffn_w1, L0_ffn_b1, L0_ffn_w2, L0_ffn_b2)
    x = _from_tokens(t, x)
    x = x + _L1_conv_ref(_ln_c(x), L1_conv_w1, L1_conv_w2, L1_conv_w_enc, L1_conv_b_enc)
    t = _to_tokens(x)
    t = t + _L1_ffn_ref(_ln_t(t), L1_ffn_gate_w, L1_ffn_gate_b, L1_ffn_w1, L1_ffn_w2, L1_ffn_w3)
    x = _from_tokens(t, x)
    x = x + _L2_conv_ref(_ln_c(x), L2_conv_wq, L2_conv_wdw, L2_conv_wpw, L2_conv_wout, L2_conv_bout)
    t = _to_tokens(x)
    t = t + _L2_ffn_ref(_ln_t(t), L2_ffn_Wr, L2_ffn_br, L2_ffn_ln_g, L2_ffn_ln_b, L2_ffn_W1, L2_ffn_b1, L2_ffn_W2, L2_ffn_b2)
    x = _from_tokens(t, x)
    x = x + _L3_conv_ref(_ln_c(x), L3_conv_w)
    t = _to_tokens(x)
    t = t + _L3_ffn_ref(_ln_t(t), L3_ffn_Wr, L3_ffn_br, L3_ffn_W1, L3_ffn_b1, L3_ffn_W2, L3_ffn_b2, L3_ffn_gamma, L3_ffn_beta)
    x = _from_tokens(t, x)
    return x

_drawn_inputs = setup_inputs


def setup_inputs(seed=0):
    import zlib

    import numpy as np

    out = dict(_drawn_inputs(seed))
    spreads = {'L0_ffn_b1': (0.0, 0.8),
     'L0_ffn_b2': (0.0, 0.77),
     'L1_ffn_gate_b': (0.0, 0.8),
     'L2_conv_bout': (0.0, 0.8),
     'L2_ffn_br': (0.0, 0.8),
     'L2_ffn_ln_g': (1.0, 0.6),
     'L2_ffn_ln_b': (0.0, 2.0),
     'L2_ffn_b1': (0.0, 2.0),
     'L2_ffn_b2': (0.0, 2.0),
     'L3_ffn_br': (0.0, 0.8),
     'L3_ffn_b1': (0.0, 2.0),
     'L3_ffn_b2': (0.0, 2.0),
     'L3_ffn_gamma': (1.0, 0.6),
     'L3_ffn_beta': (0.0, 2.0)}
    factors = {'L0_conv_conv_up_w': 64.0,
     'L0_conv_conv_up_b': 200.0,
     'L0_conv_centroids': 6.654,
     'L0_conv_upfc_w': 5.215,
     'L0_conv_upfc_b': 5.83,
     'L0_conv_t1_b': 3.143,
     'L0_ffn_wr': 5.747,
     'L0_ffn_w1': 8.0,
     'L0_ffn_w2': 8.0,
     'L1_ffn_gate_w': 8.0,
     'L1_ffn_w1': 8.0,
     'L1_ffn_w2': 8.0,
     'L1_ffn_w3': 8.0,
     'L2_conv_wq': 8.0,
     'L2_conv_wdw': 5.696,
     'L2_conv_wpw': 5.531,
     'L2_conv_wout': 5.417,
     'L2_ffn_Wr': 3.371,
     'L2_ffn_W1': 3.531,
     'L2_ffn_W2': 3.027,
     'L3_ffn_Wr': 3.71,
     'L3_ffn_W1': 4.476,
     'L3_ffn_W2': 3.895}
    for name, (base, spread) in spreads.items():
        noise = np.random.default_rng([zlib.crc32(name.encode()), seed]).standard_normal(out[name].shape)
        drawn = base * np.exp(spread * noise) if base else spread * noise
        out[name] = jnp.asarray(drawn.astype(out[name].dtype))
    for name, factor in factors.items():
        out[name] = (out[name] * factor).astype(out[name].dtype)
    return out
```

```python
from contextlib import ExitStack

import concourse.bass as bass
from concourse import mybir

F32 = mybir.dt.float32
F32R = mybir.dt.float32r
I32 = mybir.dt.int32
U32 = mybir.dt.uint32
ALU = mybir.AluOpType
ACT = mybir.ActivationFunctionType
X_AXIS = mybir.AxisListType.X

P = 128
B, C, H, W = 16, 64, 16, 16
PIX = H * W
TOK = B * PIX
NT = TOK // P
G = 4
TG = NT // G
BG = B // G
QG = BG // 2
CHUNK = 512
NCHUNK = TOK // CHUNK
PADW = W + 2
PADPIX = (H + 2) * PADW
K0 = 32
FFN0 = 256
TOPK0 = PIX // 2 - 1
E1, H1 = 16, 128
E2, H2 = 8, 256
E3, H3 = 8, 128
LAST = 8
HEADS, DH = 8, 16
INNER = HEADS * DH


def build(nc, a, out, stop=99):
    ctx = ExitStack()
    with ctx:
        SIZE = dict(all=75 * 1024, early=79 * 1024, gated=52 * 1024)
        BASE = dict(all=(nc.sbuf_base + 31) // 32 * 32)
        BASE["early"] = BASE["all"] + SIZE["all"]
        BASE["gated"] = BASE["early"] + SIZE["early"]
        SIZE["early"] -= 8 * 1024
        BASE["fc"] = BASE["hg"] = BASE["early"] + SIZE["early"]
        SIZE["fc"] = SIZE["hg"] = 8 * 1024
        BASE["late"], BASE["mid"] = BASE["gated"], BASE["early"]
        BASE["last"], SIZE["last"] = BASE["gated"], 45 * 1024
        SIZE["late"], SIZE["mid"] = SIZE["gated"], SIZE["early"] + SIZE["hg"]
        used = dict.fromkeys(BASE, 0)

        def sb(name, shape, dt=F32, region="all"):
            size = 4
            for d in shape[1:]:
                size *= d
            at = BASE[region] + used[region]
            used[region] += (size + 31) // 32 * 32
            assert used[region] <= SIZE[region], (name, region, used[region])
            return nc.alloc_sbuf_tensor_at(name, shape, dt, offset=at)

        def sem(name):
            return ctx.enter_context(nc.semaphore(name))

        class Signal:

            def __init__(self, handle, base):
                self.sem, self.base = handle, base

            def __call__(self, count):
                return self.sem, self.base + count

        free = []

        def signals(*counts):
            made = {}
            for total, names in counts:
                for name in names.split():
                    handle, base = free.pop(0) if free else (sem(name), 0)
                    made[name] = Signal(handle, base)
                    made[name].total = total
            return made

        def retire(made):
            free.extend((x.sem, x.base + x.total) for name, x in made.items() if name[0] != "x")

        ps = ctx.enter_context(nc.psum_tensor("ps", [P, 8, 512], F32))

        ident = sb("ident", [P, P])
        ones = sb("ones", [P, P])
        neghalf = sb("neghalf", [P, NT])
        band = sb("band", [P, 4])
        X = sb("X", [P, NT, C])
        XIN = sb("XIN", [P, B // 2, PIX])
        U = sb("U", [P, NT, C])
        Y = XIN[:, :, :].rearrange("p q s -> p (q s)").rearrange("p (t c) -> p t c", c=C)
        XC = [sb(f"XC{i}", [P, TG, C]) for i in range(2)]
        US = [sb(f"US{i}", [P, TG, 2, C], F32R) for i in range(2)]
        UT = sb("UT", [P, TOK], F32R)
        ST = sb("ST", [P, NT, 6])
        S1_ = sb("S1_", [P, NT])
        S2_ = sb("S2_", [P, NT])
        S3_ = sb("S3_", [P, NT])
        S4_ = sb("S4_", [P, NT])
        var = sb("var", [P, NT])
        vpe = sb("vpe", [P, NT])
        rstd = sb("rstd", [P, NT])
        n2 = sb("n2", [P, NT])
        n2b = sb("n2b", [P, NT])
        n2c = sb("n2c", [P, NT])
        rn = sb("rn", [P, NT])
        XP = [sb(f"XP{i}", [P, BG, PADPIX], F32R) for i in range(2)]
        XN = [sb(f"XN{i}", [P, TG, P], region="early") for i in range(2)]
        XS = [sb(f"XS{i}", [P, TG, 2, C], F32R, region="early") for i in range(2)]
        CV = [sb(f"CV{i}", [C, CHUNK], region="early") for i in range(2)]
        L = sb("L", [P, TG, K0], region="early")
        L2 = sb("L2", [P, TG, K0], region="early")
        LE = sb("LE", [P, TG, K0], region="early")
        SA = [sb(f"SA{i}", [P, TG, K0], region="early") for i in range(2)]
        R8 = [sb(f"R8_{i}", [P, TG]) for i in range(4)]
        w_cu_raw = sb("w_cu_raw", [K0, C * 9], region="early")
        w_cu_t = sb("w_cu_t", [P, 9, K0], region="early")
        w_cu = sb("w_cu", [P, 9, 2, K0], F32R, region="early")
        b_cu = sb("b_cu", [C, 1])
        cent_raw = sb("cent_raw", [K0, C], region="early")
        centT = sb("centT", [C, K0], region="early")
        fc_raw = sb("fc_raw", [C, K0 * C], region="fc")
        fcT = sb("fcT", [P, K0 // 2, C], region="early")
        b_fc = sb("b_fc", [C, 1])
        t1_raw = sb("t1_raw", [C, 2 * C], region="early")
        t1a_t = sb("t1a_t", [P, C], region="early")
        t1a = sb("t1a", [P, 2, 2, C], F32R, region="early")
        t1b = sb("t1b", [C, 2, C], region="early")
        b_t1 = sb("b_t1", [P, 1])
        t2_raw = sb("t2_raw", [C, C], region="early")
        t2_t = sb("t2_t", [P, C], region="early")
        t2 = sb("t2", [P, 2, C], F32R, region="early")
        b_t2 = sb("b_t2", [P, C], region="early")
        EC = [sb(f"EC{i}", [C, B, K0], region="early") for i in range(4)]
        tb = [sb(f"tb{i}", [C, B], region="early") for i in range(4)]
        upn2 = sb("upn2", [P, K0 // 2, B], region="early")
        upv = sb("upv", [C, B], region="early")
        V = sb("V", [P, B], region="early")
        HR = [sb(f"HR{i}", [P, CHUNK], region="early") for i in range(2)]
        HS = [sb(f"HS{i}", [P, CHUNK], F32R, region="early") for i in range(2)]
        OT = [sb(f"OT{i}", [P, TG, C], region="early") for i in range(2)]

        wr0 = sb("wr0", [P, C], region="early")
        br0 = sb("br0", [P, 1])
        f1_raw = sb("f1_raw", [P, FFN0], region="early")
        f1 = sb("f1", [P, 2, FFN0], F32R, region="early")
        b_f1 = sb("b_f1", [P, 2])
        f2 = sb("f2", [P, 2, C], region="early")
        b_f2 = sb("b_f2", [P, C], region="early")
        wl = sb("wl", [P, 2, B], region="early")
        wm = sb("wm", [P, NT])
        tk = sb("tk", [B, PIX + 1], region="early")
        m8 = sb("m8", [B, 8], region="early")
        HG = [sb(f"HG{i}", [P, 2, CHUNK], region="hg") for i in range(2)]
        YT = [sb(f"YT{i}", [C, CHUNK], region="early") for i in range(2)]
        rev = sb("rev", [P, 16])
        pidx = sb("pidx", [P, 1], I32)
        pbit = [sb(f"pbit{i}", [P, 1], I32) for i in range(3)]
        wenc = sb("wenc", [C, 1])
        wencb = sb("wencb", [C, C])
        b_enc = sb("b_enc", [C, 1])
        l1w1_raw = sb("l1w1_raw", [C // 2, C])
        l1w2_raw = sb("l1w2_raw", [C, C // 2])
        l1w1T = sb("l1w1T", [C, C // 2])
        l1w2T = sb("l1w2T", [C // 2, C])
        ori = sb("ori", [C, B, 4], region="mid")
        ba = [sb(f"ba{i}", [C, B, 4], region="mid") for i in range(4)]
        bs = [sb(f"bs{i}", [C, B], region="mid") for i in range(4)]
        sg = sb("sg", [C, B], region="mid")
        hq = sb("hq", [C // 2, B], region="mid")

        gw = sb("gw", [P, E1])
        gw2 = sb("gw2", [P, 2, E1], F32R)
        b_gw = sb("b_gw", [P, E1])
        w12_raw = sb("w12_raw", [P, 2, E1, H1], region="gated")
        w12 = sb("w12", [P, 2, 2, E1, H1], F32R, region="gated")
        w3 = sb("w3", [P, E1, C], region="gated")
        DS = [sb(f"DS{i}", [P, TG, P], F32R, region="mid") for i in range(2)]
        DT = sb("DT", [P, TOK], F32R, region="mid")
        sel = sb("sel", [P, E1], F32R)
        self32 = sb("self32", [P, E1])
        RT = [sb(f"RT{i}", [P, TG, E1], region="mid") for i in range(8)]
        r8 = [sb(f"r8{i}", [P, TG], region="mid") for i in range(8)]
        SB = [sb(f"SB{i}", [P, CHUNK], region="mid") for i in range(2)]
        HID = [sb(f"HID{i}", [P, CHUNK], region="mid") for i in range(4)]
        HID += [US[i][:, :, :, :].rearrange("p t h c -> p (t h c)").bitcast(F32)[:, j * CHUNK:(j + 1) * CHUNK]
                for i in range(2) for j in range(2)]
        OS = sb("OS", [P, CHUNK], region="mid")
        OA = sb("OA", [P, 4, C], region="mid")

        wq_raw = sb("wq_raw", [INNER, C])
        wq_t = sb("wq_t", [P, INNER], region="mid")
        wq = sb("wq", [P, 2, INNER], F32R)
        wkv_raw = sb("wkv_raw", [INNER, 2, C])
        wkv = sb("wkv", [P, 2, INNER], region="mid")
        wo_raw = sb("wo_raw", [C, INNER])
        wo = sb("wo", [INNER, C], region="mid")
        b_o = sb("b_o", [P, C])
        dw_raw = sb("dw_raw", [P, 9])
        dw_hi = sb("dw_hi", [P, 9], F32R)
        dw_lo = sb("dw_lo", [P, 9], region="mid")
        ident2 = sb("ident2", [P, C], region="mid")
        wdw = sb("wdw", [P, 9, 2, C], F32R, region="mid")
        hmask = sb("hmask", [P, INNER], region="mid")
        QL = sb("QL", [P, TG, INNER], region="late")
        QE = sb("QE", [P, TG, INNER], region="late")
        qr = [sb(f"qr{i}", [P, TG * HEADS], region="late") for i in range(3)]
        QT = sb("QT", [INNER, TOK], region="late")
        KD = [sb(f"KD{i}", [P, CHUNK], region="late") for i in range(2)]
        KE = HID[0:2]
        KT = [sb(f"KT{i}", [P, 4, INNER], region="late") for i in range(2)]
        VT = [sb(f"VT{i}", [P, 4, INNER], region="late") for i in range(2)]
        nkm = sb("nkm", [P, B], region="mid")
        ksum = sb("ksum", [P, B], region="mid")
        rks = sb("rks", [P, B], region="mid")
        CTX = sb("CTX", [INNER, B, INNER], region="late")

        gw_6 = sb("gw_6", [P, E2])
        gw2_6 = sb("gw2_6", [P, 2, E2], F32R)
        b_gw_6 = sb("b_gw_6", [P, E2])
        gsum = sb("gsum", [P, E2])
        lng_raw = sb("lng_raw", [E2, P])
        lnb_raw = sb("lnb_raw", [E2, C])
        lng = sb("lng", [P, E2])
        lnb = sb("lnb", [C, E2])
        b1_raw = sb("b1_raw", [2 * E2, P])
        b1_6 = sb("b1_6", [P, 2 * E2])
        b1_t = sb("b1_t", [P, 2 * E2])
        b2_6 = sb("b2_6", [P, P])
        b2s = sb("b2s", [P, 2, P], F32R)
        w1_raw = sb("w1_raw", [P, E2, H2], region="mid")
        w1_6 = sb("w1_6", [P, 2, E2, H2], F32R, region="mid")
        w2_6 = sb("w2_6", [P, E2, 2, C], region="late")

        cw_raw = sb("cw_raw", [C, C * 9], region="last")
        cw_q = [sb(f"cw_q{i}", [C, C * 9], region="last") for i in range(2)]
        amax = [sb(f"amax{i}", [C, 1], region="last") for i in range(4)]
        sc_hi = sb("sc_hi", [C, 1], F32R, region="last")
        nsc = [sb(f"nsc{i}", [C, 1], region="last") for i in range(2)]
        cq_hi = sb("cq_hi", [C, C * 9], F32R, region="last")
        cq_lo = sb("cq_lo", [C, C * 9], region="last")
        cw_t = sb("cw_t", [P, 9, C], region="last")
        cw = sb("cw", [P, 9, 2, C], F32R, region="last")
        CQ = [sb(f"CQ{i}", [P, CHUNK], region="last") for i in range(2)]

        wr_8 = sb("wr_8", [C, E3], region="last")
        br_8 = sb("br_8", [B, E3], region="last")
        gam = sb("gam", [P, C], region="last")
        bet = sb("bet", [P, C], region="last")
        w1_8raw = sb("w1_8raw", [P, E3, H3], region="last")
        w1_8 = sb("w1_8", [P, E3, 2, H3], F32R, region="last")
        w2_8 = sb("w2_8", [P, E3, C], region="last")
        b1_8 = sb("b1_8", [E3, H3], region="last")
        b2_8 = sb("b2_8", [E3, C], region="last")
        mean8 = sb("mean8", [C, B], region="last")
        im = [sb(f"im{i}", [B, E3], region="last") for i in range(8)]
        i1 = [sb(f"i1_{i}", [B, 1], region="last") for i in range(4)]
        hot = sb("hot", [B, 2, E3], region="last")
        iw = sb("iw", [B, 2, 2], region="last")
        dia = sb("dia", [B, B, 2, 2], region="last")
        hotT = sb("hotT", [E3, 2, B], region="last")
        dwT = sb("dwT", [E3, B], region="last")
        idx = sb("idx", [P, 2 * B], I32, region="last")
        wsel = sb("wsel", [P, 2 * B], region="last")
        b1u = sb("b1u", [P, 2, B], region="last")
        b2u = sb("b2u", [P, B // 2], region="last")
        W1S = [sb(f"W1S{i}", [P, 2, H3], F32R, region="last") for i in range(2)]
        W2S = [sb(f"W2S{i}", [P, C], region="last") for i in range(2)]
        GH = [sb(f"GH{i}", [P, PIX], region="last") for i in range(2)]
        YS = sb("YS", [P, PIX], region="last")

        chain = {e: [sem(f"chain_{e}"), 0] for e in ("vector", "scalar", "gpsimd", "tensor")}

        def link(eng, name, ins):
            c = chain[name]
            c[1] += 1
            ins.then_inc(c[0], 1)
            eng.wait_ge(c[0], c[1])

        vlink = lambda ins: link(nc.vector, "vector", ins)
        alink = lambda ins: link(nc.scalar, "scalar", ins)
        plink = lambda ins: link(nc.gpsimd, "gpsimd", ins)

        def bc(ap, n):
            return ap.unsqueeze(2).to_broadcast([ap.shape[0], ap.shape[1], n])

        def bcm(ap, n):
            return ap.unsqueeze(1).to_broadcast([ap.shape[0], n, ap.shape[1]])

        s = {n: sem(n) for n in """x_in consts w_small xt_ps xt_done""".split()}
        w_loaded = {}

        def wdma(eng, key, dst, src):
            if key not in w_loaded:
                w_loaded[key] = [sem("w_" + key), 0]
            w_loaded[key][1] += 16
            with nc.allow_non_contiguous_dma(reason="small weights"):
                eng.dma_start(dst, src).then_inc(w_loaded[key][0], 16)

        def wwait(eng, key):
            eng.wait_ge(w_loaded[key][0], w_loaded[key][1])


        def load_sync(sp):
            sp.dma_start(XIN[:, :, :], a["x"].rearrange("(q r) c h w -> (r c) q (h w)", r=2)).then_inc(s["x_in"], 16)
            wdma(sp, "cu", w_cu_raw[:, :], a["L0_conv_conv_up_w"].rearrange("k c h w -> k (c h w)"))
            wdma(sp, "b_cu", b_cu[0:K0, :], a["L0_conv_conv_up_b"].unsqueeze(1))
            wdma(sp, "cent", cent_raw[:, :], a["L0_conv_centroids"])
            wdma(sp, "t1", t1_raw[:, :], a["L0_conv_t1_w"].rearrange("o c h w -> o (c h w)"))
            wdma(sp, "t2", t2_raw[:, :], a["L0_conv_t2_w"].rearrange("o c h w -> o (c h w)"))
            wdma(sp, "fc", fc_raw[:, :], a["L0_conv_upfc_w"])
            wdma(sp, "b_fc", b_fc[:, :], a["L0_conv_upfc_b"].unsqueeze(1))
            for h in range(2):
                wdma(sp, "b_t1", b_t1[h * C:(h + 1) * C, :], a["L0_conv_t1_b"].unsqueeze(1))
            wdma(sp, "b_t2", b_t2[:, :], a["L0_conv_t2_b"].unsqueeze(0).to_broadcast([P, C]))

        def consts_pool(pool):
            plink(pool.memset(ident[:, :], 0.0))
            pool.affine_select(out=ident[:, :], in_=ident[:, :], compare_op=ALU.not_equal, fill=1.0, base=0,
                               pattern=[[-1, P]], channel_multiplier=1).then_inc(s["consts"], 1)
            pool.memset(ones[:, :], 1.0).then_inc(s["consts"], 1)
            pool.memset(neghalf[:, :], -0.5).then_inc(s["consts"], 1)
            for i in range(2):
                pool.memset(XN[i][:, :, C:P], 1.0).then_inc(s["consts"], 1)
                pool.memset(XP[i][:, :, :].bitcast(F32), 0.0).then_inc(s["consts"], 1)
        NCONST = 8

        s_wt = sem("w_transposed")
        s_wc = sem("w_copied")

        def w0_tensor(pe):
            pe.wait_ge(s["consts"], NCONST)
            wwait(pe, "cu")
            wv = w_cu_raw[:, :].rearrange("k (c t) -> k t c", t=9)
            for t in range(9):
                last = pe.matmul(ps[0:C, 0, t * K0:(t + 1) * K0], wv[:, t, :], ident[0:K0, 0:K0], is_transpose=True)
            last.then_inc(s_wt, 1)
            wwait(pe, "t1"); wwait(pe, "t2"); wwait(pe, "cent"); wwait(pe, "fc")
            pe.transpose(ps[0:C, 1, 0:C], t1_raw[:, 0:C], ident[0:C, 0:C])
            pe.transpose(ps[0:C, 1, C:2 * C], t1_raw[:, C:2 * C], ident[0:C, 0:C])
            pe.transpose(ps[0:C, 1, 2 * C:3 * C], t2_raw[:, :], ident[0:C, 0:C])
            pe.transpose(ps[0:C, 1, 3 * C:3 * C + K0], cent_raw[:, :], ident[0:K0, 0:K0]).then_inc(s_wt, 1)
            for j in range(K0 // 2):
                last = pe.transpose(ps[:, 2 + j // 8, (j % 8) * C:(j % 8 + 1) * C], fc_raw[:, j * P:(j + 1) * P],
                                    ident[0:C, 0:C])
            last.then_inc(s_wt, 1)

        def w0_vector(dve):
            dve.memset(b_cu[K0:C, :], 0.0).then_inc(s["consts"], 1)
            dve.wait_ge(s_wt, 1)
            src = ps[0:C, 0, 0:9 * K0].rearrange("p (t k) -> p t k", k=K0)
            dve.tensor_copy(w_cu_t[0:C, :, :], src)
            vlink(dve.tensor_copy(w_cu_t[C:P, :, :], src))
            vlink(dve.tensor_copy(w_cu[:, :, 0, :], w_cu_t[:, :, :]))
            dve.tensor_tensor(w_cu[:, :, 1, :], w_cu_t[:, :, :], w_cu[:, :, 0, :].bitcast(F32), ALU.subtract).then_inc(s_wc, 1)
            dve.wait_ge(s_wt, 2)
            for h in range(2):
                dve.tensor_copy(t1a_t[h * C:(h + 1) * C, :], ps[0:C, 1, 0:C])
                dve.tensor_copy(t1b[:, h, :], ps[0:C, 1, C:2 * C])
                dve.tensor_copy(t2_t[h * C:(h + 1) * C, :], ps[0:C, 1, 2 * C:3 * C])
            vlink(dve.tensor_copy(centT[:, :], ps[0:C, 1, 3 * C:3 * C + K0]))
            for h in range(2):
                dve.tensor_copy(t1a[:, 0, h, :], t1a_t[:, :])
            vlink(dve.tensor_copy(t2[:, 0, :], t2_t[:, :]))
            for h in range(2):
                dve.tensor_tensor(t1a[:, 1, h, :], t1a_t[:, :], t1a[:, 0, h, :].bitcast(F32), ALU.subtract)
            dve.tensor_tensor(t2[:, 1, :], t2_t[:, :], t2[:, 0, :].bitcast(F32), ALU.subtract).then_inc(s_wc, 1)
            dve.wait_ge(s_wt, 3)
            dve.tensor_copy(fcT[:, :, :].rearrange("p j c -> p (j c)"), ps[:, 2:4, :].rearrange("p a b -> p (a b)")).then_inc(s_wc, 1)

        def xt_tensor(pe):
            pe.wait_ge(s["x_in"], 16)
            for q in range(B // 2):
                for half in range(2):
                    i = q * 2 + half
                    bank = 4 + (i // 4) % 4
                    last = pe.transpose(ps[:, bank, (i % 4) * P:(i % 4 + 1) * P],
                                        XIN[:, q, half * P:(half + 1) * P], ident[:, :])
                    if i % 4 == 3:
                        last.then_inc(s["xt_ps"], 1)

        def xt_scalar(act):
            for g in range(G):
                act.wait_ge(s["xt_ps"], g + 1)
                act.activation(X[:, g * TG:(g + 1) * TG, :].rearrange("p t c -> p (t c)"), ps[:, 4 + g, :],
                               ACT.Copy).then_inc(s["xt_done"], 1)

        def ln_stats(dve, g, src, ready):
            t0, t1_ = g * TG, (g + 1) * TG
            for t in range(TG):
                last = dve.bn_stats(ST[:, t0 + t, :], src[:, t, :])
            vlink(last)
            st = ST[:, t0:t1_, :]
            dve.tensor_tensor(S1_[:, t0:t1_], st[:, :, 1], st[:, :, 4], ALU.add)
            dve.tensor_tensor(S2_[:, t0:t1_], st[:, :, 1], st[:, :, 4], ALU.subtract)
            vlink(dve.tensor_tensor(S3_[:, t0:t1_], st[:, :, 2], st[:, :, 5], ALU.add))
            vlink(dve.scalar_tensor_tensor(S4_[:, t0:t1_], S2_[:, t0:t1_], 0.25, S2_[:, t0:t1_], ALU.mult, ALU.mult))
            dve.scalar_tensor_tensor(var[:, t0:t1_], S3_[:, t0:t1_], 1.0 / C, S4_[:, t0:t1_], ALU.mult,
                                     ALU.add).then_inc(ready.sem, 1)

        def ln_rstd(pool, g, eps, ready, done):
            t0, t1_ = g * TG, (g + 1) * TG
            pool.wait_ge(*ready(g + 1))
            plink(pool.tensor_scalar(vpe[:, t0:t1_], var[:, t0:t1_], eps, None, ALU.add))
            pool.tensor_tensor(rstd[:, t0:t1_], vpe[:, t0:t1_], neghalf[:, t0:t1_], ALU.pow).then_inc(done.sem, 1)

        def ln_center(dve, g, src, dst):
            return dve.scalar_tensor_tensor(dst, bc(S1_[:, g * TG:(g + 1) * TG], C), -0.5, src, ALU.mult, ALU.add)

        def split(dve, us, u, ready):
            vlink(dve.tensor_copy(us[:, :, 0, :], u))
            dve.tensor_tensor(us[:, :, 1, :], u, us[:, :, 0, :].bitcast(F32), ALU.subtract).then_inc(ready.sem, 1)

        def transpose_tiles(pe, us, banks, done):
            for t in range(TG):
                last = pe.transpose(ps[:, banks[t // 4], (t % 4) * P:(t % 4 + 1) * P],
                                    us[:, t, :, :].rearrange("p h c -> p (h c)").bitcast(F32), ident[:, :])
                if t % 4 == 3:
                    last.then_inc(done.sem, 1)

        def to_padded(act, bank, xp, qi, done, extra_wait=None):
            v = ps[:, bank, :].rearrange("p (h r y x) -> p h r y x", h=2, r=2, x=W)
            for half in range(2):
                dst = xp[:, 2 * qi:2 * qi + 2, :].rearrange("p r (y x) -> p r y x", x=PADW)
                last = act.activation(dst[:, :, 1 + half * 8:9 + half * 8, 1:1 + W], v[:, half, :, :, :], ACT.Copy)
            last.then_inc(done.sem, 1)

        sig1 = signals((G, "c0_var c0_rstd c0_rstd2 c0_fs c0_xs c0_lt c0_sub c0_le c0_sa c0_up"),
                       (NCHUNK, "c0_ft_ps c0_ft c0_xt_ps c0_xp c0_cv_ps c0_cv"),
                       (1, "u_sq u_n2 u_sqrt u_tot u_tsq u_upn u_fc u_upv u_v u_vd"),
                       (NCHUNK, "t_h_ps t_h t_hs t_o_ps"), (G, "t_o x1"))
        m = dict(sig1)

        def c0_pool(pool):
            for g in range(G):
                sl = slice(g * TG, (g + 1) * TG)
                ln_rstd(pool, g, 1e-6, m["c0_var"], m["c0_rstd"])
                pool.wait_ge(*m["c0_rstd"](g + 1))
                plink(pool.tensor_tensor(n2[:, sl], rstd[:, sl], rstd[:, sl], ALU.mult))
                plink(pool.tensor_tensor(n2b[:, sl], n2[:, sl], var[:, sl], ALU.mult))
                plink(pool.tensor_scalar(n2c[:, sl], n2b[:, sl], float(C), 1e-24, ALU.mult, ALU.max))
                pool.tensor_tensor(rn[:, sl], n2c[:, sl], neghalf[:, sl], ALU.pow).then_inc(m["c0_rstd2"].sem, 1)

        def c0_vector(dve):
            dve.wait_ge(s["consts"], NCONST)

            def stats(g):
                dve.wait_ge(s["xt_done"], g + 1)
                src = X[:, g * TG:(g + 1) * TG, :]
                ln_stats(dve, g, src, m["c0_var"])

            def norm(g):
                sl = slice(g * TG, (g + 1) * TG)
                src = X[:, sl, :]
                xc, us, xs, xn = XC[g % 2], US[g % 2], XS[g % 2], XN[g % 2]
                vlink(ln_center(dve, g, src, xc[:, :, :]))
                dve.wait_ge(*m["c0_rstd"](g + 1))
                vlink(dve.tensor_tensor(U[:, sl, :], xc[:, :, :], bc(rstd[:, sl], C), ALU.mult))
                if g >= 2:
                    dve.wait_ge(*m["c0_ft_ps"](2 * (g - 1)))
                split(dve, us, U[:, sl, :], m["c0_fs"])
                dve.wait_ge(*m["c0_rstd2"](g + 1))
                if g >= 2:
                    dve.wait_ge(*m["c0_up"](g - 1))
                    dve.wait_ge(*m["c0_xt_ps"](2 * (g - 1)))
                vlink(dve.tensor_tensor(xn[:, :, 0:C], U[:, sl, :], bc(rn[:, sl], C), ALU.mult))
                split(dve, xs, xn[:, :, 0:C], m["c0_xs"])

            def soft(g):
                sa = SA[g % 2]
                dve.wait_ge(*m["c0_lt"](g + 1))
                bank = ps[:, 6, :].rearrange("p (t h k) -> p t k h", t=TG, h=2)
                vlink(dve.tensor_reduce(L[:, :, :], bank, X_AXIS, ALU.add))
                vlink(dve.tensor_reduce(R8[0][:, :], L[:, :, :], X_AXIS, ALU.max))
                dve.tensor_tensor(L2[:, :, :], L[:, :, :], bc(R8[0][:, :], K0), ALU.subtract).then_inc(m["c0_sub"].sem, 1)
                dve.wait_ge(*m["c0_le"](g + 1))
                vlink(dve.tensor_reduce(R8[1][:, :], LE[:, :, :], X_AXIS, ALU.add))
                vlink(dve.reciprocal(R8[2][:, :], R8[1][:, :]))
                if g >= 2:
                    dve.wait_ge(*m["c0_up"](g - 1))
                dve.tensor_tensor(sa[:, :, :], LE[:, :, :], bc(R8[2][:, :], K0), ALU.mult).then_inc(m["c0_sa"].sem, 1)
            stats(0)
            for g in range(G):
                if g + 1 < G:
                    stats(g + 1)
                norm(g)
                if g >= 1:
                    soft(g - 1)
            soft(G - 1)

        def c0_scalar(act):
            act.wait_ge(s["consts"], NCONST)
            wwait(act, "b_cu")

            def move(g):
                for j in range(2):
                    act.wait_ge(*m["c0_ft_ps"](2 * g + j + 1))
                    act.activation(UT[:, (2 * g + j) * 512:(2 * g + j + 1) * 512], ps[:, j, :], ACT.Copy).then_inc(m["c0_ft"].sem, 1)
                if g >= 2:
                    act.wait_ge(*m["c0_cv_ps"](2 * (g - 1)))
                for j in range(2):
                    act.wait_ge(*m["c0_xt_ps"](2 * g + j + 1))
                    to_padded(act, 2 + j, XP[g % 2], j, m["c0_xp"])

            def conv_out(g):
                for j in range(2):
                    act.wait_ge(*m["c0_cv_ps"](2 * g + j + 1))
                    if g >= 1:
                        act.wait_ge(*m["c0_lt"](g))
                    act.activation(CV[j][:, :], ps[0:C, 4 + j, :], ACT.Identity, bias=b_cu[:, :]).then_inc(m["c0_cv"].sem, 1)

            def expo(g):
                act.wait_ge(*m["c0_sub"](g + 1))
                if g >= 1:
                    act.wait_ge(*m["c0_sa"](g))
                act.activation(LE[:, :, :], L2[:, :, :], ACT.Exp).then_inc(m["c0_le"].sem, 1)
            for g in range(G + 1):
                if g < G:
                    move(g)
                    conv_out(g)
                if g >= 1:
                    expo(g - 1)

        def c0_tensor(pe):
            def first(g):
                pe.wait_ge(*m["c0_fs"](g + 1))
                if g == 0:
                    pe.wait_ge(s_wc, 3)
                if g >= 1:
                    pe.wait_ge(*m["c0_ft"](2 * g))
                transpose_tiles(pe, US[g % 2], (0, 1), m["c0_ft_ps"])
                pe.wait_ge(*m["c0_xs"](g + 1))
                if g >= 1:
                    pe.wait_ge(*m["c0_xp"](2 * g))
                transpose_tiles(pe, XS[g % 2], (2, 3), m["c0_xt_ps"])

            def conv(g):
                xp = XP[g % 2][:, :, :].rearrange("p b (y x) -> p b y x", x=PADW)
                for j in range(2):
                    pe.wait_ge(*m["c0_xp"](2 * g + j + 1))
                    if g == 0:
                        pe.wait_ge(s["xt_done"], G)
                    else:
                        pe.wait_ge(*m["c0_cv"](2 * (g - 1) + j + 1))
                    for t in range(9):
                        dy, dx = t // 3, t % 3
                        last = pe.matmul(ps[0:C, 4 + j, :], w_cu[:, t, :, :].rearrange("p h k -> p (h k)"),
                                         xp[:, 2 * j:2 * j + 2, dy:dy + H, dx:dx + W], start=(t == 0), stop=(t == 8))
                    last.then_inc(m["c0_cv_ps"].sem, 1)

            def logits_t(g):
                if g >= 1:
                    pe.wait_ge(*m["c0_sub"](g))
                for j in range(2):
                    pe.wait_ge(*m["c0_cv"](2 * g + j + 1))
                    for t in range(4):
                        half, r = t // 2, t % 2
                        c0 = r * PIX + half * P
                        last = pe.transpose(ps[:, 6, (4 * j + t) * C:(4 * j + t + 1) * C], CV[j][:, c0:c0 + P],
                                            ident[0:C, 0:C])
                last.then_inc(m["c0_lt"].sem, 1)

            def pool_up(g):
                pe.wait_ge(*m["c0_sa"](g + 1))
                for j in range(2):
                    for r in range(2):
                        b = 4 * g + 2 * j + r
                        for half in range(2):
                            t = 4 * j + 2 * half + r
                            last = pe.matmul(ps[:, 7, b * K0:(b + 1) * K0], XN[g % 2][:, t, :], SA[g % 2][:, t, :],
                                             start=(half == 0), stop=(half == 1))
                last.then_inc(m["c0_up"].sem, 1)
            for g in range(G + 1):
                if g < G:
                    first(g)
                    conv(g)
                    logits_t(g)
                if g >= 1:
                    pool_up(g - 1)



        def u_vector(dve):
            e0, e1, e2, e3 = [x[:, :, :] for x in EC]
            dve.wait_ge(*m["c0_up"](G))
            dve.wait_ge(s_wc, 3)
            bank = ps[:, 7, :].rearrange("p (b k) -> p b k", k=K0)
            vlink(dve.tensor_tensor(e0, bank[C:P], bcm(centT[:, :], B), ALU.mult))
            vlink(dve.tensor_tensor(e1, bank[0:C], e0, ALU.subtract))
            dve.tensor_tensor(e2, e1, e1, ALU.mult).then_inc(m["u_sq"].sem, 1)
            dve.wait_ge(*m["u_sqrt"](1))
            vlink(dve.tensor_scalar(e0, e0, 1e-12, None, ALU.max))
            vlink(dve.reciprocal(e3, e0))
            vlink(dve.tensor_tensor(e1, e1, e3, ALU.mult))
            n2p = ps[0:C, 6, :].rearrange("p (b k) -> p b k", k=K0)
            vlink(dve.tensor_tensor(e2, e3, n2p, ALU.mult))
            vlink(dve.tensor_tensor(e2, e2, e3, ALU.mult))
            dve.tensor_reduce(tb[0][:, :], e2, X_AXIS, ALU.add).then_inc(m["u_tot"].sem, 1)
            ev = e1.rearrange("p b (k two) -> p two k b", two=2)
            dve.tensor_copy(upn2[0:C, :, :], ev[:, 0, :, :])
            dve.tensor_copy(upn2[C:P, :, :], ev[:, 1, :, :]).then_inc(m["u_upn"].sem, 1)
            dve.wait_ge(*m["u_tsq"](1))
            vlink(dve.tensor_scalar(tb[1][:, :], tb[1][:, :], 1e-12, None, ALU.max))
            vlink(dve.reciprocal(tb[2][:, :], tb[1][:, :]))
            dve.wait_ge(*m["u_fc"](1))
            wwait(dve, "b_fc")
            vlink(dve.tensor_tensor(tb[3][:, :], ps[0:C, 0, 0:B], tb[2][:, :], ALU.mult))
            dve.tensor_scalar(upv[:, :], tb[3][:, :], b_fc[:, :], None, ALU.add).then_inc(m["u_upv"].sem, 1)
            dve.wait_ge(*m["u_v"](1))
            wwait(dve, "b_t1")
            dve.tensor_scalar(V[:, :], ps[:, 1, 0:B], b_t1[:, :], None, ALU.add).then_inc(m["u_vd"].sem, 1)

        def u_scalar(act):
            act.wait_ge(*m["u_n2"](1))
            act.activation(EC[0][:, :, :].rearrange("p b k -> p (b k)"), ps[0:C, 6, :], ACT.Sqrt).then_inc(m["u_sqrt"].sem, 1)
            act.wait_ge(*m["u_tot"](1))
            act.activation(tb[1][:, :], tb[0][:, :], ACT.Sqrt).then_inc(m["u_tsq"].sem, 1)

        def u_tensor(pe):
            pe.wait_ge(*m["u_sq"](1))
            pe.matmul(ps[0:C, 6, :], ones[0:C, 0:C], EC[2][:, :, :].rearrange("p b k -> p (b k)"), start=True,
                      stop=True).then_inc(m["u_n2"].sem, 1)
            pe.wait_ge(*m["u_upn"](1))
            pe.wait_ge(*m["c0_ft"](2 * G))
            for j in range(K0 // 2):
                last = pe.matmul(ps[0:C, 0, 0:B], fcT[:, j, :], upn2[:, j, :], start=(j == 0), stop=(j == K0 // 2 - 1))
            last.then_inc(m["u_fc"].sem, 1)
            pe.wait_ge(*m["u_upv"](1))
            pe.matmul(ps[:, 1, 0:B], t1b[:, :, :].rearrange("p h c -> p (h c)"), upv[:, :], start=True,
                      stop=True).then_inc(m["u_v"].sem, 1)



        def t_tensor(pe):
            def hidden(j):
                if j >= 2:
                    pe.wait_ge(*m["t_h"](j - 1))
                else:
                    pe.wait_ge(*m["c0_xp"](2 * G))
                for part in range(2):
                    last = pe.matmul(ps[:, 2 + j % 2, :], t1a[:, part, :, :].rearrange("p h c -> p (h c)"),
                                     UT[:, j * CHUNK:(j + 1) * CHUNK], start=(part == 0), stop=(part == 1))
                last.then_inc(m["t_h_ps"].sem, 1)

            def outp(j):
                g = j // 2
                pe.wait_ge(*m["t_hs"](j + 1))
                if j % 2 == 0:
                    if g >= 2:
                        pe.wait_ge(*m["t_o"](g - 1))
                    else:
                        pe.wait_ge(*m["c0_cv"](2 * G))
                for t in range(4):
                    o = (j % 2) * 4 + t
                    for part in range(2):
                        last = pe.matmul(ps[:, 4 + g % 2, o * C:(o + 1) * C], HS[j % 2][:, t * P:(t + 1) * P],
                                         t2[:, part, :], start=(part == 0), stop=(part == 1))
                last.then_inc(m["t_o_ps"].sem, 1)
            hidden(0)
            for j in range(NCHUNK):
                if j + 1 < NCHUNK:
                    hidden(j + 1)
                outp(j)

        def t_scalar(act):
            act.wait_ge(*m["u_vd"](1))
            for j in range(NCHUNK):
                act.wait_ge(*m["t_h_ps"](j + 1))
                if j >= 2:
                    act.wait_ge(*m["t_hs"](j - 1))
                for r in range(2):
                    b = 2 * j + r
                    src = ps[:, 2 + j % 2, :].rearrange("p (h r s) -> p h r s", h=2, r=2)[:, :, r, :]
                    dst = HR[j % 2][:, :].rearrange("p (h r s) -> p h r s", h=2, r=2)[:, :, r, :]
                    last = act.activation(dst, src, ACT.Relu, bias=V[:, b:b + 1])
                last.then_inc(m["t_h"].sem, 1)

        def t_vector(dve):
            wwait(dve, "b_t2")

            def hs(j):
                dve.wait_ge(*m["t_h"](j + 1))
                if j >= 2:
                    dve.wait_ge(*m["t_o_ps"](j - 1))
                vlink(dve.tensor_copy(HS[j % 2][:, :], HR[j % 2][:, :]))
                dve.tensor_tensor(HS[j % 2][C:P, :], HR[j % 2][C:P, :], HS[j % 2][C:P, :].bitcast(F32),
                                  ALU.subtract).then_inc(m["t_hs"].sem, 1)

            def fin(g):
                sl = slice(g * TG, (g + 1) * TG)
                dve.wait_ge(*m["t_o_ps"](2 * g + 2))
                if g >= 2:
                    dve.wait_ge(*m["x1"](g - 1))
                dve.tensor_tensor(OT[g % 2][:, :, :], ps[:, 4 + g % 2, :].rearrange("p (t c) -> p t c", c=C),
                                  bcm(b_t2[:, :], TG), ALU.add).then_inc(m["t_o"].sem, 1)
                dve.wait_ge(*m["t_o"](g + 1))
                dve.scalar_tensor_tensor(X[:, sl, :], OT[g % 2][:, :, :], 0.0, X[:, sl, :], ALU.max,
                                         ALU.add).then_inc(m["x1"].sem, 1)
            for j in range(NCHUNK):
                hs(j)
                if j % 2 == 0 and j >= 2:
                    fin(j // 2 - 1)
            fin(G - 1)
        sig2 = signals((G, "f_var f_rstd f_fs f_xu f_wl f_u f_yb x2"), (NCHUNK, "f_ft_ps f_ft f_y_ps f_y f_yt_ps"),
                       (1, "f_tk_ps f_mask f_mt_ps f_wm"), (2 * NCHUNK, "f_h_ps f_h"))
        m.update(sig2)

        def f_sync(sp):
            wdma(sp, "wr0", wr0[:, :], a["L0_ffn_wr"].rearrange("d o -> o d").to_broadcast([P, C]))
            wdma(sp, "wr0", br0[:, :], a["L0_ffn_br"].unsqueeze(0).to_broadcast([P, 1]))
            for h in range(2):
                wdma(sp, "f1", f1_raw[h * C:(h + 1) * C, :], a["L0_ffn_w1"])
            wdma(sp, "f2", b_f1[:, :], a["L0_ffn_b1"].rearrange("(h p) -> p h", p=P))
            wdma(sp, "f2", f2[:, :, :], a["L0_ffn_w2"].rearrange("(h p) o -> p h o", p=P))
            wdma(sp, "b_f2", b_f2[:, :], a["L0_ffn_b2"].unsqueeze(0).to_broadcast([P, C]))

        def ln_pool(pool, eps, var_sem, rstd_sem):
            for g in range(G):
                ln_rstd(pool, g, eps, var_sem, rstd_sem)

        def ln_vector(dve, x_sem, var_sem, rstd_sem, fs_sem, ps_sem, do_split=True, extra=None, u_sem=None, x_per=1):
            def stats(g):
                dve.wait_ge(*x_sem(x_per * (g + 1)))
                ln_stats(dve, g, X[:, g * TG:(g + 1) * TG, :], var_sem)
                dve.wait_ge(*var_sem(g + 1))
            stats(0)
            for g in range(G):
                sl = slice(g * TG, (g + 1) * TG)
                if g + 1 < G:
                    stats(g + 1)
                vlink(ln_center(dve, g, X[:, sl, :], XC[g % 2][:, :, :]))
                dve.wait_ge(*rstd_sem(g + 1))
                mul = dve.tensor_tensor(U[:, sl, :], XC[g % 2][:, :, :], bc(rstd[:, sl], C), ALU.mult)
                if u_sem is None:
                    vlink(mul)
                else:
                    mul.then_inc(u_sem.sem, 1)
                    dve.wait_ge(*u_sem(g + 1))
                if do_split:
                    if g >= 2:
                        dve.wait_ge(*ps_sem(2 * (g - 1)))
                    split(dve, US[g % 2], U[:, sl, :], fs_sem)
                if extra:
                    extra(g, sl)

        def ln_tensor(pe, fs_sem, ps_sem, ft_sem, first_wait=()):
            for g in range(G):
                pe.wait_ge(*fs_sem(g + 1))
                if g >= 1:
                    pe.wait_ge(*ft_sem(2 * g))
                else:
                    for sem_, v in first_wait:
                        pe.wait_ge(*sem_(v))
                transpose_tiles(pe, US[g % 2], (0, 1), ps_sem)

        def ln_scalar(act, ps_sem, ft_sem, first_wait=()):
            for sem_, v in first_wait:
                act.wait_ge(*sem_(v))
            for j in range(NCHUNK):
                act.wait_ge(*ps_sem(j + 1))
                act.activation(UT[:, j * CHUNK:(j + 1) * CHUNK], ps[:, j % 2, :], ACT.Copy).then_inc(ft_sem.sem, 1)

        def f_pool(pool):
            ln_pool(pool, 1e-5, m["f_var"], m["f_rstd"])
            for g in range(G):
                sl = slice(g * TG, (g + 1) * TG)
                pool.wait_ge(*m["f_xu"](g + 1))
                pool.tensor_tensor(X[:, sl, :], X[:, sl, :], U[:, sl, :], ALU.add).then_inc(m["f_u"].sem, 1)

        wl_q = wl[:, :, :].rearrange("p h (q r) -> p q h r", r=2)

        def f_vector(dve):
            wwait(dve, "wr0")

            def extra(g, sl):
                vlink(dve.tensor_tensor(XC[g % 2][:, :, :], U[:, sl, :], bcm(wr0[:, :], TG), ALU.mult))
                vlink(dve.tensor_reduce(R8[0][:, :], XC[g % 2][:, :, :], X_AXIS, ALU.add))
                dve.tensor_scalar(wl_q[:, QG * g:QG * (g + 1), :, :], R8[0][:, :].rearrange("p (q h r) -> p q h r", h=2, r=2),
                                  br0[:, :], None, ALU.add).then_inc(m["f_wl"].sem, 1)
                dve.wait_ge(*m["f_wl"](g + 1))
            ln_vector(dve, x_ready1, m["f_var"], m["f_rstd"], m["f_fs"], m["f_ft_ps"], extra=extra, u_sem=m["f_xu"])
            dve.memset(tk[:, PIX:PIX + 1], 3.0e38)
            dve.wait_ge(*m["f_tk_ps"](1))
            vlink(dve.tensor_copy(tk[:, 0:PIX], ps[0:B, 7, 0:PIX]))
            for i in range((TOPK0 + 1) // 8):
                vlink(dve.max(m8[:, :], tk[:, :]))
                vlink(dve.match_replace(tk[:, :], m8[:, :], tk[:, :], -3.0e38))
            dve.tensor_scalar(tk[:, 0:PIX], tk[:, 0:PIX], -2.9e38, None, ALU.is_le).then_inc(m["f_mask"].sem, 1)
            dve.wait_ge(*m["f_mt_ps"](1))
            dve.tensor_tensor(wm[:, :].rearrange("p (q h r) -> p q h r", h=2, r=2),
                              ps[:, 7, 0:2 * B].rearrange("p (h q r) -> p q h r", h=2, r=2), wl_q, ALU.mult).then_inc(m["f_wm"].sem, 1)
            dve.wait_ge(*m["f_wm"](1))
            wwait(dve, "b_f2")
            for g in range(G):
                sl = slice(g * TG, (g + 1) * TG)
                dve.wait_ge(*m["f_yt_ps"](2 * g + 2))
                dve.wait_ge(*m["f_u"](g + 1))
                dve.tensor_tensor(Y[:, sl, :], ps[:, 6, :].rearrange("p (t c) -> p t c", c=C), bcm(b_f2[:, :], TG),
                                  ALU.add).then_inc(m["f_yb"].sem, 1)
                dve.wait_ge(*m["f_yb"](g + 1))
                vlink(dve.tensor_tensor(Y[:, sl, :], Y[:, sl, :], bc(wm[:, sl], C), ALU.mult))
                dve.tensor_tensor(X[:, sl, :], X[:, sl, :], Y[:, sl, :], ALU.add).then_inc(m["x2"].sem, 1)
        x_ready1 = m["x1"]

        def f_weights(dve):
            wwait(dve, "f1")
            vlink(dve.tensor_copy(f1[:, 0, :], f1_raw[:, :]))
            dve.tensor_tensor(f1[:, 1, :], f1_raw[:, :], f1[:, 0, :].bitcast(F32), ALU.subtract).then_inc(s_f1, 1)
        s_f1 = sem("f1_split")

        def f_scalar(act):
            ln_scalar(act, m["f_ft_ps"], m["f_ft"], [(m["t_h_ps"], NCHUNK)])
            wwait(act, "f2")

            def gelu(j):
                for hc in range(2):
                    act.wait_ge(*m["f_h_ps"](2 * j + hc + 1))
                    if j >= 2:
                        act.wait_ge(*m["f_y_ps"](j - 1))
                    act.activation(HG[j % 2][:, hc, :], ps[:, 2 + hc, :], ACT.Gelu_apprx_tanh,
                                   bias=b_f1[:, hc:hc + 1]).then_inc(m["f_h"].sem, 1)

            def move(j):
                act.wait_ge(*m["f_y_ps"](j + 1))
                if j >= 2:
                    act.wait_ge(*m["f_yt_ps"](j - 1))
                act.activation(YT[j % 2][:, :], ps[0:C, 4 + j % 2, :], ACT.Copy).then_inc(m["f_y"].sem, 1)
            for j in range(NCHUNK + 1):
                if j < NCHUNK:
                    gelu(j)
                if j >= 1:
                    move(j - 1)

        def f_tensor(pe):
            ln_tensor(pe, m["f_fs"], m["f_ft_ps"], m["f_ft"], [(m["u_vd"], 1)])
            pe.wait_ge(*m["f_wl"](G))
            for half in range(2):
                last = pe.transpose(ps[0:B, 7, half * P:(half + 1) * P], wl[:, half, :], ident[:, :])
            last.then_inc(m["f_tk_ps"].sem, 1)
            wwait(pe, "f2")
            pe.wait_ge(s_f1, 1)
            pe.wait_ge(*m["t_h"](NCHUNK))
            pe.wait_ge(*m["t_o"](G))

            def hidden(j):
                pe.wait_ge(*m["f_ft"](j + 1))
                for hc in range(2):
                    if j >= 1:
                        pe.wait_ge(*m["f_h"](2 * (j - 1) + hc + 1))
                    for part in range(2):
                        last = pe.matmul(ps[:, 2 + hc, :], f1[:, part, hc * P:(hc + 1) * P],
                                         UT[:, j * CHUNK:(j + 1) * CHUNK], start=(part == 0), stop=(part == 1))
                    last.then_inc(m["f_h_ps"].sem, 1)

            def outp(j):
                pe.wait_ge(*m["f_h"](2 * j + 2))
                if j >= 2:
                    pe.wait_ge(*m["f_y"](j - 1))
                for hc in range(2):
                    last = pe.matmul(ps[0:C, 4 + j % 2, :], f2[:, hc, :], HG[j % 2][:, hc, :], start=(hc == 0), stop=(hc == 1))
                last.then_inc(m["f_y_ps"].sem, 1)

            def back(j):
                pe.wait_ge(*m["f_y"](j + 1))
                if j >= 2 and j % 2 == 0:
                    pe.wait_ge(*m["f_yb"](j // 2))
                for t in range(4):
                    o = (j % 2) * 4 + t
                    last = pe.transpose(ps[:, 6, o * C:(o + 1) * C], YT[j % 2][:, t * P:(t + 1) * P], ident[0:C, 0:C])
                last.then_inc(m["f_yt_ps"].sem, 1)
            hidden(0)
            for j in range(NCHUNK + 1):
                if j + 1 < NCHUNK:
                    hidden(j + 1)
                if j < NCHUNK:
                    outp(j)
                if j == 1:
                    pe.wait_ge(*m["f_mask"](1))
                    for half in range(2):
                        last = pe.transpose(ps[:, 7, half * B:(half + 1) * B], tk[:, half * P:(half + 1) * P], ident[0:B, 0:B])
                    last.then_inc(m["f_mt_ps"].sem, 1)
                if j >= 1:
                    back(j - 1)

        retire(sig1)
        sig3 = signals((G, "v_var v_rstd v_u v_sb_ps x3"), (2, "v_bits v_band"),
                       (1, "v_ori_ps v_ori v_lg_ps v_a v_y v_h_ps v_h v_s_ps v_s v_w_ps v_w"))
        m.update(sig3)

        def v_sync(sp):
            wdma(sp, "wenc", wenc[:, :], a["L1_conv_w_enc"].rearrange("o c -> c o"))
            wdma(sp, "wenc", b_enc[:, :], a["L1_conv_b_enc"].unsqueeze(0).to_broadcast([C, 1]))
            wdma(sp, "l1w", l1w1_raw[:, :], a["L1_conv_w1"])
            wdma(sp, "l1w", l1w2_raw[:, :], a["L1_conv_w2"])

        def v_pool(pool):
            pool.iota(pidx[:, :], pattern=[[0, 1]], base=0, channel_multiplier=1).then_inc(m["v_bits"].sem, 1)
            pool.iota(rev[:, :], pattern=[[-1, 16]], base=16, channel_multiplier=0,
                      allow_small_or_imprecise_dtypes=True).then_inc(m["v_bits"].sem, 1)
            ln_pool(pool, 1e-6, m["v_var"], m["v_rstd"])

        def v_consts(dve):
            dve.wait_ge(*m["v_bits"](2))
            dve.tensor_scalar(pbit[0][:, :], pidx[:, :], 1, None, ALU.bitwise_and)
            vlink(dve.tensor_scalar(pbit[1][:, :], pidx[:, :], 4, None, ALU.logical_shift_right))
            vlink(dve.tensor_scalar(pbit[2][:, :], pbit[1][:, :], 1, None, ALU.bitwise_and))
            scale = 0.5 / (PIX // 4)
            dve.memset(band[:, 0:1], scale)
            dve.tensor_scalar(band[:, 1:2], pbit[0][:, :], 2 * scale, -scale, ALU.mult, ALU.add)
            vlink(dve.tensor_scalar(band[:, 2:3], pbit[2][:, :], 2 * scale, -scale, ALU.mult, ALU.add))
            dve.scalar_tensor_tensor(band[:, 3:4], band[:, 1:2], 1.0 / scale, band[:, 2:3], ALU.mult, ALU.mult).then_inc(m["v_band"].sem, 1)
            wwait(dve, "wenc")
            dve.wait_ge(s["consts"], NCONST)
            dve.tensor_scalar(wencb[:, :], ones[0:C, 0:C], wenc[:, :], None, ALU.mult).then_inc(m["v_band"].sem, 1)

        def v_vector(dve):
            dve.wait_ge(*m["v_w_ps"](1))
            dve.tensor_copy(l1w1T[:, :], ps[0:C, 7, 64:96])
            dve.tensor_copy(l1w2T[:, :], ps[0:C // 2, 7, 128:192]).then_inc(m["v_w"].sem, 1)

            ln_vector(dve, m["x2"], m["v_var"], m["v_rstd"], None, None, do_split=False, u_sem=m["v_u"])
            o = ori[:, :, :]
            dve.wait_ge(*m["v_ori_ps"](1))
            dve.tensor_copy(o.rearrange("p b k -> p (b k)"), ps[0:C, 0, 0:C]).then_inc(m["v_ori"].sem, 1)
            dve.wait_ge(*m["v_a"](1))
            A = ba[0][:, :, :]
            vlink(dve.tensor_reduce(bs[0][:, :], A, X_AXIS, ALU.max))
            vlink(dve.tensor_tensor(ba[1][:, :, :], A, bc(bs[0][:, :], 4), ALU.is_equal))
            vlink(dve.tensor_tensor(ba[2][:, :, :], ba[1][:, :, :], bcm(rev[0:C, 0:4], B), ALU.mult))
            vlink(dve.tensor_reduce(bs[1][:, :], ba[2][:, :, :], X_AXIS, ALU.max))
            vlink(dve.tensor_tensor(ba[1][:, :, :], ba[2][:, :, :], bc(bs[1][:, :], 4), ALU.is_equal))
            dve.wait_ge(*m["v_ori"](1))
            vlink(dve.tensor_tensor(ba[3][:, :, :], ba[1][:, :, :], o, ALU.mult))
            vlink(dve.tensor_reduce(bs[2][:, :], ba[3][:, :, :], X_AXIS, ALU.add))
            vlink(dve.tensor_tensor(ba[1][:, :, :], o, bc(bs[2][:, :], 4), ALU.subtract))
            vlink(dve.tensor_scalar(ba[2][:, :, :], ba[1][:, :, :], 0.0, None, ALU.max))
            dve.tensor_reduce(bs[3][:, :], ba[2][:, :, :], X_AXIS, ALU.add).then_inc(m["v_y"].sem, 1)
            dve.wait_ge(*m["v_h_ps"](1))
            dve.tensor_scalar(hq[:, :], ps[0:C // 2, 2, 0:B], 0.0, None, ALU.max).then_inc(m["v_h"].sem, 1)
            for g in range(G):
                sl = slice(g * TG, (g + 1) * TG)
                dve.wait_ge(*m["v_sb_ps"](g + 1))
                gate = ps[:, 4 + g, 0:BG * C].rearrange("p (q rc) -> p q rc", q=QG)
                gate = gate.unsqueeze(2).to_broadcast([P, QG, 2, P])
                u4 = U[:, sl, :].rearrange("p (q h r) c -> p q h (r c)", h=2, r=2)
                xc = XC[g % 2][:, :, :]
                vlink(dve.tensor_tensor(xc.rearrange("p (q h r) c -> p q h (r c)", h=2, r=2), u4, gate, ALU.mult))
                dve.tensor_tensor(X[:, sl, :], X[:, sl, :], xc, ALU.add).then_inc(m["x3"].sem, 1)

        def v_scalar(act):
            act.wait_ge(*m["v_lg_ps"](1))
            wwait(act, "wenc")
            act.activation(ba[0][:, :, :].rearrange("p b k -> p (b k)"), ps[0:C, 1, 0:C], ACT.Sigmoid,
                           bias=b_enc[:, :]).then_inc(m["v_a"].sem, 1)
            act.wait_ge(*m["v_s_ps"](1))
            act.activation(sg[:, :], ps[0:C, 3, 0:B], ACT.Sigmoid).then_inc(m["v_s"].sem, 1)

        def v_tensor(pe):
            wwait(pe, "l1w")
            pe.wait_ge(*m["f_wm"](1))
            pe.transpose(ps[0:C, 7, 64:96], l1w1_raw[:, :], ident[0:C // 2, 0:C // 2])
            pe.transpose(ps[0:C // 2, 7, 128:192], l1w2_raw[:, :], ident[0:C, 0:C]).then_inc(m["v_w_ps"].sem, 1)
            pe.wait_ge(*m["v_band"](2))
            for b in range(B):
                q, r = b // 2, b % 2
                if b % BG == 0:
                    pe.wait_ge(*m["v_u"](b // BG + 1))
                for half in range(2):
                    last = pe.matmul(ps[0:C, 0, 4 * b:4 * b + 4], U[:, 4 * q + 2 * half + r, :], band[:, :],
                                     start=(half == 0), stop=(half == 1))
            last.then_inc(m["v_ori_ps"].sem, 1)
            pe.wait_ge(*m["v_ori"](1))
            pe.matmul(ps[0:C, 1, 0:C], wencb[:, :], ori[:, :, :].rearrange("p b k -> p (b k)"), start=True,
                      stop=True).then_inc(m["v_lg_ps"].sem, 1)
            pe.wait_ge(*m["v_w"](1))
            pe.wait_ge(*m["v_y"](1))
            pe.wait_ge(*m["f_h"](2 * NCHUNK))
            pe.matmul(ps[0:C // 2, 2, 0:B], l1w1T[:, :], bs[3][:, :], start=True, stop=True).then_inc(m["v_h_ps"].sem, 1)
            pe.wait_ge(*m["v_h"](1))
            pe.matmul(ps[0:C, 3, 0:B], l1w2T[:, :], hq[:, :], start=True, stop=True).then_inc(m["v_s_ps"].sem, 1)
            pe.wait_ge(*m["v_s"](1))
            pe.wait_ge(*m["f_y"](NCHUNK))
            for b in range(B):
                last = pe.matmul(ps[:, 4 + b // BG, (b % BG) * C:(b % BG + 1) * C], sg[:, b:b + 1].to_broadcast([C, P]),
                                 ident[0:C, 0:C], start=True, stop=True)
                if b % BG == BG - 1:
                    last.then_inc(m["v_sb_ps"].sem, 1)
        def router_tensor(pe, mm, w2, ne, bank, first_wait=()):
            for sem_, v in first_wait:
                pe.wait_ge(*sem_(v))
            for g in range(G):
                pe.wait_ge(*mm["ft"](2 * g + 2))
                if g >= 1:
                    pe.wait_ge(*mm["lg"](g))
                for t in range(TG):
                    for part in range(2):
                        c0 = (g * TG + t) * P
                        last = pe.matmul(ps[:, bank, t * ne:(t + 1) * ne], UT[:, c0:c0 + P], w2[:, part, 0:ne],
                                         start=(part == 0), stop=(part == 1))
                last.then_inc(mm["lg_ps"].sem, 1)

        def router_transpose(pe, mm, banks):
            for g in range(G):
                pe.wait_ge(*mm["ds"](g + 1))
                if g >= 1:
                    pe.wait_ge(*mm["dt"](2 * g))
                for t in range(TG):
                    last = pe.transpose(ps[:, banks[t // 4], (t % 4) * P:(t % 4 + 1) * P],
                                        DS[g % 2][:, t, :].bitcast(F32), ident[:, :])
                    if t % 4 == 3:
                        last.then_inc(mm["dt_ps"].sem, 1)

        def router_logits(dve, mm, g, ne, bias, bank, rescale=None):
            rt = [x[:, :, 0:ne] for x in RT]
            dve.wait_ge(*mm["lg_ps"](g + 1))
            lp = ps[:, bank, 0:TG * ne].rearrange("p (t e) -> p t e", e=ne)
            if rescale is not None:
                lp = rescale(dve, g, lp, mm)
                vlink(dve.tensor_tensor(rt[0], lp, bcm(bias, TG), ALU.add))
            else:
                dve.tensor_tensor(rt[0], lp, bcm(bias, TG), ALU.add).then_inc(mm["lg"].sem, 1)
                dve.wait_ge(*mm["lg"](g + 1))
            vlink(dve.tensor_reduce(r8[0][:, :], rt[0], X_AXIS, ALU.max))
            dve.tensor_tensor(rt[1], rt[0], bc(r8[0][:, :], ne), ALU.subtract).then_inc(mm["sub"].sem, 1)

        def router_top2(dve, mm, g, ne):
            rt = [x[:, :, 0:ne] for x in RT]
            rv = bcm(rev[:, 0:ne], TG)
            dve.wait_ge(*mm["exp"](g + 1))
            vlink(dve.tensor_reduce(r8[1][:, :], rt[2], X_AXIS, ALU.add))
            vlink(dve.reciprocal(r8[2][:, :], r8[1][:, :]))
            vlink(dve.tensor_tensor(rt[3], rt[2], bc(r8[2][:, :], ne), ALU.mult))
            for k in range(2):
                prob, hot = (rt[3], rt[4]) if k == 0 else (rt[6], rt[7])
                vlink(dve.tensor_reduce(r8[3 + k][:, :], prob, X_AXIS, ALU.max))
                vlink(dve.tensor_tensor(rt[5], prob, bc(r8[3 + k][:, :], ne), ALU.is_equal))
                vlink(dve.tensor_tensor(rt[5], rt[5], rv, ALU.mult))
                vlink(dve.tensor_reduce(r8[5][:, :], rt[5], X_AXIS, ALU.max))
                vlink(dve.tensor_tensor(hot, rt[5], bc(r8[5][:, :], ne), ALU.is_equal))
                if k == 0:
                    vlink(dve.scalar_tensor_tensor(rt[6], rt[4], -2.0, rt[3], ALU.mult, ALU.add))
            vlink(dve.tensor_tensor(r8[6][:, :], r8[3][:, :], r8[4][:, :], ALU.add))
            vlink(dve.reciprocal(r8[7][:, :], r8[6][:, :]))
            dve.tensor_tensor(r8[3][:, :], r8[3][:, :], r8[7][:, :], ALU.mult)
            vlink(dve.tensor_tensor(r8[4][:, :], r8[4][:, :], r8[7][:, :], ALU.mult))
            dve.tensor_tensor(rt[4], rt[4], bc(r8[3][:, :], ne), ALU.mult)
            vlink(dve.tensor_tensor(rt[7], rt[7], bc(r8[4][:, :], ne), ALU.mult))
            vlink(dve.tensor_tensor(rt[5], rt[4], rt[7], ALU.add))
            if g >= 2:
                dve.wait_ge(*mm["dt_ps"](2 * (g - 1)))
            vlink(dve.tensor_copy(DS[g % 2][:, :, 0:ne], rt[5]))
            dve.tensor_tensor(DS[g % 2][:, :, 32:32 + ne], rt[5], DS[g % 2][:, :, 0:ne].bitcast(F32), ALU.subtract).then_inc(mm["ds"].sem, 1)

        def router_scalar(act, mm, ne):
            for g in range(G):
                act.wait_ge(*mm["sub"](g + 1))
                act.activation(RT[2][:, :, 0:ne], RT[1][:, :, 0:ne], ACT.Exp).then_inc(mm["exp"].sem, 1)

        def router_move(act, mm, banks):
            for j in range(NCHUNK):
                act.wait_ge(*mm["dt_ps"](j + 1))
                act.activation(DT[:, j * CHUNK:(j + 1) * CHUNK], ps[:, banks[j % 2], :], ACT.Copy).then_inc(mm["dt"].sem, 1)

        N1 = NCHUNK * E1
        retire(sig2)
        e1 = signals((G, "var rstd fs xu lg_ps lg sub exp ds"), (NCHUNK, "ft_ps ft dt_ps dt x"), (N1, "act h_ps h2_ps d_ps"),
                     (2 + N1, "m1 hid"), (8 + N1, "o_ps"), (1 + NCHUNK, "oc t_ps ta"))
        s_w12 = sem("w12_split")
        s_w12h = sem("w12_hi")
        s_gw = sem("gw_split")
        s_sel = sem("sel_ready")

        def e1_sync(sp):
            for h in range(2):
                wdma(sp, "gw", gw[h * C:(h + 1) * C, :], a["L1_ffn_gate_w"])
            wdma(sp, "gw", b_gw[:, :], a["L1_ffn_gate_b"].unsqueeze(0).to_broadcast([P, E1]))
            for h in range(2):
                for k, nm in enumerate(("L1_ffn_w1", "L1_ffn_w2")):
                    wdma(sp, "w12", w12_raw[h * C:(h + 1) * C, k, :, :], a[nm].rearrange("e d h -> d e h"))
            wdma(sp, "w3", w3[:, :, :], a["L1_ffn_w3"].rearrange("e h o -> h e o"))

        def e1_consts(dve):
            dve.wait_ge(s["consts"], NCONST)
            dve.memset(DS[0][:, :, :].bitcast(F32), 0.0)
            dve.memset(DS[1][:, :, :].bitcast(F32), 0.0)
            vlink(dve.tensor_tensor(self32[:, :], ident[:, 0:E1], ident[:, 32:32 + E1], ALU.add))
            dve.tensor_copy(sel[:, :], self32[:, :]).then_inc(s_sel, 1)
            wwait(dve, "gw")
            vlink(dve.tensor_copy(gw2[:, 0, :], gw[:, :]))
            dve.tensor_tensor(gw2[:, 1, :], gw[:, :], gw2[:, 0, :].bitcast(F32), ALU.subtract).then_inc(s_gw, 1)

        def e1_whi(act):
            wwait(act, "w12")
            for k in range(2):
                for i in range(4):
                    act.activation(w12[:, 0, k, 4 * i:4 * i + 4, :], w12_raw[:, k, 4 * i:4 * i + 4, :], ACT.Copy).then_inc(s_w12h, 1)

        def e1_pool(pool):
            for k in range(2):
                for i in range(4):
                    sl = slice(4 * i, 4 * i + 4)
                    pool.wait_ge(s_w12h, 4 * k + i + 1)
                    pool.tensor_tensor(w12[:, 1, k, sl, :], w12_raw[:, k, sl, :], w12[:, 0, k, sl, :].bitcast(F32),
                                       ALU.subtract).then_inc(s_w12, 1)
            ln_pool(pool, 1e-5, e1["var"], e1["rstd"])

        def experts_finish(dve, mm, i):
            dve.wait_ge(*mm["t_ps"](i + 2))
            dve.tensor_reduce(OA[:, :, :], ps[:, 7, :].rearrange("p (t h c) -> p t c h", h=2, c=C), X_AXIS,
                              ALU.add).then_inc(mm["ta"].sem, 1)
            dve.wait_ge(*mm["ta"](i + 2))
            xs = X[:, bass.ts(i, 4), :]
            dve.tensor_tensor(xs, xs, OA[:, :, :], ALU.add).then_inc(mm["x"].sem, 1)
            dve.wait_ge(*mm["x"](i + 1))

        def e1_vector(dve):
            mm = e1
            ln_vector(dve, m["x3"], mm["var"], mm["rstd"], mm["fs"], mm["ft_ps"], u_sem=mm["xu"])
            for g in range(G):
                router_logits(dve, mm, g, E1, b_gw[:, :], 7)
                router_top2(dve, mm, g, E1)
            dve.sem_inc(mm["m1"].sem, 2)
            dve.sem_inc(mm["hid"].sem, 2)
            dve.sem_inc(mm["ta"].sem, 1)

            def gate(i, e):
                dve.wait_ge(*mm["act"](i * E1 + (e + 1)))
                dve.wait_ge(*mm["h2_ps"](i * E1 + (e + 1)))
                dve.wait_ge(*mm["o_ps"](i * E1 + (e + 1)))
                dve.tensor_tensor(HID[e % 8][:, :], SB[e % 2][:, :], ps[:, 2 + e % 2, :], ALU.mult).then_inc(mm["m1"].sem, 1)

            def weigh(i, e):
                dve.wait_ge(*mm["m1"](i * E1 + (e + 3)))
                dve.wait_ge(*mm["d_ps"](i * E1 + (e + 1)))
                dve.tensor_tensor(HID[e % 8][:, :], HID[e % 8][:, :], ps[:, 4 + e % 2, :], ALU.mult).then_inc(mm["hid"].sem, 1)

            def chunk(i, prev):
                for e in range(E1):
                    gate(i, e)
                    if e >= 1:
                        weigh(i, e - 1)
                    elif prev is not None:
                        weigh(prev, E1 - 1)
                    if e == 8 and prev is not None:
                        experts_finish(dve, mm, prev)
            chunk(0, None)
            with dve.Fori(1, NCHUNK) as i:
                chunk(i, i - 1)
            weigh(NCHUNK - 1, E1 - 1)
            experts_finish(dve, mm, NCHUNK - 1)

        def e1_scalar2(act):
            mm = e1
            ln_scalar(act, mm["ft_ps"], mm["ft"])
            router_scalar(act, mm, E1)
            router_move(act, mm, (4, 5))
            act.sem_inc(mm["oc"].sem, 1)

            def chunk(i, prev):
                for e in range(E1):
                    act.wait_ge(*mm["h_ps"](i * E1 + (e + 1)))
                    act.wait_ge(*mm["m1"](i * E1 + (e + 1)))
                    act.activation(SB[e % 2][:, :], ps[:, e % 2, :], ACT.Silu).then_inc(mm["act"].sem, 1)
                    if e == 3 and prev is not None:
                        move(prev)

            def move(i):
                act.wait_ge(*mm["o_ps"](i * E1 + (E1 + 8)))
                act.wait_ge(*mm["t_ps"](i + 1))
                act.activation(OS[:, :], ps[:, 6, :], ACT.Copy).then_inc(mm["oc"].sem, 1)
            chunk(0, None)
            with act.Fori(1, NCHUNK) as i:
                chunk(i, i - 1)
            move(NCHUNK - 1)

        def e1_tensor(pe):
            mm = e1
            ln_tensor(pe, mm["fs"], mm["ft_ps"], mm["ft"])
            pe.wait_ge(s_gw, 1)
            pe.wait_ge(*m["x3"](G))
            router_tensor(pe, mm, gw2, E1, 7)
            router_transpose(pe, mm, (4, 5))
            pe.wait_ge(s_w12, 8)
            pe.wait_ge(s_sel, 1)
            wwait(pe, "w3")
            pe.wait_ge(*mm["dt"](NCHUNK))
            pe.sem_inc(mm["o_ps"].sem, 8)
            pe.sem_inc(mm["t_ps"].sem, 1)

            def hidden(i, e):
                pe.wait_ge(*mm["m1"](i * E1 + (e + 1)))
                for k in range(2):
                    for part in range(2):
                        last = pe.matmul(ps[:, 2 * k + e % 2, :], w12[:, part, k, e, :], UT[:, bass.ts(i, CHUNK)],
                                         start=(part == 0), stop=(part == 1))
                    last.then_inc(mm[("h_ps", "h2_ps")[k]].sem, 1)

            def spread(i, e):
                pe.wait_ge(*mm["hid"](i * E1 + (e + 1)))
                pe.matmul(ps[:, 4 + e % 2, :], sel[:, e:e + 1].to_broadcast([P, P]), DT[:, bass.ts(i, CHUNK)], start=True,
                          stop=True).then_inc(mm["d_ps"].sem, 1)

            def outp(i, e):
                pe.wait_ge(*mm["hid"](i * E1 + (e + 4)))
                for f in (e, e + 1):
                    o = C * (f % 2)
                    pe.matmul(ps[o:o + C, 6, :], w3[:, f, :], HID[f % 8][:, :], start=(f < 2),
                              stop=(f >= E1 - 2)).then_inc(mm["o_ps"].sem, 1)

            def chunk(i, prev):
                for e in range(E1):
                    hidden(i, e)
                    if e >= 1:
                        spread(i, e - 1)
                    elif prev is not None:
                        spread(prev, E1 - 1)
                    if e in (0, 2) and prev is not None:
                        outp(prev, E1 - 4 + e)
                    if e == 4:
                        pe.wait_ge(*mm["oc"](i + 1))
                    if e % 2 == 0 and e >= 4:
                        outp(i, e - 4)
                    if e == 5 and prev is not None:
                        back(prev)

            def back(i):
                pe.wait_ge(*mm["oc"](i + 2))
                pe.wait_ge(*mm["ta"](i + 1))
                for t in range(4):
                    last = pe.transpose(ps[:, 7, t * P:(t + 1) * P], OS[:, t * P:(t + 1) * P], ident[:, :])
                last.then_inc(mm["t_ps"].sem, 1)
            chunk(0, None)
            with pe.Fori(1, NCHUNK) as i:
                chunk(i, i - 1)
            spread(NCHUNK - 1, E1 - 1)
            outp(NCHUNK - 1, E1 - 4)
            outp(NCHUNK - 1, E1 - 2)
            back(NCHUNK - 1)
        retire(sig3)
        sig5 = signals((G, "d_var d_rstd d_fs d_qe d_qn d_y x5"), (1, "d_w_ps d_w"), (3, "d_hm"),
                       (NCHUNK, "d_ft_ps d_xp d_ql_ps d_ql d_qt_ps d_qt d_cv_ps d_kd d_k_ps d_km d_ke d_v_ps d_v d_kt_ps d_kt"),
                       (NCHUNK, "d_c_ps d_c d_o_ps d_g d_y_ps"))
        m.update(sig5)

        def d_sync(sp):
            wdma(sp, "datt", wq_raw[:, :], a["L2_conv_wq"])
            wdma(sp, "datt", wkv_raw[:, :, :], a["L2_conv_wpw"].rearrange("(k p) c -> p k c", p=INNER))
            wdma(sp, "datt", wo_raw[:, :], a["L2_conv_wout"])
            for h in range(2):
                wdma(sp, "datt", dw_raw[h * C:(h + 1) * C, :], a["L2_conv_wdw"].rearrange("c i h w -> c (i h w)"))
            wdma(sp, "datt", b_o[:, :], a["L2_conv_bout"].unsqueeze(0).to_broadcast([P, C]))

        def d_pool(pool):
            pool.memset(hmask[:, :], 1.0).then_inc(m["d_hm"].sem, 1)
            hv = hmask[:, :].rearrange("p (h e) -> p h e", e=DH)
            pool.wait_ge(*m["d_hm"](1))
            pool.affine_select(out=hv, in_=hv, compare_op=ALU.is_ge, fill=0.0, base=0, pattern=[[-DH, HEADS], [0, DH]],
                               channel_multiplier=1).then_inc(m["d_hm"].sem, 1)
            pool.wait_ge(*m["d_hm"](2))
            pool.affine_select(out=hv, in_=hv, compare_op=ALU.is_ge, fill=0.0, base=DH - 1, pattern=[[DH, HEADS], [0, DH]],
                               channel_multiplier=-1).then_inc(m["d_hm"].sem, 1)
            ln_pool(pool, 1e-6, m["d_var"], m["d_rstd"])

        def d_vector(dve):
            dve.wait_ge(*m["d_w_ps"](1))
            wwait(dve, "datt")
            for h in range(2):
                hs = slice(h * C, (h + 1) * C)
                dve.tensor_copy(wq_t[hs, :], ps[0:C, 0, 0:INNER])
                dve.tensor_copy(wkv[hs, :, :].rearrange("p k i -> p (k i)"), ps[0:C, 0, INNER:3 * INNER])
                dve.tensor_copy(ident2[hs, :], ident[hs, hs])
            dve.tensor_copy(wo[:, :], ps[:, 1, 0:C])
            vlink(dve.tensor_copy(dw_hi[:, :], dw_raw[:, :]))
            vlink(dve.tensor_copy(wq[:, 0, :], wq_t[:, :]))
            dve.tensor_tensor(wq[:, 1, :], wq_t[:, :], wq[:, 0, :].bitcast(F32), ALU.subtract)
            vlink(dve.tensor_tensor(dw_lo[:, :], dw_raw[:, :], dw_hi[:, :].bitcast(F32), ALU.subtract))
            for t in range(9):
                dve.tensor_scalar(wdw[:, t, 0, :], ident2[:, :], dw_hi[:, t:t + 1].bitcast(F32), None, ALU.mult)
                last = dve.tensor_scalar(wdw[:, t, 1, :], ident2[:, :], dw_lo[:, t:t + 1], None, ALU.mult)
            last.then_inc(m["d_w"].sem, 1)
            ln_vector(dve, e1["x"], m["d_var"], m["d_rstd"], m["d_fs"], m["d_ft_ps"], x_per=2)
            dve.wait_ge(*m["d_hm"](3))

            def q_soft(g):
                for j in range(2):
                    dve.wait_ge(*m["d_ql_ps"](2 * g + j + 1))
                    last = dve.tensor_reduce(qr[0][:, j * 32:(j + 1) * 32], ps[:, 2 + j, :].rearrange("p (t d) -> p t d", d=DH),
                                             X_AXIS, ALU.max)
                vlink(last)
                for j in range(2):
                    dve.tensor_tensor(QL[:, 4 * j:4 * j + 4, :].rearrange("p t (h d) -> p (t h) d", d=DH),
                                      ps[:, 2 + j, :].rearrange("p (t d) -> p t d", d=DH),
                                      bc(qr[0][:, j * 32:(j + 1) * 32], DH), ALU.subtract).then_inc(m["d_ql"].sem, 1)
                dve.wait_ge(*m["d_qe"](g + 1))
                vlink(dve.tensor_reduce(qr[1][:, :], QE[:, :, :].rearrange("p t (h d) -> p (t h) d", d=DH), X_AXIS, ALU.add))
                vlink(dve.reciprocal(qr[2][:, :], qr[1][:, :]))
                vlink(dve.tensor_scalar(qr[1][:, :], qr[2][:, :], DH ** -0.5, None, ALU.mult))
                if g >= 1:
                    dve.wait_ge(*m["d_qt_ps"](2 * g))
                qe = QE[:, :, :].rearrange("p t (h d) -> p (t h) d", d=DH)
                dve.tensor_tensor(qe, qe, bc(qr[1][:, :], DH), ALU.mult).then_inc(m["d_qn"].sem, 1)

            def kmax(j):
                dve.wait_ge(*m["d_k_ps"](j + 1))
                dve.tensor_reduce(nkm[:, 2 * j:2 * j + 2], ps[:, 5, :].rearrange("p (r s) -> p r s", r=2), X_AXIS, ALU.max,
                                  negate=True).then_inc(m["d_km"].sem, 1)

            def ctx_out(j):
                dve.wait_ge(*m["d_ke"](j + 1))
                vlink(dve.reciprocal(rks[:, 2 * j:2 * j + 2], ksum[:, 2 * j:2 * j + 2]))
                dve.wait_ge(*m["d_c_ps"](j + 1))
                for r in range(2):
                    b = 2 * j + r
                    last = dve.scalar_tensor_tensor(CTX[:, b, :], ps[:, 5, r * INNER:(r + 1) * INNER], rks[:, b:b + 1],
                                                    hmask[:, :], ALU.mult, ALU.mult)
                last.then_inc(m["d_c"].sem, 1)
            for g in range(G):
                q_soft(g)
                for j in (2 * g, 2 * g + 1):
                    kmax(j)
                    ctx_out(j)
            for g in range(G):
                sl = slice(g * TG, (g + 1) * TG)
                dve.wait_ge(*m["d_y_ps"](2 * g + 2))
                dve.tensor_tensor(XC[g % 2][:, :, :], ps[:, 4 + g % 2, :].rearrange("p (t c) -> p t c", c=C), bcm(b_o[:, :], TG),
                                  ALU.add).then_inc(m["d_y"].sem, 1)
                dve.wait_ge(*m["d_y"](g + 1))
                dve.tensor_tensor(X[:, sl, :], X[:, sl, :], XC[g % 2][:, :, :], ALU.add).then_inc(m["x5"].sem, 1)

        def d_scalar(act):
            act.wait_ge(*m["d_w"](1))

            def padded(g):
                if g >= 2:
                    act.wait_ge(*m["d_cv_ps"](2 * (g - 1)))
                for j in range(2):
                    act.wait_ge(*m["d_ft_ps"](2 * g + j + 1))
                    act.activation(UT[:, (2 * g + j) * CHUNK:(2 * g + j + 1) * CHUNK], ps[:, j, :], ACT.Copy)
                    to_padded(act, j, XP[g % 2], j, m["d_xp"])

            def q_exp(g):
                act.wait_ge(*m["d_ql"](2 * g + 2))
                if g >= 1:
                    act.wait_ge(*m["d_qt_ps"](2 * g))
                act.activation(QE[:, :, :].rearrange("p t c -> p (t c)"), QL[:, :, :].rearrange("p t c -> p (t c)"),
                               ACT.Exp).then_inc(m["d_qe"].sem, 1)

            def q_move(g):
                for j in range(2):
                    act.wait_ge(*m["d_qt_ps"](2 * g + j + 1))
                    act.activation(QT[:, (2 * g + j) * CHUNK:(2 * g + j + 1) * CHUNK], ps[:, j, :], ACT.Copy).then_inc(m["d_qt"].sem, 1)

            def kd(j):
                act.wait_ge(*m["d_cv_ps"](j + 1))
                if j >= 2:
                    act.wait_ge(*m["d_v_ps"](j - 1))
                act.activation(KD[j % 2][:, :], ps[:, 4, :], ACT.Copy).then_inc(m["d_kd"].sem, 1)

            def kexp(j):
                act.wait_ge(*m["d_v_ps"](j + 1))
                if j >= 2:
                    act.wait_ge(*m["d_c_ps"](j - 1))
                act.activation(VT[j % 2][:, :, :].rearrange("p t c -> p (t c)"), ps[:, 6, :], ACT.Copy).then_inc(m["d_v"].sem, 1)
                act.wait_ge(*m["d_km"](j + 1))
                for r in range(2):
                    b = 2 * j + r
                    last = act.activation(KE[j % 2][:, r * PIX:(r + 1) * PIX], ps[:, 5, r * PIX:(r + 1) * PIX], ACT.Exp,
                                          bias=nkm[:, b:b + 1], accum_out=ksum[:, b:b + 1])
                last.then_inc(m["d_ke"].sem, 1)

            def kt(j):
                act.wait_ge(*m["d_kt_ps"](j + 1))
                act.activation(KT[j % 2][:, :, :].rearrange("p t c -> p (t c)"), ps[:, 7, :], ACT.Copy).then_inc(m["d_kt"].sem, 1)
            padded(0)
            for g in range(G):
                if g + 1 < G:
                    padded(g + 1)
                q_exp(g)
                q_move(g)
                for j in (2 * g, 2 * g + 1):
                    kd(j)
                    kexp(j)
                    kt(j)
            wwait(act, "datt")
            for j in range(NCHUNK):
                act.wait_ge(*m["d_o_ps"](j + 1))
                if j >= 2:
                    act.wait_ge(*m["d_y_ps"](j - 1))
                act.activation(KE[j % 2][:, :], ps[:, 2 + j % 2, :], ACT.Gelu).then_inc(m["d_g"].sem, 1)

        def d_tensor(pe):
            wwait(pe, "datt")
            pe.wait_ge(*e1["ta"](NCHUNK + 1))
            pe.transpose(ps[0:C, 0, 0:INNER], wq_raw[:, :], ident[:, :])
            for k in range(2):
                pe.transpose(ps[0:C, 0, (1 + k) * INNER:(2 + k) * INNER], wkv_raw[:, k, :], ident[:, :])
            pe.transpose(ps[:, 1, 0:C], wo_raw[:, :], ident[0:C, 0:C]).then_inc(m["d_w_ps"].sem, 1)
            pe.wait_ge(*m["d_w"](1))

            def tr(g):
                pe.wait_ge(*m["d_fs"](g + 1))
                if g >= 1:
                    pe.wait_ge(*m["d_xp"](2 * g))
                    if g >= 2:
                        pe.wait_ge(*m["d_qt"](2 * (g - 1)))
                transpose_tiles(pe, US[g % 2], (0, 1), m["d_ft_ps"])

            def qlog(g):
                for j in range(2):
                    pe.wait_ge(*m["d_xp"](2 * g + j + 1))
                    if g >= 1:
                        pe.wait_ge(*m["d_ql"](2 * (g - 1) + j + 1))
                    for t in range(4):
                        lhs = UT[:, (2 * g + j) * CHUNK + t * P:(2 * g + j) * CHUNK + (t + 1) * P]
                        for part in range(2):
                            last = pe.matmul(ps[:, 2 + j, t * P:(t + 1) * P], lhs, wq[:, part, :], start=(part == 0), stop=(part == 1))
                    last.then_inc(m["d_ql_ps"].sem, 1)

            def conv(j):
                g, jj = j // 2, j % 2
                xp = XP[g % 2][:, :, :].rearrange("p b (y x) -> p b y x", x=PADW)
                if j >= 1:
                    pe.wait_ge(*m["d_kd"](j))
                for t in range(9):
                    dy, dx = t // 3, t % 3
                    last = pe.matmul(ps[:, 4, :], wdw[:, t, :, :].rearrange("p h c -> p (h c)"),
                                     xp[:, 2 * jj:2 * jj + 2, dy:dy + H, dx:dx + W], start=(t == 0), stop=(t == 8))
                last.then_inc(m["d_cv_ps"].sem, 1)

            def kv(j):
                pe.wait_ge(*m["d_kd"](j + 1))
                if j >= 1:
                    pe.wait_ge(*m["d_c"](j))
                    pe.wait_ge(*m["d_v"](j))
                pe.matmul(ps[:, 5, :], wkv[:, 0, :], KD[j % 2][:, :], start=True, stop=True).then_inc(m["d_k_ps"].sem, 1)
                for t in range(4):
                    last = pe.matmul(ps[:, 6, t * P:(t + 1) * P], KD[j % 2][:, t * P:(t + 1) * P], wkv[:, 1, :], start=True, stop=True)
                last.then_inc(m["d_v_ps"].sem, 1)

            def ktr(j):
                pe.wait_ge(*m["d_ke"](j + 1))
                if j >= 1:
                    pe.wait_ge(*m["d_kt"](j))
                for t in range(4):
                    last = pe.transpose(ps[:, 7, t * P:(t + 1) * P], KE[j % 2][:, t * P:(t + 1) * P], ident[:, :])
                last.then_inc(m["d_kt_ps"].sem, 1)

            def ctxm(j):
                pe.wait_ge(*m["d_kt"](j + 1))
                pe.wait_ge(*m["d_v"](j + 1))
                for r in range(2):
                    for half in range(2):
                        t = 2 * r + half
                        last = pe.matmul(ps[:, 5, r * INNER:(r + 1) * INNER], KT[j % 2][:, t, :], VT[j % 2][:, t, :],
                                         start=(half == 0), stop=(half == 1))
                last.then_inc(m["d_c_ps"].sem, 1)

            def qtr(g):
                pe.wait_ge(*m["d_qn"](g + 1))
                if g + 1 < G:
                    pe.wait_ge(*m["d_xp"](2 * g + 4))
                for t in range(TG):
                    last = pe.transpose(ps[:, t // 4, (t % 4) * P:(t % 4 + 1) * P], QE[:, t, :], ident[:, :])
                    if t % 4 == 3:
                        last.then_inc(m["d_qt_ps"].sem, 1)
            tr(0)
            for g in range(G):
                qlog(g)
                if g + 1 < G:
                    tr(g + 1) if g < 1 else None
                conv(2 * g)
                qtr(g)
                kv(2 * g)
                ktr(2 * g)
                conv(2 * g + 1)
                ctxm(2 * g)
                kv(2 * g + 1)
                if g >= 0 and g + 2 < G:
                    pe.wait_ge(*m["d_qt"](2 * (g + 1)))
                    tr(g + 2)
                ktr(2 * g + 1)
                ctxm(2 * g + 1)
            def att(j):
                pe.wait_ge(*m["d_c"](NCHUNK))
                pe.wait_ge(*m["d_qt"](NCHUNK))
                if j >= 2:
                    pe.wait_ge(*m["d_g"](j - 1))
                for r in range(2):
                    b = 2 * j + r
                    image = lambda cols: cols.rearrange("p (h r s) -> p r h s", h=2, r=2)[:, r, :, :]
                    last = pe.matmul(image(ps[:, 2 + j % 2, :]), CTX[:, b, :], image(QT[:, j * CHUNK:(j + 1) * CHUNK]),
                                     start=True, stop=True)
                last.then_inc(m["d_o_ps"].sem, 1)

            def proj(j):
                g = j // 2
                pe.wait_ge(*m["d_g"](j + 1))
                if g >= 2 and j % 2 == 0:
                    pe.wait_ge(*m["d_y"](g - 1))
                for t in range(4):
                    o = (j % 2) * 4 + t
                    last = pe.matmul(ps[:, 4 + g % 2, o * C:(o + 1) * C], KE[j % 2][:, t * P:(t + 1) * P], wo[:, :], start=True, stop=True)
                last.then_inc(m["d_y_ps"].sem, 1)
            att(0)
            for j in range(NCHUNK):
                if j + 1 < NCHUNK:
                    att(j + 1)
                proj(j)
        retire(e1)
        U2 = 2 * E2
        e2 = signals((G, "var rstd var2 rstd2 fs xu lg_ps lg sub exp ds"), (NCHUNK, "ft_ps ft dt_ps dt x"),
                     (4 + NCHUNK * U2, "act"), (NCHUNK * U2, "h_ps"), (NCHUNK * E2, "d_ps"), (3 + NCHUNK * U2, "hid"),
                     (8 + NCHUNK * U2, "o_ps"), (1 + NCHUNK, "oc t_ps ta"), (1, "w_ps w ws"), (E2, "whi wlo"))

        def e2_sync(sp):
            for h in range(2):
                wdma(sp, "e2s", gw_6[h * C:(h + 1) * C, :], a["L2_ffn_Wr"])
                wdma(sp, "e2s", lng_raw[:, h * C:(h + 1) * C], a["L2_ffn_ln_g"])
            wdma(sp, "e2s", b_gw_6[:, :], a["L2_ffn_br"].unsqueeze(0).to_broadcast([P, E2]))
            wdma(sp, "e2s", lnb_raw[:, :], a["L2_ffn_ln_b"])
            wdma(sp, "e2s", b1_raw[:, :], a["L2_ffn_b1"].rearrange("e (h p) -> (e h) p", p=P))
            sp.wait_ge(*m["x3"](1))
            for r in (0, 32):
                wdma(sp, "e2s", b2_6[r:r + E2, 0:C], a["L2_ffn_b2"])
            for h in range(2):
                wdma(sp, "e2w1", w1_raw[h * C:(h + 1) * C, :, :], a["L2_ffn_W1"].rearrange("e d h -> d e h"))
            sp.wait_ge(*e1["x"](NCHUNK))
            wdma(sp, "e2w2", w2_6[:, :, :, :], a["L2_ffn_W2"].rearrange("e (h p) o -> p e h o", p=P))

        def e2_pool(pool):
            ln_rstd(pool, 0, 1e-5, e2["var"], e2["rstd"])
            for g in range(G):
                if g + 1 < G:
                    ln_rstd(pool, g + 1, 1e-5, e2["var"], e2["rstd"])
                ln_rstd(pool, g, 1e-5, e2["var2"], e2["rstd2"])

        def e2_vector(dve):
            mm = e2
            wwait(dve, "e2s")
            vlink(dve.tensor_copy(gw2_6[:, 0, :], gw_6[:, :]))
            dve.tensor_tensor(gw2_6[:, 1, :], gw_6[:, :], gw2_6[:, 0, :].bitcast(F32), ALU.subtract)
            vlink(dve.tensor_copy(b2s[:, 0, :], b2_6[:, :]))
            dve.tensor_tensor(b2s[:, 1, :], b2_6[:, :], b2s[:, 0, :].bitcast(F32), ALU.subtract)
            for i in range(2):
                dve.memset(DS[i][:, :, :].bitcast(F32), 0.0)
            dve.wait_ge(*mm["w_ps"](1))
            dve.tensor_copy(lnb[:, :], ps[0:C, 7, 2 * U2 + E2:2 * U2 + 2 * E2])
            dve.tensor_copy(gsum[:, :], ps[:, 7, 0:E2])
            dve.tensor_copy(b1_t[:, :], ps[:, 7, U2:2 * U2])
            dve.tensor_copy(lng[:, :], ps[:, 7, 2 * U2:2 * U2 + E2]).then_inc(mm["w"].sem, 1)
            for e in range(E2):
                dve.wait_ge(*mm["whi"](e + 1))
                dve.scalar_tensor_tensor(w1_6[:, 1, e, :], w1_raw[:, e, :], lng[:, e:e + 1], w1_6[:, 0, e, :].bitcast(F32),
                                         ALU.mult, ALU.subtract).then_inc(mm["wlo"].sem, 1)
            dve.wait_ge(*mm["ws"](1))
            dve.tensor_tensor(b1_6[:, :], b1_t[:, :], ps[:, 6, 0:U2], ALU.add).then_inc(mm["x_b1"].sem, 1)

            def stats(g):
                dve.wait_ge(*m["x5"](g + 1))
                ln_stats(dve, g, X[:, g * TG:(g + 1) * TG, :], mm["var"])
                dve.wait_ge(*mm["var"](g + 1))
            stats(0)
            for g in range(G):
                sl = slice(g * TG, (g + 1) * TG)
                xc = XC[g % 2][:, :, :]
                if g + 1 < G:
                    stats(g + 1)
                vlink(ln_center(dve, g, X[:, sl, :], xc))
                dve.wait_ge(*mm["rstd"](g + 1))
                vlink(dve.tensor_tensor(U[:, sl, :], xc, bc(rstd[:, sl], C), ALU.mult))
                ln_stats(dve, g, U[:, sl, :], mm["var2"])
                dve.wait_ge(*mm["var2"](g + 1))
                vlink(ln_center(dve, g, U[:, sl, :], xc))
                dve.wait_ge(*mm["rstd2"](g + 1))
                vlink(dve.tensor_tensor(xc, xc, bc(rstd[:, sl], C), ALU.mult))
                if g >= 2:
                    dve.wait_ge(*mm["ft_ps"](2 * (g - 1)))
                split(dve, US[g % 2], xc, mm["fs"])

            def rescale(dve, g, lp, mm):
                sl = slice(g * TG, (g + 1) * TG)
                dve.tensor_tensor(r8[6][:, :], vpe[:, sl], rstd[:, sl], ALU.mult)
                vlink(dve.tensor_scalar(r8[7][:, :], S1_[:, sl], 0.5, None, ALU.mult))
                dve.tensor_tensor(RT[2][:, :, 0:E2], bc(r8[7][:, :], E2), bcm(gsum[:, :], TG), ALU.mult)
                dve.tensor_tensor(RT[1][:, :, 0:E2], lp, bc(r8[6][:, :], E2), ALU.mult).then_inc(mm["lg"].sem, 1)
                dve.wait_ge(*mm["lg"](g + 1))
                vlink(dve.tensor_tensor(RT[1][:, :, 0:E2], RT[1][:, :, 0:E2], RT[2][:, :, 0:E2], ALU.add))
                return RT[1][:, :, 0:E2]
            for g in range(G):
                router_logits(dve, mm, g, E2, b_gw_6[:, :], 7, rescale)
                router_top2(dve, mm, g, E2)
            dve.sem_inc(mm["hid"].sem, 3)
            dve.sem_inc(mm["ta"].sem, 1)

            def weigh(i, u):
                dve.wait_ge(*mm["act"](i * U2 + (u + 5)))
                if u % 2 == 0:
                    dve.wait_ge(*mm["d_ps"](i * E2 + (u // 2 + 1)))
                dve.tensor_tensor(HID[u % 8][:, :], HID[u % 8][:, :], ps[:, 4 + (u // 2) % 2, :], ALU.mult).then_inc(mm["hid"].sem, 1)

            def chunk(i, prev):
                for u in range(U2):
                    weigh(i, u)
                    if u == 6 and prev is not None:
                        experts_finish(dve, mm, prev)
            chunk(0, None)
            with dve.Fori(1, NCHUNK) as i:
                chunk(i, i - 1)
            experts_finish(dve, mm, NCHUNK - 1)
        e2["x_b1"] = signals((1, "x_b1"))["x_b1"]

        def e2_scalar(act):
            mm = e2
            act.wait_ge(*mm["w"](1))
            wwait(act, "e2w1")
            for e in range(E2):
                act.activation(w1_6[:, 0, e, :], w1_raw[:, e, :], ACT.Copy, scale=lng[:, e:e + 1]).then_inc(mm["whi"].sem, 1)
            ln_scalar(act, mm["ft_ps"], mm["ft"])
            router_scalar(act, mm, E2)
            router_move(act, mm, (4, 5))
            act.wait_ge(*mm["x_b1"](1))
            act.sem_inc(mm["act"].sem, 4)
            act.sem_inc(mm["oc"].sem, 1)

            def chunk(i, prev):
                for u in range(U2):
                    act.wait_ge(*mm["h_ps"](i * U2 + (u + 1)))
                    act.wait_ge(*mm["o_ps"](i * U2 + (u + 1)))
                    act.activation(HID[u % 8][:, :], ps[:, u % 4, :], ACT.Gelu, bias=b1_6[:, u:u + 1]).then_inc(mm["act"].sem, 1)
                    if u == 2 and prev is not None:
                        move(prev)

            def move(i):
                act.wait_ge(*mm["o_ps"](i * U2 + (U2 + 8)))
                act.wait_ge(*mm["t_ps"](i + 1))
                act.activation(OS[:, :], ps[:, 6, :], ACT.Copy).then_inc(mm["oc"].sem, 1)
            chunk(0, None)
            with act.Fori(1, NCHUNK) as i:
                chunk(i, i - 1)
            move(NCHUNK - 1)

        def e2_tensor(pe):
            mm = e2
            wwait(pe, "e2s")
            wwait(pe, "e2w1")
            pe.wait_ge(*m["d_kt"](NCHUNK))
            pe.matmul(ps[:, 7, 0:E2], ones[0:C, :], gw_6[0:C, :], start=True, stop=True)
            pe.transpose(ps[:, 7, U2:2 * U2], b1_raw[:, :], ident[0:U2, 0:U2])
            pe.transpose(ps[:, 7, 2 * U2:2 * U2 + E2], lng_raw[:, :], ident[0:E2, 0:E2])
            pe.transpose(ps[0:C, 7, 2 * U2 + E2:2 * U2 + 2 * E2], lnb_raw[:, :], ident[0:E2, 0:E2]).then_inc(mm["w_ps"].sem, 1)
            pe.wait_ge(*mm["w"](1))
            pe.wait_ge(*m["d_v"](NCHUNK))
            for u in range(U2):
                e, h = u // 2, u % 2
                last = pe.matmul(ps[:, 6, u:u + 1], w1_raw[0:C, e, h * P:(h + 1) * P], lnb[:, e:e + 1], start=True, stop=True)
            last.then_inc(mm["ws"].sem, 1)
            ln_tensor(pe, mm["fs"], mm["ft_ps"], mm["ft"])
            router_tensor(pe, mm, gw2_6, E2, 7)
            router_transpose(pe, mm, (4, 5))
            pe.wait_ge(*mm["wlo"](E2))
            wwait(pe, "e2w2")
            pe.wait_ge(*mm["dt"](NCHUNK))
            pe.sem_inc(mm["o_ps"].sem, 8)
            pe.sem_inc(mm["t_ps"].sem, 1)

            def hidden(i, u):
                e, h = u // 2, u % 2
                pe.wait_ge(*mm["act"](i * U2 + (u + 1)))
                for part in range(2):
                    last = pe.matmul(ps[:, u % 4, :], w1_6[:, part, e, h * P:(h + 1) * P], UT[:, bass.ts(i, CHUNK)],
                                     start=(part == 0), stop=(part == 1))
                last.then_inc(mm["h_ps"].sem, 1)

            def spread(i, e):
                pe.wait_ge(*mm["hid"](i * U2 + (2 * e + 1)))
                pe.matmul(ps[:, 4 + e % 2, :], sel[:, e:e + 1].to_broadcast([P, P]), DT[:, bass.ts(i, CHUNK)], start=True,
                          stop=True).then_inc(mm["d_ps"].sem, 1)

            def outp(i, e):
                if e == 0:
                    pe.wait_ge(*mm["oc"](i + 1))
                    for part in range(2):
                        pe.matmul(ps[:, 6, :], b2s[:, part, :], DT[:, bass.ts(i, CHUNK)], start=(part == 0), stop=False)
                pe.wait_ge(*mm["hid"](i * U2 + (2 * e + 5)))
                for h in range(2):
                    u = 2 * e + h
                    pe.matmul(ps[h * C:(h + 1) * C, 6, :], w2_6[:, e, h, :], HID[u % 8][:, :], start=False,
                              stop=(e == E2 - 1)).then_inc(mm["o_ps"].sem, 1)

            def chunk(i, prev):
                for e in range(E2):
                    hidden(i, 2 * e)
                    hidden(i, 2 * e + 1)
                    spread(i, e)
                    if e >= 1:
                        outp(i, e - 1)
                    elif prev is not None:
                        outp(prev, E2 - 1)
                    if e == 2 and prev is not None:
                        back(prev)

            def back(i):
                pe.wait_ge(*mm["oc"](i + 2))
                pe.wait_ge(*mm["ta"](i + 1))
                for t in range(4):
                    last = pe.transpose(ps[:, 7, t * P:(t + 1) * P], OS[:, t * P:(t + 1) * P], ident[:, :])
                last.then_inc(mm["t_ps"].sem, 1)
            chunk(0, None)
            with pe.Fori(1, NCHUNK) as i:
                chunk(i, i - 1)
            outp(NCHUNK - 1, E2 - 1)
            back(NCHUNK - 1)
        retire(sig5)
        sig7 = signals((G, "q_var q_rstd q_fs"), (NCHUNK, "q_ft_ps q_xp q_cv_ps q_cv q_t_ps q_ta x7"),
                       (1, "q_wt q_wps q_w"))
        m.update(sig7)
        ROUND = 1.5 * 2 ** 23

        def q_sync(sp):
            sp.wait_ge(*m["x5"](G))
            wdma(sp, "cw", cw_raw[:, :], a["L3_conv_w"].rearrange("o c h w -> o (c h w)"))

        def q_pool(pool):
            ln_pool(pool, 1e-6, m["q_var"], m["q_rstd"])

        def q_vector(dve):
            wwait(dve, "cw")
            dve.tensor_reduce(amax[0][:, :], cw_raw[:, :], X_AXIS, ALU.max)
            vlink(dve.tensor_reduce(amax[2][:, :], cw_raw[:, :], X_AXIS, ALU.min, negate=True))
            vlink(dve.tensor_tensor(amax[1][:, :], amax[0][:, :], amax[2][:, :], ALU.max))
            vlink(dve.tensor_scalar(amax[2][:, :], amax[1][:, :], 1.0 / 7.0, None, ALU.mult))
            vlink(dve.scalar_tensor_tensor(amax[0][:, :], amax[2][:, :], -8.0, amax[1][:, :], ALU.mult, ALU.add))
            vlink(dve.tensor_tensor(amax[0][:, :], amax[0][:, :], amax[2][:, :], ALU.add))
            vlink(dve.scalar_tensor_tensor(amax[2][:, :], amax[0][:, :], 1.0 / 7.0, amax[2][:, :], ALU.mult, ALU.add))
            vlink(dve.tensor_scalar(amax[3][:, :], amax[2][:, :], 2e-16, None, ALU.max))
            vlink(dve.tensor_copy(sc_hi[:, :], amax[3][:, :]))
            dve.tensor_tensor(nsc[1][:, :], sc_hi[:, :].bitcast(F32), amax[3][:, :], ALU.subtract)
            dve.tensor_scalar(nsc[0][:, :], sc_hi[:, :].bitcast(F32), -1.0, None, ALU.mult)
            vlink(dve.reciprocal(amax[0][:, :], amax[3][:, :]))
            vlink(dve.tensor_scalar(cw_q[0][:, :], cw_raw[:, :], amax[0][:, :], None, ALU.mult))
            vlink(dve.tensor_copy(cq_hi[:, :], cw_q[0][:, :]))
            vlink(dve.tensor_tensor(cq_lo[:, :], cw_q[0][:, :], cq_hi[:, :].bitcast(F32), ALU.subtract))
            vlink(dve.scalar_tensor_tensor(cw_q[1][:, :], cq_hi[:, :].bitcast(F32), nsc[0][:, :], cw_raw[:, :], ALU.mult, ALU.add))
            for q, sc in ((cq_hi[:, :].bitcast(F32), 1), (cq_lo[:, :], 0), (cq_lo[:, :], 1)):
                vlink(dve.scalar_tensor_tensor(cw_q[1][:, :], q, nsc[sc][:, :], cw_q[1][:, :], ALU.mult, ALU.add))
            vlink(dve.scalar_tensor_tensor(cw_q[0][:, :], cw_q[1][:, :], amax[0][:, :], cw_q[0][:, :], ALU.mult, ALU.add))
            vlink(dve.tensor_scalar(cw_q[1][:, :], cw_q[0][:, :], ROUND, None, ALU.add))
            vlink(dve.tensor_scalar(cw_q[0][:, :], cw_q[1][:, :], -ROUND, None, ALU.add))
            vlink(dve.tensor_scalar(cw_q[1][:, :], cw_q[0][:, :], 7.0, -7.0, ALU.min, ALU.max))
            vlink(dve.tensor_scalar(cw_q[0][:, :], cw_q[1][:, :], amax[3][:, :], None, ALU.mult))
            vlink(dve.tensor_tensor(cw_q[1][:, :], cw_q[0][:, :], cw_raw[:, :], ALU.subtract))
            dve.tensor_tensor(cw_q[0][:, :], cw_raw[:, :], cw_q[1][:, :], ALU.add).then_inc(m["q_wt"].sem, 1)
            dve.wait_ge(*m["q_wps"](1))
            for h in range(2):
                hs = slice(h * C, (h + 1) * C)
                dve.tensor_copy(cw_t[hs, 0:8, :], ps[0:C, 2, :].rearrange("p (t o) -> p t o", o=C))
                last = dve.tensor_copy(cw_t[hs, 8, :], ps[0:C, 3, 0:C])
            vlink(last)
            vlink(dve.tensor_copy(cw[:, :, 0, :], cw_t[:, :, :]))
            dve.tensor_tensor(cw[:, :, 1, :], cw_t[:, :, :], cw[:, :, 0, :].bitcast(F32), ALU.subtract).then_inc(m["q_w"].sem, 1)

            ln_vector(dve, e2["x"], m["q_var"], m["q_rstd"], m["q_fs"], m["q_ft_ps"], x_per=2)
            for j in range(NCHUNK):
                sl = slice(4 * j, 4 * j + 4)
                dve.wait_ge(*m["q_t_ps"](j + 1))
                dve.tensor_reduce(OA[:, :, :], ps[:, 4 + j % 2, :].rearrange("p (t h c) -> p t c h", h=2, c=C), X_AXIS,
                                  ALU.add).then_inc(m["q_ta"].sem, 1)
                dve.wait_ge(*m["q_ta"](j + 1))
                dve.tensor_tensor(X[:, sl, :], X[:, sl, :], OA[:, :, :], ALU.add).then_inc(m["x7"].sem, 1)
                dve.wait_ge(*m["x7"](j + 1))

        def q_scalar(act):
            def padded(g):
                if g >= 2:
                    act.wait_ge(*m["q_cv_ps"](2 * (g - 1)))
                for j in range(2):
                    act.wait_ge(*m["q_ft_ps"](2 * g + j + 1))
                    to_padded(act, j, XP[g % 2], j, m["q_xp"])

            def move(j):
                act.wait_ge(*m["q_cv_ps"](j + 1))
                if j >= 2:
                    act.wait_ge(*m["q_t_ps"](j - 1))
                act.activation(CQ[j % 2][:, :], ps[:, 2 + j % 2, :], ACT.Copy).then_inc(m["q_cv"].sem, 1)
            padded(0)
            for g in range(G):
                if g + 1 < G:
                    padded(g + 1)
                move(2 * g)
                move(2 * g + 1)

        def q_tensor(pe):
            pe.wait_ge(*m["q_wt"](1))
            wv = cw_q[0][:, :].rearrange("o (c t) -> o t c", t=9)
            for t in range(9):
                last = pe.matmul(ps[0:C, 2 + t // 8, (t % 8) * C:(t % 8 + 1) * C], wv[:, t, :], ident[0:C, 0:C], is_transpose=True)
            last.then_inc(m["q_wps"].sem, 1)
            pe.wait_ge(*m["q_w"](1))

            def tr(g):
                pe.wait_ge(*m["q_fs"](g + 1))
                if g >= 1:
                    pe.wait_ge(*m["q_xp"](2 * g))
                transpose_tiles(pe, US[g % 2], (0, 1), m["q_ft_ps"])

            def conv(j):
                g, jj = j // 2, j % 2
                xp = XP[g % 2][:, :, :].rearrange("p b (y x) -> p b y x", x=PADW)
                pe.wait_ge(*m["q_xp"](j + 1))
                if j >= 2:
                    pe.wait_ge(*m["q_cv"](j - 1))
                for t in range(9):
                    dy, dx = t // 3, t % 3
                    last = pe.matmul(ps[:, 2 + jj, :], cw[:, t, :, :].rearrange("p h c -> p (h c)"),
                                     xp[:, 2 * jj:2 * jj + 2, dy:dy + H, dx:dx + W], start=(t == 0), stop=(t == 8))
                last.then_inc(m["q_cv_ps"].sem, 1)

            def back(j):
                pe.wait_ge(*m["q_cv"](j + 1))
                if j >= 2:
                    pe.wait_ge(*m["q_ta"](j - 1))
                for t in range(4):
                    half, r = t // 2, t % 2
                    c0 = r * PIX + half * P
                    last = pe.transpose(ps[:, 4 + j % 2, t * P:(t + 1) * P], CQ[j % 2][:, c0:c0 + P], ident[:, :])
                last.then_inc(m["q_t_ps"].sem, 1)
            tr(0)
            for g in range(G):
                if g + 1 < G:
                    tr(g + 1)
                conv(2 * g)
                if g:
                    back(2 * g - 1)
                conv(2 * g + 1)
                back(2 * g)
            back(NCHUNK - 1)
        retire(e2)
        NU = 2 * B
        sig8 = signals((G, "i_var i_rstd i_fs i_u z_var z_rstd x8"), (NCHUNK, "i_ft_ps i_ft"),
                       (1, "i_mean_ps i_mean i_lg_ps i_l i_e i_rw i_ld_ps i_l2 i_e2 i_w i_we i_top i_tr_ps i_tr i_bc_ps i_ready i_whi i_wlo"),
                       (2 + NU, "i_h i_y_ps"), (NU, "i_h_ps i_ws"), (1 + NCHUNK, "i_yc i_t_ps i_z"))
        m.update(sig8)
        CAP = -(-TOK * 5 // 4 // E3)

        def i_sync(sp):
            wdma(sp, "i8", wr_8[:, :], a["L3_ffn_Wr"])
            wdma(sp, "i8", br_8[:, :], a["L3_ffn_br"].unsqueeze(0).to_broadcast([B, E3]))
            wdma(sp, "i8", gam[:, :], a["L3_ffn_gamma"].unsqueeze(0).to_broadcast([P, C]))
            wdma(sp, "i8", bet[:, :], a["L3_ffn_beta"].unsqueeze(0).to_broadcast([P, C]))
            for h in range(2):
                wdma(sp, "i8", w1_8raw[h * C:(h + 1) * C, :, :], a["L3_ffn_W1"].rearrange("e d f -> d e f"))
            wdma(sp, "i8", w2_8[:, :, :], a["L3_ffn_W2"].rearrange("e f o -> f e o"))
            wdma(sp, "i8", b1_8[:, :], a["L3_ffn_b1"])
            wdma(sp, "i8", b2_8[:, :], a["L3_ffn_b2"])

        def i_pool(pool):
            ln_pool(pool, 1e-5, m["i_var"], m["i_rstd"])
            ln_pool(pool, 1e-5, m["z_var"], m["z_rstd"])

        def i_vector(dve):
            wwait(dve, "i8")
            dve.wait_ge(*m["i_whi"](1))
            dve.tensor_tensor(w1_8[:, :, 1, :], w1_8raw[:, :, :], w1_8[:, :, 0, :].bitcast(F32), ALU.subtract).then_inc(m["i_wlo"].sem, 1)
            ln_vector(dve, m["x7"], m["i_var"], m["i_rstd"], m["i_fs"], m["i_ft_ps"], u_sem=m["i_u"], x_per=2)

            dve.wait_ge(*m["i_mean_ps"](1))
            dve.tensor_scalar(mean8[:, :], ps[0:C, 2, 0:B], 1.0 / PIX, None, ALU.mult).then_inc(m["i_mean"].sem, 1)
            dve.wait_ge(*m["i_lg_ps"](1))
            vlink(dve.tensor_tensor(im[0][:, :], ps[0:B, 3, 0:E3], br_8[:, :], ALU.add))
            vlink(dve.tensor_reduce(i1[0][:, :], im[0][:, :], X_AXIS, ALU.max))
            dve.tensor_scalar(im[1][:, :], im[0][:, :], i1[0][:, :], None, ALU.subtract).then_inc(m["i_l"].sem, 1)
            dve.wait_ge(*m["i_e"](1))
            vlink(dve.tensor_reduce(i1[0][:, :], im[2][:, :], X_AXIS, ALU.add))
            vlink(dve.reciprocal(i1[1][:, :], i1[0][:, :]))
            dve.tensor_scalar(im[3][:, :], im[2][:, :], i1[1][:, :], None, ALU.mult).then_inc(m["i_rw"].sem, 1)
            dve.wait_ge(*m["i_ld_ps"](1))
            vlink(dve.tensor_scalar(im[4][:, :], ps[0:B, 3, 0:E3], float(PIX), None, ALU.mult))
            vlink(dve.reciprocal(im[5][:, :], im[4][:, :]))
            vlink(dve.tensor_scalar(im[4][:, :], im[5][:, :], float(CAP), 1.0, ALU.mult, ALU.min))
            vlink(dve.tensor_tensor(im[0][:, :], im[3][:, :], im[4][:, :], ALU.mult))
            vlink(dve.tensor_reduce(i1[0][:, :], im[0][:, :], X_AXIS, ALU.max))
            dve.tensor_scalar(im[1][:, :], im[0][:, :], i1[0][:, :], None, ALU.subtract).then_inc(m["i_l2"].sem, 1)
            dve.wait_ge(*m["i_e2"](1))
            vlink(dve.tensor_reduce(i1[0][:, :], im[2][:, :], X_AXIS, ALU.add))
            vlink(dve.reciprocal(i1[1][:, :], i1[0][:, :]))
            vlink(dve.tensor_scalar(im[3][:, :], im[2][:, :], i1[1][:, :], None, ALU.mult))
            rv = rev[0:B, 0:E3]
            for k in range(2):
                prob = im[3] if k == 0 else im[6]
                vlink(dve.tensor_reduce(i1[2 + k][:, :], prob[:, :], X_AXIS, ALU.max))
                vlink(dve.tensor_scalar(im[4][:, :], prob[:, :], i1[2 + k][:, :], None, ALU.is_equal))
                vlink(dve.tensor_tensor(im[5][:, :], im[4][:, :], rv, ALU.mult))
                vlink(dve.tensor_reduce(i1[1][:, :], im[5][:, :], X_AXIS, ALU.max))
                dve.tensor_scalar(iw[:, k, 0:1], i1[1][:, :], -1.0, 16.0, ALU.mult, ALU.add)
                vlink(dve.tensor_scalar(hot[:, k, :], im[5][:, :], i1[1][:, :], None, ALU.is_equal))
                if k == 0:
                    vlink(dve.scalar_tensor_tensor(im[6][:, :], hot[:, 0, :], -2.0, im[3][:, :], ALU.mult, ALU.add))
            dve.tensor_tensor(i1[0][:, :], i1[3][:, :], i1[2][:, :], ALU.subtract).then_inc(m["i_w"].sem, 1)
            dve.wait_ge(*m["i_we"](1))
            vlink(dve.tensor_scalar(i1[3][:, :], i1[1][:, :], 1.0, None, ALU.add))
            vlink(dve.reciprocal(iw[:, 0, 1:2], i1[3][:, :]))
            vlink(dve.tensor_tensor(iw[:, 1, 1:2], i1[1][:, :], iw[:, 0, 1:2], ALU.mult))
            vlink(dve.tensor_scalar(im[0][:, :], hot[:, 0, :], iw[:, 0, 1:2], None, ALU.mult))
            dve.scalar_tensor_tensor(im[7][:, :], hot[:, 1, :], iw[:, 1, 1:2], im[0][:, :], ALU.mult, ALU.add)
            dve.tensor_tensor(dia[:, :, :, :].rearrange("p b k v -> p b (k v)"), bc(ident[0:B, 0:B], 4),
                              bcm(iw[:, :, :].rearrange("p k v -> p (k v)"), B), ALU.mult).then_inc(m["i_top"].sem, 1)
            dve.wait_ge(*m["i_tr_ps"](1))
            tp = ps[0:E3, 2, :]
            dve.tensor_copy(hotT[:, :, :].rearrange("p k b -> p (k b)"), tp[:, 0:2 * B])
            dve.tensor_copy(dwT[:, :], tp[:, 2 * B:3 * B])
            pairs = ps[:, 2, P:P + 4 * B].rearrange("p (n v) -> p n v", v=2)
            dve.tensor_copy(idx[:, :], pairs[:, :, 0])
            dve.tensor_copy(wsel[:, :], pairs[:, :, 1]).then_inc(m["i_tr"].sem, 1)
            dve.wait_ge(*m["i_bc_ps"](1))
            dve.tensor_copy(b1u[:, :, :].rearrange("p k b -> p (k b)"), ps[:, 3, 0:2 * B])
            dve.tensor_copy(b2u[:, :], ps[:, 3, 2 * B:2 * B + B // 2]).then_inc(m["i_ready"].sem, 1)
            dve.wait_ge(*m["i_ready"](1))
            dve.sem_inc(m["i_z"].sem, 1)

            def finish(i):
                dve.wait_ge(*m["i_t_ps"](i + 2))
                us_ = U[:, bass.ts(i, 4), :]
                dve.tensor_tensor(us_, us_, ps[:, 7, 0:4 * C].rearrange("p (t c) -> p t c", c=C), ALU.add).then_inc(m["i_z"].sem, 1)

            def chunk(i, prev):
                for n in range(4):
                    e = dve.value_load(idx[0:1, bass.ds(i * 4 + n, 1)], min_val=0, max_val=E3 - 1)
                    dve.wait_ge(*m["i_y_ps"](i * 4 + (n + 1)))
                    dve.tensor_copy(W1S[n % 2][:, :, :], w1_8[:, bass.ds(e, 1), :, :].rearrange("p e h f -> p (e h) f"))
                    dve.tensor_scalar(W2S[n % 2][:, :], w2_8[:, bass.ds(e, 1), :].rearrange("p e c -> p (e c)"),
                                      wsel[:, bass.ds(i * 4 + n, 1)], None, ALU.mult).then_inc(m["i_ws"].sem, 1)
                if prev is not None:
                    finish(prev)
            chunk(0, None)
            with dve.Fori(1, NCHUNK) as i:
                chunk(i, i - 1)
            finish(NCHUNK - 1)
            dve.wait_ge(*m["i_z"](NCHUNK + 1))

            def zstats(g):
                ln_stats(dve, g, U[:, g * TG:(g + 1) * TG, :], m["z_var"])
                dve.wait_ge(*m["z_var"](g + 1))
            zstats(0)
            for g in range(G):
                sl = slice(g * TG, (g + 1) * TG)
                xc = XC[g % 2][:, :, :]
                if g + 1 < G:
                    zstats(g + 1)
                vlink(ln_center(dve, g, U[:, sl, :], xc))
                dve.wait_ge(*m["z_rstd"](g + 1))
                vlink(dve.tensor_tensor(xc, xc, bc(rstd[:, sl], C), ALU.mult))
                vlink(dve.tensor_tensor(xc, xc, bcm(gam[:, :], TG), ALU.mult))
                vlink(dve.tensor_tensor(xc, xc, bcm(bet[:, :], TG), ALU.add))
                dve.tensor_tensor(X[:, sl, :], X[:, sl, :], xc, ALU.add).then_inc(m["x8"].sem, 1)

        def i_scalar(act):
            wwait(act, "i8")
            act.activation(w1_8[:, :, 0, :], w1_8raw[:, :, :], ACT.Copy).then_inc(m["i_whi"].sem, 1)
            ln_scalar(act, m["i_ft_ps"], m["i_ft"])
            act.wait_ge(*m["i_l"](1))
            act.activation(im[2][:, :], im[1][:, :], ACT.Exp).then_inc(m["i_e"].sem, 1)
            act.wait_ge(*m["i_l2"](1))
            act.activation(im[2][:, :], im[1][:, :], ACT.Exp).then_inc(m["i_e2"].sem, 1)
            act.wait_ge(*m["i_w"](1))
            act.activation(i1[1][:, :], i1[0][:, :], ACT.Exp).then_inc(m["i_we"].sem, 1)
            act.wait_ge(*m["i_ready"](1))
            act.sem_inc(m["i_yc"].sem, 1)
            act.sem_inc(m["i_h"].sem, 2)

            def chunk(i, prev):
                for n in range(4):
                    act.wait_ge(*m["i_h_ps"](i * 4 + (n + 1)))
                    act.wait_ge(*m["i_y_ps"](i * 4 + (n + 1)))
                    act.activation(GH[n % 2][:, :], ps[:, 4 + n % 2, 0:PIX], ACT.Gelu,
                                   bias=b1u[:, n % 2, bass.ds(i * 2 + n // 2, 1)]).then_inc(m["i_h"].sem, 1)
                act.wait_ge(*m["i_y_ps"](i * 4 + 6))
                act.wait_ge(*m["i_t_ps"](i + 1))
                act.activation(YS[:, :], ps[:, 6, 0:PIX], ACT.Identity, bias=b2u[:, bass.ds(i, 1)]).then_inc(m["i_yc"].sem, 1)
            chunk(0, None)
            with act.Fori(1, NCHUNK) as i:
                chunk(i, None)

        def i_tensor(pe):
            pe.wait_ge(*m["x7"](NCHUNK))
            ln_tensor(pe, m["i_fs"], m["i_ft_ps"], m["i_ft"])
            pe.wait_ge(*m["i_u"](G))
            for b in range(B):
                q, r = b // 2, b % 2
                for half in range(2):
                    last = pe.matmul(ps[0:C, 2, b:b + 1], U[:, q * 4 + half * 2 + r, :], ones[:, 0:1], start=(half == 0), stop=(half == 1))
            last.then_inc(m["i_mean_ps"].sem, 1)
            pe.wait_ge(*m["i_mean"](1))
            wwait(pe, "i8")
            pe.matmul(ps[0:B, 3, 0:E3], mean8[:, :], wr_8[:, :], start=True, stop=True).then_inc(m["i_lg_ps"].sem, 1)
            pe.wait_ge(*m["i_rw"](1))
            pe.matmul(ps[0:B, 3, 0:E3], ones[0:B, 0:B], im[3][:, :], start=True, stop=True).then_inc(m["i_ld_ps"].sem, 1)
            pe.wait_ge(*m["i_top"](1))
            for k in range(2):
                pe.transpose(ps[0:E3, 2, k * B:(k + 1) * B], hot[:, k, :], ident[0:B, 0:B])
            pe.transpose(ps[0:E3, 2, 2 * B:3 * B], im[7][:, :], ident[0:B, 0:B])
            pe.matmul(ps[:, 2, P:P + 4 * B], ones[0:B, :], dia[:, :, :, :].rearrange("p b k v -> p (b k v)"), start=True,
                      stop=True).then_inc(m["i_tr_ps"].sem, 1)
            pe.wait_ge(*m["i_tr"](1))
            pe.matmul(ps[:, 3, 0:2 * B], b1_8[:, :], hotT[:, :, :].rearrange("p k b -> p (k b)"), start=True, stop=True)
            dv = dwT[:, :].rearrange("p (q r) -> p r q", r=2)
            for r in range(2):
                last = pe.matmul(ps[r * C:(r + 1) * C, 3, 2 * B:2 * B + B // 2], b2_8[:, :], dv[:, r, :], start=True, stop=True)
            last.then_inc(m["i_bc_ps"].sem, 1)
            pe.wait_ge(*m["i_ready"](1))
            pe.wait_ge(*m["i_ft"](NCHUNK))
            pe.sem_inc(m["i_y_ps"].sem, 2)
            pe.sem_inc(m["i_t_ps"].sem, 1)

            def chunk(i, prev):
                cols = UT[:, bass.ts(i, CHUNK)].rearrange("p (h r s) -> p r h s", h=2, r=2)

                def hidden(n):
                    pe.wait_ge(*m["i_ws"](i * 4 + (n + 1)))
                    pe.wait_ge(*m["i_h"](i * 4 + (n + 1)))
                    for part in range(2):
                        last = pe.matmul(ps[:, 4 + n % 2, 0:PIX], W1S[n % 2][:, part, :], cols[:, n // 2, :, :],
                                         start=(part == 0), stop=(part == 1))
                    last.then_inc(m["i_h_ps"].sem, 1)

                def outp(n):
                    r, k = n // 2, n % 2
                    pe.wait_ge(*m["i_h"](i * 4 + (n + 3)))
                    if n == 0:
                        pe.wait_ge(*m["i_yc"](i + 1))
                    pe.matmul(ps[r * C:(r + 1) * C, 6, 0:PIX], W2S[n % 2][:, :], GH[n % 2][:, :], start=(k == 0),
                              stop=(k == 1)).then_inc(m["i_y_ps"].sem, 1)
                for n in range(5):
                    if n < 4:
                        hidden(n)
                    if n == 1 and prev is not None:
                        back(prev)
                    if n >= 1:
                        outp(n - 1)

            def back(i):
                pe.wait_ge(*m["i_yc"](i + 2))
                pe.wait_ge(*m["i_z"](i + 1))
                for h in range(2):
                    last = pe.transpose(ps[:, 7, h * P:(h + 1) * P], YS[:, h * P:(h + 1) * P], ident[:, :])
                last.then_inc(m["i_t_ps"].sem, 1)
            chunk(0, None)
            with pe.Fori(1, NCHUNK) as i:
                chunk(i, i - 1)
            back(NCHUNK - 1)
        x_ready = {7: m["x7"], 8: m["x8"]}[min(stop, LAST)]

        s_ot = sem("o_ps"); s_oc = sem("o_copied"); s_out = sem("o_stored")
        s_fin = x_ready
        XM = 2 if min(stop, LAST) in (4, 6, 7) else 1

        def o_tensor(pe):
            for g in range(G):
                pe.wait_ge(*s_fin((g + 1) * XM))
                if g >= 2:
                    pe.wait_ge(s_oc, g - 1)
                for i in range(4):
                    t = g * TG + 2 * i
                    last = pe.transpose(ps[:, g % 2, i * P:(i + 1) * P], X[:, t:t + 2, :].rearrange("p t c -> p (t c)"), ident[:, :])
                last.then_inc(s_ot, 1)
        OUTB = XIN

        def o_scalar(act):
            for g in range(G):
                act.wait_ge(s_ot, g + 1)
                act.activation(OUTB[:, 2 * g:2 * g + 2, :].rearrange("p q s -> p (q s)"), ps[:, g % 2, :], ACT.Copy).then_inc(s_oc, 1)

        def o_sync(sp):
            ov = out.rearrange("(q r) c h w -> (r c) q (h w)", r=2)
            for g in range(G):
                sp.wait_ge(s_oc, g + 1)
                sp.dma_start(ov[:, 2 * g:2 * g + 2, :], OUTB[:, 2 * g:2 * g + 2, :]).then_inc(s_out, 16)
            sp.wait_ge(s_out, 16 * G)

        block = ctx.enter_context(nc.Block())
        @block.sync
        def _(sp):
            load_sync(sp)
            f_sync(sp)
            v_sync(sp)
            e1_sync(sp)
            d_sync(sp)
            e2_sync(sp)
            q_sync(sp)
            i_sync(sp)
            o_sync(sp)

        @block.gpsimd
        def _(pool):
            consts_pool(pool)
            c0_pool(pool)
            f_pool(pool)
            v_pool(pool)
            e1_pool(pool)
            d_pool(pool)
            e2_pool(pool)
            q_pool(pool)
            i_pool(pool)

        @block.scalar
        def _(act):
            xt_scalar(act)
            c0_scalar(act)
            u_scalar(act)
            t_scalar(act)
            f_scalar(act)
            v_scalar(act)
            e1_whi(act)
            e1_scalar2(act)
            d_scalar(act)
            e2_scalar(act)
            q_scalar(act)
            i_scalar(act)
            o_scalar(act)

        @block.vector
        def _(dve):
            vlink(dve.memset(b2_6[:, :], 0.0))
            w0_vector(dve)
            c0_vector(dve)
            u_vector(dve)
            t_vector(dve)
            f_weights(dve)
            f_vector(dve)
            v_consts(dve)
            v_vector(dve)
            e1_consts(dve)
            e1_vector(dve)
            d_vector(dve)
            e2_vector(dve)
            q_vector(dve)
            i_vector(dve)

        @block.tensor
        def _(pe):
            w0_tensor(pe)
            xt_tensor(pe)
            c0_tensor(pe)
            u_tensor(pe)
            t_tensor(pe)
            f_tensor(pe)
            v_tensor(pe)
            e1_tensor(pe)
            d_tensor(pe)
            e2_tensor(pe)
            q_tensor(pe)
            i_tensor(pe)
            o_tensor(pe)


_OUT = (B, C, H, W)


def kernel(**inputs):
    import numpy as np
    import concourse.bacc as bacc
    from concourse.bass_utils import run_bass_kernel_spmd as run

    nc = bacc.Bacc("TRN2", target_bir_lowering=False, num_devices=1)
    arrays, aps = {}, {}
    for name, value in inputs.items():
        v = np.ascontiguousarray(value)
        arrays["in_" + name] = v
        aps[name] = nc.dram_tensor("in_" + name, v.shape, mybir.dt.from_np(v.dtype), kind="ExternalInput").ap()
    out = nc.dram_tensor("out", _OUT, F32, kind="ExternalOutput").ap()
    build(nc, aps, out)
    return run(nc, [arrays], core_ids=[0]).results[0]["out"]
```

```python
from contextlib import ExitStack, contextmanager

import concourse.bass as bass
from concourse import mybir

F32 = mybir.dt.float32
F32R = mybir.dt.float32r
I32 = mybir.dt.int32
U32 = mybir.dt.uint32
ALU = mybir.AluOpType
ACT = mybir.ActivationFunctionType
X_AXIS = mybir.AxisListType.X

P = 128
B, C, H, W = 16, 64, 16, 16
PIX = H * W
TOK = B * PIX
NT = TOK // P
G = 4
TG = NT // G
BG = B // G
QG = BG // 2
CHUNK = 512
NCHUNK = TOK // CHUNK
PADW = W + 2
PADPIX = (H + 2) * PADW
K0 = 32
FFN0 = 256
TOPK0 = PIX // 2 - 1
E1, H1 = 16, 128
E2, H2 = 8, 256
E3, H3 = 8, 128
LAST = 8
HEADS, DH = 8, 16
INNER = HEADS * DH


def build(nc, a, out, stop=99):
    ctx = ExitStack()
    with ctx:
        SIZE = dict(all=75 * 1024, early=79 * 1024, gated=52 * 1024)
        BASE = dict(all=(nc.sbuf_base + 31) // 32 * 32)
        BASE["early"] = BASE["all"] + SIZE["all"]
        BASE["gated"] = BASE["early"] + SIZE["early"]
        SIZE["early"] -= 8 * 1024
        BASE["fc"] = BASE["hg"] = BASE["early"] + SIZE["early"]
        SIZE["fc"] = SIZE["hg"] = 8 * 1024
        BASE["late"], BASE["mid"] = BASE["gated"], BASE["early"]
        BASE["last"], SIZE["last"] = BASE["gated"], 45 * 1024
        SIZE["late"], SIZE["mid"] = SIZE["gated"], SIZE["early"] + SIZE["hg"]
        used = dict.fromkeys(BASE, 0)
        place = {}

        def sb(name, shape, dt=F32, region="all"):
            size = 4
            for d in shape[1:]:
                size *= d
            at = BASE[region] + used[region]
            used[region] += (size + 31) // 32 * 32
            assert used[region] <= SIZE[region], (name, region, used[region])
            place[name] = at
            return nc.alloc_sbuf_tensor_at(name, shape, dt, offset=at)

        def over(name, other, shape, dt=F32):
            return nc.alloc_sbuf_tensor_at(name, shape, dt, offset=place[other])

        def sem(name):
            return ctx.enter_context(nc.semaphore(name))

        class Signal:

            def __init__(self, handle, base):
                self.sem, self.base = handle, base

            def __call__(self, count):
                return self.sem, self.base + count

        free = []

        def signals(*counts):
            made = {}
            for total, names in counts:
                for name in names.split():
                    handle, base = free.pop(0) if free else (sem(name), 0)
                    made[name] = Signal(handle, base)
                    made[name].total = total
            return made

        def retire(made):
            free.extend((x.sem, x.base + x.total) for name, x in made.items() if name[0] != "x")

        ps = ctx.enter_context(nc.psum_tensor("ps", [P, 8, 512], F32))

        ident = sb("ident", [P, P])
        ones = sb("ones", [P, P])
        neghalf = sb("neghalf", [P, NT])
        eps_c = sb("eps_c", [P, 4])
        band = sb("band", [P, 4])
        X = sb("X", [P, NT, C])
        XIN = sb("XIN", [P, B // 2, PIX])
        U = sb("U", [P, NT, C])
        Y = XIN[:, :, :].rearrange("p q s -> p (q s)").rearrange("p (t c) -> p t c", c=C)
        XC = [sb(f"XC{i}", [P, TG, C]) for i in range(2)]
        US = [sb(f"US{i}", [P, TG, 2, C], F32R) for i in range(2)]
        UT = sb("UT", [P, TOK], F32R)
        ST = sb("ST", [P, NT, 6])
        S1_ = sb("S1_", [P, NT])
        S2_ = sb("S2_", [P, NT])
        S3_ = sb("S3_", [P, NT])
        S4_ = sb("S4_", [P, NT])
        var = sb("var", [P, NT])
        vpe = sb("vpe", [P, NT])
        rstd = sb("rstd", [P, NT])
        nmean = sb("nmean", [P, NT])
        nmr = sb("nmr", [P, NT])
        n2 = sb("n2", [P, NT])
        n2b = sb("n2b", [P, NT])
        n2c = sb("n2c", [P, NT])
        rn = sb("rn", [P, NT])
        XP = [sb(f"XP{i}", [P, BG, PADPIX], F32R) for i in range(2)]
        XN = [sb(f"XN{i}", [P, TG, P], region="early") for i in range(2)]
        XS = [sb(f"XS{i}", [P, TG, 2, C], F32R, region="early") for i in range(2)]
        CV = [sb(f"CV{i}", [C, CHUNK], region="early") for i in range(2)]
        L = sb("L", [P, TG, K0], region="early")
        L2 = sb("L2", [P, TG, K0], region="early")
        LE = sb("LE", [P, TG, K0], region="early")
        SA = [sb(f"SA{i}", [P, TG, K0], region="early") for i in range(2)]
        R8 = [sb(f"R8_{i}", [P, TG]) for i in range(4)]
        w_cu_raw = sb("w_cu_raw", [K0, C * 9], region="early")
        w_cu_t = sb("w_cu_t", [P, 9, K0], region="early")
        w_cu = sb("w_cu", [P, 9, 2, K0], F32R, region="early")
        b_cu = sb("b_cu", [C, 1])
        cent_raw = sb("cent_raw", [K0, C], region="early")
        centT = sb("centT", [C, K0], region="early")
        fc_raw = sb("fc_raw", [C, K0 * C], region="fc")
        fcT = sb("fcT", [P, K0 // 2, C], region="early")
        b_fc = sb("b_fc", [C, 1])
        t1_raw = sb("t1_raw", [C, 2 * C], region="early")
        t1a_t = sb("t1a_t", [P, C], region="early")
        t1a = sb("t1a", [P, 2, 2, C], F32R, region="early")
        t1b = sb("t1b", [C, 2, C], region="early")
        b_t1 = sb("b_t1", [P, 1])
        t2_raw = sb("t2_raw", [C, C], region="early")
        t2_t = sb("t2_t", [P, C], region="early")
        t2 = sb("t2", [P, 2, C], F32R, region="early")
        b_t2 = sb("b_t2", [P, C], region="early")
        EC = [sb(f"EC{i}", [C, B, K0], region="early") for i in range(4)]
        tb = [sb(f"tb{i}", [C, B], region="early") for i in range(4)]
        upn2 = sb("upn2", [P, K0 // 2, B], region="early")
        upv = sb("upv", [C, B], region="early")
        V = sb("V", [P, B], region="early")
        HR = [sb(f"HR{i}", [P, CHUNK], region="early") for i in range(2)]
        HS = [sb(f"HS{i}", [P, CHUNK], F32R, region="early") for i in range(2)]
        OT = [sb(f"OT{i}", [P, TG, C], region="early") for i in range(2)]

        wr0 = sb("wr0", [P, C], region="early")
        br0 = sb("br0", [P, 1])
        f1_raw = sb("f1_raw", [P, FFN0], region="early")
        f1 = sb("f1", [P, 2, FFN0], F32R, region="early")
        b_f1 = sb("b_f1", [P, 2])
        f2 = sb("f2", [P, 2, C], region="early")
        b_f2 = sb("b_f2", [P, C], region="early")
        wl = sb("wl", [P, 2, B], region="early")
        wm = sb("wm", [P, NT])
        tk = sb("tk", [B, PIX + 1], region="early")
        m8 = sb("m8", [B, 8], region="early")
        HG = [sb(f"HG{i}", [P, 2, CHUNK], region="hg") for i in range(2)]
        YT = [sb(f"YT{i}", [C, CHUNK], region="early") for i in range(2)]
        rev = sb("rev", [P, 16])
        pidx = sb("pidx", [P, 1], I32)
        pbit = [sb(f"pbit{i}", [P, 1], I32) for i in range(3)]
        wenc = sb("wenc", [C, 1])
        wencb = sb("wencb", [C, C])
        b_enc = sb("b_enc", [C, 1])
        l1w1_raw = sb("l1w1_raw", [C // 2, C])
        l1w2_raw = sb("l1w2_raw", [C, C // 2])
        l1w1T = sb("l1w1T", [C, C // 2])
        l1w2T = sb("l1w2T", [C // 2, C])
        ori = sb("ori", [C, B, 4], region="mid")
        ba = [sb(f"ba{i}", [C, B, 4], region="mid") for i in range(4)]
        bs = [sb(f"bs{i}", [C, B], region="mid") for i in range(4)]
        sg = sb("sg", [C, B], region="mid")
        hq = sb("hq", [C // 2, B], region="mid")

        gw = sb("gw", [P, E1])
        gw2 = sb("gw2", [P, 2, E1], F32R)
        b_gw = sb("b_gw", [P, E1])
        w12_raw = sb("w12_raw", [P, 2, E1, H1], region="gated")
        w12 = sb("w12", [P, 2, 2, E1, H1], F32R, region="gated")
        w3 = sb("w3", [P, E1, C], region="gated")
        DS = [sb(f"DS{i}", [P, TG, P], F32R, region="mid") for i in range(2)]
        DT = sb("DT", [P, TOK], F32R, region="mid")
        sel = sb("sel", [P, E1], F32R)
        self32 = sb("self32", [P, E1])
        RT7 = sb("RT7", [P, NT, E1], region="mid")
        r8 = [sb(f"r8{i}", [P, NT], region="mid") for i in range(8)]
        SB = [sb(f"SB{i}", [P, CHUNK], region="mid") for i in range(2)]
        HID = [sb(f"HID{i}", [P, CHUNK], region="mid") for i in range(4)]
        HID += [US[i][:, :, :, :].rearrange("p t h c -> p (t h c)").bitcast(F32)[:, j * CHUNK:(j + 1) * CHUNK]
                for i in range(2) for j in range(2)]
        OS = sb("OS", [P, CHUNK], region="mid")
        RT = [x[:, :].rearrange("p (t e) -> p t e", e=E1) for x in HID[0:4] + SB + [OS]] + [RT7[:, :, :]]
        OA = sb("OA", [P, 4, C], region="mid")

        wq_raw = sb("wq_raw", [INNER, C])
        wq_t = sb("wq_t", [P, INNER], region="mid")
        wq = sb("wq", [P, 2, INNER], F32R)
        wkv_raw = sb("wkv_raw", [INNER, 2, C])
        wkv = sb("wkv", [P, 2, INNER], region="mid")
        wo_raw = sb("wo_raw", [C, INNER])
        wo = sb("wo", [INNER, C], region="mid")
        b_o = sb("b_o", [P, C])
        dw_raw = sb("dw_raw", [P, 9])
        dw_hi = sb("dw_hi", [P, 9], F32R)
        dw_lo = sb("dw_lo", [P, 9], region="mid")
        ident2 = sb("ident2", [P, C], region="mid")
        wdw = sb("wdw", [P, 9, 2, C], F32R, region="mid")
        hmask = sb("hmask", [P, INNER], region="mid")
        QL = sb("QL", [P, TG, INNER], region="late")
        QE = sb("QE", [P, TG, INNER], region="late")
        qr = [sb(f"qr{i}", [P, TG * HEADS], region="late") for i in range(3)]
        QT = sb("QT", [INNER, TOK], region="late")
        KD = [sb(f"KD{i}", [P, CHUNK], region="late") for i in range(2)]
        KE = HID[0:2]
        KT = [sb(f"KT{i}", [P, 4, INNER], region="late") for i in range(2)]
        VT = [sb(f"VT{i}", [P, 4, INNER], region="late") for i in range(2)]
        nkm = sb("nkm", [P, B], region="mid")
        ksum = sb("ksum", [P, B], region="mid")
        rks = sb("rks", [P, B], region="mid")
        CTX = sb("CTX", [INNER, B, INNER], region="late")

        gw_6 = sb("gw_6", [P, E2])
        gw2_6 = sb("gw2_6", [P, 2, E2], F32R)
        b_gw_6 = sb("b_gw_6", [P, E2])
        gsum = sb("gsum", [P, E2])
        lng_raw = sb("lng_raw", [E2, P])
        lnb_raw = sb("lnb_raw", [E2, C])
        lng = sb("lng", [P, E2])
        lnb = sb("lnb", [C, E2])
        b1_raw = sb("b1_raw", [2 * E2, P])
        b1_6 = sb("b1_6", [P, 2 * E2])
        b1_t = sb("b1_t", [P, 2 * E2])
        b2_6 = sb("b2_6", [P, P])
        b2s = sb("b2s", [P, 2, P], F32R)
        w1_raw = sb("w1_raw", [P, E2, H2], region="mid")
        w1_6 = sb("w1_6", [P, 2, E2, H2], F32R, region="mid")
        w1_whole = over("w1_whole", "w1_6", [P, 2, E2, H2])
        w2_6 = sb("w2_6", [P, E2, 2, C], region="late")

        cw_buf = over("cw_buf", "DT", [C, 4, 9 * C])
        cw_raw, cw_q1, cq_lo, cq_hi = [cw_buf[:, i, :] for i in range(4)]
        cq_hi = cq_hi.bitcast(F32R)
        cw_q = sb("cw_q", [C, C * 9], region="mid")
        amax = [sb(f"amax{i}", [C, 1], region="mid") for i in range(4)]
        sc_hi = sb("sc_hi", [C, 1], F32R, region="mid")
        nsc = [sb(f"nsc{i}", [C, 1], region="mid") for i in range(2)]
        cw_t = sb("cw_t", [P, 9, C], region="last")
        cw = sb("cw", [P, 9, 2, C], F32R, region="last")
        CQ = [sb(f"CQ{i}", [P, CHUNK], region="last") for i in range(2)]

        wr_8 = sb("wr_8", [P, E3], region="last")
        br_8 = sb("br_8", [B, E3], region="last")
        gam = sb("gam", [P, C], region="last")
        bet = sb("bet", [P, C], region="last")
        w1_8raw = sb("w1_8raw", [P, E3, H3], region="last")
        w1_8 = sb("w1_8", [P, E3, 2, H3], F32R, region="last")
        w2_8 = sb("w2_8", [P, E3, C], region="last")
        b1_8 = sb("b1_8", [E3, H3], region="last")
        b2_8 = sb("b2_8", [E3, C], region="last")
        tsum = sb("tsum", [P, B], region="last")
        mean8 = sb("mean8", [P, B], region="last")
        im = [sb(f"im{i}", [B, E3], region="last") for i in range(8)]
        i1 = [sb(f"i1_{i}", [B, 1], region="last") for i in range(4)]
        hot = sb("hot", [B, 2, E3], region="last")
        iw = sb("iw", [B, 2, 2], region="last")
        dia = sb("dia", [B, B, 2, 2], region="last")
        hotT = sb("hotT", [E3, 2, B], region="last")
        dwT = sb("dwT", [E3, B], region="last")
        idx = sb("idx", [P, 2 * B], I32, region="last")
        wsel = sb("wsel", [P, 2 * B], region="last")
        b1u = sb("b1u", [P, 2, B], region="last")
        b2u = sb("b2u", [P, B // 2], region="last")
        W1S = [sb(f"W1S{i}", [P, 2, H3], F32R, region="last") for i in range(8)]
        W2S = [sb(f"W2S{i}", [P, C], region="last") for i in range(8)]
        GH = [HID[i // 2][:, (i % 2) * PIX:(i % 2 + 1) * PIX] for i in range(8)]
        YS = [sb(f"YS{i}", [P, PIX], region="last") for i in range(2)]

        class Chain:
            def __init__(self, eng, name):
                self.eng, self.sem, self.count, self.turn = eng, sem("chain_" + name), 0, None

            def link(self, ins):
                ins.then_inc(self.sem, 1)
                self.count += 1
                if self.turn is None:
                    self.eng.wait_ge(self.sem, self.count)
                else:
                    i, first, per = self.turn
                    self.eng.wait_ge(self.sem, i * per + (self.count - first * per))

            @contextmanager
            def loop(self, first, last, per):
                base = self.count
                with self.eng.Fori(first, last) as i:
                    self.turn = (i, first, per)
                    yield i
                    assert self.count == base + per, (self.count - base, per)
                self.turn = None
                self.count = base + (last - first) * per

        vchain, pchain = Chain(nc.vector, "vector"), Chain(nc.gpsimd, "gpsimd")
        vlink, plink = vchain.link, pchain.link

        def bc(ap, n):
            return ap.unsqueeze(2).to_broadcast([ap.shape[0], ap.shape[1], n])

        def bcm(ap, n):
            return ap.unsqueeze(1).to_broadcast([ap.shape[0], n, ap.shape[1]])

        s = {n: sem(n) for n in """x_in consts w_small xt_ps xt_done""".split()}
        w_loaded = {}

        def wdma(eng, key, dst, src):
            if key not in w_loaded:
                w_loaded[key] = [sem("w_" + key), 0]
            w_loaded[key][1] += 16
            with nc.allow_non_contiguous_dma(reason="small weights"):
                eng.dma_start(dst, src).then_inc(w_loaded[key][0], 16)

        def wwait(eng, key):
            eng.wait_ge(w_loaded[key][0], w_loaded[key][1])


        def load_sync(sp):
            sp.dma_start(XIN[:, :, :], a["x"].rearrange("(q r) c h w -> (r c) q (h w)", r=2)).then_inc(s["x_in"], 16)
            wdma(sp, "cu", w_cu_raw[:, :], a["L0_conv_conv_up_w"].rearrange("k c h w -> k (c h w)"))
            wdma(sp, "b_cu", b_cu[0:K0, :], a["L0_conv_conv_up_b"].unsqueeze(1))
            wdma(sp, "cent", cent_raw[:, :], a["L0_conv_centroids"])
            wdma(sp, "t1", t1_raw[:, :], a["L0_conv_t1_w"].rearrange("o c h w -> o (c h w)"))
            wdma(sp, "t2", t2_raw[:, :], a["L0_conv_t2_w"].rearrange("o c h w -> o (c h w)"))
            wdma(sp, "fc", fc_raw[:, :], a["L0_conv_upfc_w"])
            wdma(sp, "b_fc", b_fc[:, :], a["L0_conv_upfc_b"].unsqueeze(1))
            for h in range(2):
                wdma(sp, "b_t1", b_t1[h * C:(h + 1) * C, :], a["L0_conv_t1_b"].unsqueeze(1))
            wdma(sp, "b_t2", b_t2[:, :], a["L0_conv_t2_b"].unsqueeze(0).to_broadcast([P, C]))

        def consts_pool(pool):
            plink(pool.memset(ident[:, :], 0.0))
            pool.affine_select(out=ident[:, :], in_=ident[:, :], compare_op=ALU.not_equal, fill=1.0, base=0,
                               pattern=[[-1, P]], channel_multiplier=1).then_inc(s["consts"], 1)
            pool.memset(ones[:, :], 1.0).then_inc(s["consts"], 1)
            pool.memset(neghalf[:, :], -0.5).then_inc(s["consts"], 1)
            plink(pool.memset(eps_c[:, :], 1e-6))
            for i in range(2):
                pool.memset(XN[i][:, :, C:P], 1.0).then_inc(s["consts"], 1)
                pool.memset(XP[i][:, :, :].bitcast(F32), 0.0).then_inc(s["consts"], 1)
        NCONST = 8

        s_wt = sem("w_transposed")
        s_wc = sem("w_copied")

        def w0_tensor(pe):
            pe.wait_ge(s["consts"], NCONST)
            wwait(pe, "cu")
            wv = w_cu_raw[:, :].rearrange("k (c t) -> k t c", t=9)
            for t in range(9):
                last = pe.matmul(ps[0:C, 0, t * K0:(t + 1) * K0], wv[:, t, :], ident[0:K0, 0:K0], is_transpose=True)
            last.then_inc(s_wt, 1)
            wwait(pe, "t1"); wwait(pe, "t2"); wwait(pe, "cent"); wwait(pe, "fc")
            pe.transpose(ps[0:C, 1, 0:C], t1_raw[:, 0:C], ident[0:C, 0:C])
            pe.transpose(ps[0:C, 1, C:2 * C], t1_raw[:, C:2 * C], ident[0:C, 0:C])
            pe.transpose(ps[0:C, 1, 2 * C:3 * C], t2_raw[:, :], ident[0:C, 0:C])
            pe.transpose(ps[0:C, 1, 3 * C:3 * C + K0], cent_raw[:, :], ident[0:K0, 0:K0]).then_inc(s_wt, 1)
            for j in range(K0 // 2):
                last = pe.transpose(ps[:, 2 + j // 8, (j % 8) * C:(j % 8 + 1) * C], fc_raw[:, j * P:(j + 1) * P],
                                    ident[0:C, 0:C])
            last.then_inc(s_wt, 1)

        def w0_vector(dve):
            dve.memset(b_cu[K0:C, :], 0.0).then_inc(s["consts"], 1)
            dve.wait_ge(s_wt, 1)
            src = ps[0:C, 0, 0:9 * K0].rearrange("p (t k) -> p t k", k=K0)
            dve.tensor_copy(w_cu_t[0:C, :, :], src)
            vlink(dve.tensor_copy(w_cu_t[C:P, :, :], src))
            vlink(dve.tensor_copy(w_cu[:, :, 0, :], w_cu_t[:, :, :]))
            dve.tensor_tensor(w_cu[:, :, 1, :], w_cu_t[:, :, :], w_cu[:, :, 0, :].bitcast(F32), ALU.subtract).then_inc(s_wc, 1)
            dve.wait_ge(s_wt, 2)
            for h in range(2):
                dve.tensor_copy(t1a_t[h * C:(h + 1) * C, :], ps[0:C, 1, 0:C])
                dve.tensor_copy(t1b[:, h, :], ps[0:C, 1, C:2 * C])
                dve.tensor_copy(t2_t[h * C:(h + 1) * C, :], ps[0:C, 1, 2 * C:3 * C])
            vlink(dve.tensor_copy(centT[:, :], ps[0:C, 1, 3 * C:3 * C + K0]))
            for h in range(2):
                dve.tensor_copy(t1a[:, 0, h, :], t1a_t[:, :])
            vlink(dve.tensor_copy(t2[:, 0, :], t2_t[:, :]))
            for h in range(2):
                dve.tensor_tensor(t1a[:, 1, h, :], t1a_t[:, :], t1a[:, 0, h, :].bitcast(F32), ALU.subtract)
            dve.tensor_tensor(t2[:, 1, :], t2_t[:, :], t2[:, 0, :].bitcast(F32), ALU.subtract).then_inc(s_wc, 1)
            dve.wait_ge(s_wt, 3)
            dve.tensor_copy(fcT[:, :, :].rearrange("p j c -> p (j c)"), ps[:, 2:4, :].rearrange("p a b -> p (a b)")).then_inc(s_wc, 1)

        def xt_tensor(pe):
            pe.wait_ge(s["x_in"], 16)
            for q in range(B // 2):
                for half in range(2):
                    i = q * 2 + half
                    bank = 4 + (i // 4) % 4
                    last = pe.transpose(ps[:, bank, (i % 4) * P:(i % 4 + 1) * P],
                                        XIN[:, q, half * P:(half + 1) * P], ident[:, :])
                    if i % 4 == 3:
                        last.then_inc(s["xt_ps"], 1)

        def xt_scalar(act):
            for g in range(G):
                act.wait_ge(s["xt_ps"], g + 1)
                act.activation(X[:, g * TG:(g + 1) * TG, :].rearrange("p t c -> p (t c)"), ps[:, 4 + g, :],
                               ACT.Copy).then_inc(s["xt_done"], 1)

        def ln_stats(dve, g, src, ready):
            t0, t1_ = g * TG, (g + 1) * TG
            for t in range(TG):
                last = dve.bn_stats(ST[:, t0 + t, :], src[:, t, :])
            vlink(last)
            st = ST[:, t0:t1_, :]
            dve.tensor_tensor(S1_[:, t0:t1_], st[:, :, 1], st[:, :, 4], ALU.add)
            dve.tensor_tensor(S2_[:, t0:t1_], st[:, :, 1], st[:, :, 4], ALU.subtract)
            vlink(dve.tensor_tensor(S3_[:, t0:t1_], st[:, :, 2], st[:, :, 5], ALU.add))
            vlink(dve.scalar_tensor_tensor(S4_[:, t0:t1_], S2_[:, t0:t1_], 0.25, S2_[:, t0:t1_], ALU.mult, ALU.mult))
            dve.scalar_tensor_tensor(var[:, t0:t1_], S3_[:, t0:t1_], 1.0 / C, S4_[:, t0:t1_], ALU.mult,
                                     ALU.add).then_inc(ready.sem, 1)

        def ln_stats_of(dve, g, x_sem, var_sem, per=1):
            dve.wait_ge(*x_sem(per * (g + 1)))
            ln_stats(dve, g, X[:, g * TG:(g + 1) * TG, :], var_sem)
            dve.wait_ge(*var_sem(g + 1))

        def ln_rstd(pool, g, eps, ready, done):
            t0, t1_ = g * TG, (g + 1) * TG
            pool.wait_ge(*ready(g + 1))
            pool.tensor_tensor(nmean[:, t0:t1_], S1_[:, t0:t1_], neghalf[:, t0:t1_], ALU.mult)
            plink(pool.tensor_scalar(vpe[:, t0:t1_], var[:, t0:t1_], eps, None, ALU.add))
            plink(pool.tensor_tensor(rstd[:, t0:t1_], vpe[:, t0:t1_], neghalf[:, t0:t1_], ALU.pow))
            pool.tensor_tensor(nmr[:, t0:t1_], nmean[:, t0:t1_], rstd[:, t0:t1_], ALU.mult).then_inc(done.sem, 1)

        def ln_norm(act, g, rstd_sem, u_sem, src=X, dst=None):
            act.wait_ge(*rstd_sem(g + 1))
            for t in range(TG // 2, TG):
                tt = g * TG + t
                last = act.activation(U[:, tt, :] if dst is None else dst[:, t, :], src[:, tt, :], ACT.Identity,
                                      bias=nmr[:, tt:tt + 1], scale=rstd[:, tt:tt + 1])
            last.then_inc(u_sem.sem, 1)

        STEPS = 6

        def chunk_stats(dve, i, src, ready, step):
            sl = bass.ts(i, 4)
            st = ST[:, sl, :]
            if step < 4:
                last = dve.bn_stats(ST[:, bass.ds(i * 4 + step, 1), :], src[:, bass.ds(i * 4 + step, 1), :])
                if step == 3:
                    vlink(last)
            elif step == 4:
                dve.tensor_tensor(S1_[:, sl], st[:, :, 1], st[:, :, 4], ALU.add)
                dve.tensor_tensor(S2_[:, sl], st[:, :, 1], st[:, :, 4], ALU.subtract)
                vlink(dve.tensor_tensor(S3_[:, sl], st[:, :, 2], st[:, :, 5], ALU.add))
            else:
                vlink(dve.scalar_tensor_tensor(S4_[:, sl], S2_[:, sl], 0.25, S2_[:, sl], ALU.mult, ALU.mult))
                dve.scalar_tensor_tensor(var[:, sl], S3_[:, sl], 1.0 / C, S4_[:, sl], ALU.mult, ALU.add).then_inc(ready.sem, 1)

        def chunk_rstd(pool, eps, ready, done):
            with pchain.loop(0, NCHUNK, 2) as i:
                sl = bass.ts(i, 4)
                pool.wait_ge(*ready(i + 1))
                pool.tensor_tensor(nmean[:, sl], S1_[:, sl], neghalf[:, 0:4], ALU.mult)
                plink(pool.tensor_tensor(vpe[:, sl], var[:, sl], eps[:, :], ALU.add))
                plink(pool.tensor_tensor(rstd[:, sl], vpe[:, sl], neghalf[:, 0:4], ALU.pow))
                pool.tensor_tensor(nmr[:, sl], nmean[:, sl], rstd[:, sl], ALU.mult).then_inc(done.sem, 1)

        def chunk_norm(act, i, rstd_sem, u_sem, src=X, dst=U):
            act.wait_ge(*rstd_sem(i + 1))
            for t in range(4):
                one = bass.ds(i * 4 + t, 1)
                last = act.activation(dst[:, one, :], src[:, one, :], ACT.Identity, bias=nmr[:, one], scale=rstd[:, one])
            last.then_inc(u_sem.sem, 1)

        def chunk_splits(dve, u_sem, fs_sem, ps_sem, groups):
            for g in groups:
                dve.wait_ge(*u_sem(2 * g + 2))
                if g >= 2:
                    dve.wait_ge(*ps_sem(2 * (g - 1)))
                split(dve, US[g % 2], U[:, g * TG:(g + 1) * TG, :], fs_sem)

        def ln_norm_vector(dve, g, rstd_sem, u_sem, src=X, dst=None):
            dve.wait_ge(*rstd_sem(g + 1))
            for t in range(TG // 2):
                tt = g * TG + t
                last = dve.tensor_scalar(U[:, tt, :] if dst is None else dst[:, t, :], src[:, tt, :], rstd[:, tt:tt + 1],
                                         nmr[:, tt:tt + 1], ALU.mult, ALU.add)
            vlink(last)
            dve.wait_ge(*u_sem(g + 1))

        def ln_center(dve, g, src, dst):
            return dve.scalar_tensor_tensor(dst, bc(S1_[:, g * TG:(g + 1) * TG], C), -0.5, src, ALU.mult, ALU.add)

        def split(dve, us, u, ready):
            vlink(dve.tensor_copy(us[:, :, 0, :], u))
            dve.tensor_tensor(us[:, :, 1, :], u, us[:, :, 0, :].bitcast(F32), ALU.subtract).then_inc(ready.sem, 1)

        def transpose_tiles(pe, us, banks, done):
            for t in range(TG):
                last = pe.transpose(ps[:, banks[t // 4], (t % 4) * P:(t % 4 + 1) * P],
                                    us[:, t, :, :].rearrange("p h c -> p (h c)").bitcast(F32), ident[:, :])
                if t % 4 == 3:
                    last.then_inc(done.sem, 1)

        def to_padded(act, bank, xp, qi, done, extra_wait=None):
            v = ps[:, bank, :].rearrange("p (h r y x) -> p h r y x", h=2, r=2, x=W)
            for half in range(2):
                dst = xp[:, 2 * qi:2 * qi + 2, :].rearrange("p r (y x) -> p r y x", x=PADW)
                last = act.activation(dst[:, :, 1 + half * 8:9 + half * 8, 1:1 + W], v[:, half, :, :, :], ACT.Copy)
            last.then_inc(done.sem, 1)

        sig1 = signals((G, "c0_var c0_rstd c0_rstd2 c0_fs c0_xs c0_lt c0_sub c0_le c0_sa c0_up"),
                       (NCHUNK, "c0_ft_ps c0_ft c0_xt_ps c0_xp c0_cv_ps c0_cv"),
                       (1, "u_sq u_n2 u_sqrt u_tot u_tsq u_upn u_fc u_upv u_v u_vd"),
                       (NCHUNK, "t_h_ps t_h t_hs t_o_ps"), (G, "t_o x1"))
        m = dict(sig1)

        def c0_pool(pool):
            for g in range(G):
                sl = slice(g * TG, (g + 1) * TG)
                ln_rstd(pool, g, 1e-6, m["c0_var"], m["c0_rstd"])
                pool.wait_ge(*m["c0_rstd"](g + 1))
                plink(pool.tensor_tensor(n2[:, sl], rstd[:, sl], rstd[:, sl], ALU.mult))
                plink(pool.tensor_tensor(n2b[:, sl], n2[:, sl], var[:, sl], ALU.mult))
                plink(pool.tensor_scalar(n2c[:, sl], n2b[:, sl], float(C), 1e-24, ALU.mult, ALU.max))
                pool.tensor_tensor(rn[:, sl], n2c[:, sl], neghalf[:, sl], ALU.pow).then_inc(m["c0_rstd2"].sem, 1)

        def c0_vector(dve):
            dve.wait_ge(s["consts"], NCONST)

            def stats(g):
                dve.wait_ge(s["xt_done"], g + 1)
                src = X[:, g * TG:(g + 1) * TG, :]
                ln_stats(dve, g, src, m["c0_var"])

            def norm(g):
                sl = slice(g * TG, (g + 1) * TG)
                src = X[:, sl, :]
                xc, us, xs, xn = XC[g % 2], US[g % 2], XS[g % 2], XN[g % 2]
                vlink(ln_center(dve, g, src, xc[:, :, :]))
                dve.wait_ge(*m["c0_rstd"](g + 1))
                vlink(dve.tensor_tensor(U[:, sl, :], xc[:, :, :], bc(rstd[:, sl], C), ALU.mult))
                if g >= 2:
                    dve.wait_ge(*m["c0_ft_ps"](2 * (g - 1)))
                split(dve, us, U[:, sl, :], m["c0_fs"])
                dve.wait_ge(*m["c0_rstd2"](g + 1))
                if g >= 2:
                    dve.wait_ge(*m["c0_up"](g - 1))
                    dve.wait_ge(*m["c0_xt_ps"](2 * (g - 1)))
                vlink(dve.tensor_tensor(xn[:, :, 0:C], U[:, sl, :], bc(rn[:, sl], C), ALU.mult))
                split(dve, xs, xn[:, :, 0:C], m["c0_xs"])

            def soft(g):
                sa = SA[g % 2]
                dve.wait_ge(*m["c0_lt"](g + 1))
                bank = ps[:, 6, :].rearrange("p (t h k) -> p t k h", t=TG, h=2)
                vlink(dve.tensor_reduce(L[:, :, :], bank, X_AXIS, ALU.add))
                vlink(dve.tensor_reduce(R8[0][:, :], L[:, :, :], X_AXIS, ALU.max))
                dve.tensor_tensor(L2[:, :, :], L[:, :, :], bc(R8[0][:, :], K0), ALU.subtract).then_inc(m["c0_sub"].sem, 1)
                dve.wait_ge(*m["c0_le"](g + 1))
                vlink(dve.tensor_reduce(R8[1][:, :], LE[:, :, :], X_AXIS, ALU.add))
                vlink(dve.reciprocal(R8[2][:, :], R8[1][:, :]))
                if g >= 2:
                    dve.wait_ge(*m["c0_up"](g - 1))
                dve.tensor_tensor(sa[:, :, :], LE[:, :, :], bc(R8[2][:, :], K0), ALU.mult).then_inc(m["c0_sa"].sem, 1)
            stats(0)
            for g in range(G):
                if g + 1 < G:
                    stats(g + 1)
                norm(g)
                if g >= 1:
                    soft(g - 1)
            soft(G - 1)

        def c0_scalar(act):
            act.wait_ge(s["consts"], NCONST)
            wwait(act, "b_cu")

            def move(g):
                for j in range(2):
                    act.wait_ge(*m["c0_ft_ps"](2 * g + j + 1))
                    act.activation(UT[:, (2 * g + j) * 512:(2 * g + j + 1) * 512], ps[:, j, :], ACT.Copy).then_inc(m["c0_ft"].sem, 1)
                if g >= 2:
                    act.wait_ge(*m["c0_cv_ps"](2 * (g - 1)))
                for j in range(2):
                    act.wait_ge(*m["c0_xt_ps"](2 * g + j + 1))
                    to_padded(act, 2 + j, XP[g % 2], j, m["c0_xp"])

            def conv_out(g):
                for j in range(2):
                    act.wait_ge(*m["c0_cv_ps"](2 * g + j + 1))
                    if g >= 1:
                        act.wait_ge(*m["c0_lt"](g))
                    act.activation(CV[j][:, :], ps[0:C, 4 + j, :], ACT.Identity, bias=b_cu[:, :]).then_inc(m["c0_cv"].sem, 1)

            def expo(g):
                act.wait_ge(*m["c0_sub"](g + 1))
                if g >= 1:
                    act.wait_ge(*m["c0_sa"](g))
                act.activation(LE[:, :, :], L2[:, :, :], ACT.Exp).then_inc(m["c0_le"].sem, 1)
            for g in range(G + 1):
                if g < G:
                    move(g)
                    conv_out(g)
                if g >= 1:
                    expo(g - 1)

        def c0_tensor(pe):
            def first(g):
                pe.wait_ge(*m["c0_fs"](g + 1))
                if g == 0:
                    pe.wait_ge(s_wc, 3)
                if g >= 1:
                    pe.wait_ge(*m["c0_ft"](2 * g))
                transpose_tiles(pe, US[g % 2], (0, 1), m["c0_ft_ps"])
                pe.wait_ge(*m["c0_xs"](g + 1))
                if g >= 1:
                    pe.wait_ge(*m["c0_xp"](2 * g))
                transpose_tiles(pe, XS[g % 2], (2, 3), m["c0_xt_ps"])

            def conv(g):
                xp = XP[g % 2][:, :, :].rearrange("p b (y x) -> p b y x", x=PADW)
                for j in range(2):
                    pe.wait_ge(*m["c0_xp"](2 * g + j + 1))
                    if g == 0:
                        pe.wait_ge(s["xt_done"], G)
                    else:
                        pe.wait_ge(*m["c0_cv"](2 * (g - 1) + j + 1))
                    for t in range(9):
                        dy, dx = t // 3, t % 3
                        last = pe.matmul(ps[0:C, 4 + j, :], w_cu[:, t, :, :].rearrange("p h k -> p (h k)"),
                                         xp[:, 2 * j:2 * j + 2, dy:dy + H, dx:dx + W], start=(t == 0), stop=(t == 8))
                    last.then_inc(m["c0_cv_ps"].sem, 1)

            def logits_t(g):
                if g >= 1:
                    pe.wait_ge(*m["c0_sub"](g))
                for j in range(2):
                    pe.wait_ge(*m["c0_cv"](2 * g + j + 1))
                    for t in range(4):
                        half, r = t // 2, t % 2
                        c0 = r * PIX + half * P
                        last = pe.transpose(ps[:, 6, (4 * j + t) * C:(4 * j + t + 1) * C], CV[j][:, c0:c0 + P],
                                            ident[0:C, 0:C])
                last.then_inc(m["c0_lt"].sem, 1)

            def pool_up(g):
                pe.wait_ge(*m["c0_sa"](g + 1))
                for j in range(2):
                    for r in range(2):
                        b = 4 * g + 2 * j + r
                        for half in range(2):
                            t = 4 * j + 2 * half + r
                            last = pe.matmul(ps[:, 7, b * K0:(b + 1) * K0], XN[g % 2][:, t, :], SA[g % 2][:, t, :],
                                             start=(half == 0), stop=(half == 1))
                last.then_inc(m["c0_up"].sem, 1)
            for g in range(G + 1):
                if g < G:
                    first(g)
                    conv(g)
                    logits_t(g)
                if g >= 1:
                    pool_up(g - 1)



        def u_vector(dve):
            e0, e1, e2, e3 = [x[:, :, :] for x in EC]
            dve.wait_ge(*m["c0_up"](G))
            dve.wait_ge(s_wc, 3)
            bank = ps[:, 7, :].rearrange("p (b k) -> p b k", k=K0)
            vlink(dve.tensor_tensor(e0, bank[C:P], bcm(centT[:, :], B), ALU.mult))
            vlink(dve.tensor_tensor(e1, bank[0:C], e0, ALU.subtract))
            dve.tensor_tensor(e2, e1, e1, ALU.mult).then_inc(m["u_sq"].sem, 1)
            dve.wait_ge(*m["u_sqrt"](1))
            vlink(dve.tensor_scalar(e0, e0, 1e-12, None, ALU.max))
            vlink(dve.reciprocal(e3, e0))
            vlink(dve.tensor_tensor(e1, e1, e3, ALU.mult))
            n2p = ps[0:C, 6, :].rearrange("p (b k) -> p b k", k=K0)
            vlink(dve.tensor_tensor(e2, e3, n2p, ALU.mult))
            vlink(dve.tensor_tensor(e2, e2, e3, ALU.mult))
            dve.tensor_reduce(tb[0][:, :], e2, X_AXIS, ALU.add).then_inc(m["u_tot"].sem, 1)
            ev = e1.rearrange("p b (k two) -> p two k b", two=2)
            dve.tensor_copy(upn2[0:C, :, :], ev[:, 0, :, :])
            dve.tensor_copy(upn2[C:P, :, :], ev[:, 1, :, :]).then_inc(m["u_upn"].sem, 1)
            dve.wait_ge(*m["u_tsq"](1))
            vlink(dve.tensor_scalar(tb[1][:, :], tb[1][:, :], 1e-12, None, ALU.max))
            vlink(dve.reciprocal(tb[2][:, :], tb[1][:, :]))
            dve.wait_ge(*m["u_fc"](1))
            wwait(dve, "b_fc")
            vlink(dve.tensor_tensor(tb[3][:, :], ps[0:C, 0, 0:B], tb[2][:, :], ALU.mult))
            dve.tensor_scalar(upv[:, :], tb[3][:, :], b_fc[:, :], None, ALU.add).then_inc(m["u_upv"].sem, 1)
            dve.wait_ge(*m["u_v"](1))
            wwait(dve, "b_t1")
            dve.tensor_scalar(V[:, :], ps[:, 1, 0:B], b_t1[:, :], None, ALU.add).then_inc(m["u_vd"].sem, 1)

        def u_scalar(act):
            act.wait_ge(*m["u_n2"](1))
            act.activation(EC[0][:, :, :].rearrange("p b k -> p (b k)"), ps[0:C, 6, :], ACT.Sqrt).then_inc(m["u_sqrt"].sem, 1)
            act.wait_ge(*m["u_tot"](1))
            act.activation(tb[1][:, :], tb[0][:, :], ACT.Sqrt).then_inc(m["u_tsq"].sem, 1)

        def u_tensor(pe):
            pe.wait_ge(*m["u_sq"](1))
            pe.matmul(ps[0:C, 6, :], ones[0:C, 0:C], EC[2][:, :, :].rearrange("p b k -> p (b k)"), start=True,
                      stop=True).then_inc(m["u_n2"].sem, 1)
            pe.wait_ge(*m["u_upn"](1))
            pe.wait_ge(*m["c0_ft"](2 * G))
            for j in range(K0 // 2):
                last = pe.matmul(ps[0:C, 0, 0:B], fcT[:, j, :], upn2[:, j, :], start=(j == 0), stop=(j == K0 // 2 - 1))
            last.then_inc(m["u_fc"].sem, 1)
            pe.wait_ge(*m["u_upv"](1))
            pe.matmul(ps[:, 1, 0:B], t1b[:, :, :].rearrange("p h c -> p (h c)"), upv[:, :], start=True,
                      stop=True).then_inc(m["u_v"].sem, 1)



        def t_tensor(pe):
            def hidden(j):
                if j >= 2:
                    pe.wait_ge(*m["t_h"](j - 1))
                else:
                    pe.wait_ge(*m["c0_xp"](2 * G))
                for part in range(2):
                    last = pe.matmul(ps[:, 2 + j % 2, :], t1a[:, part, :, :].rearrange("p h c -> p (h c)"),
                                     UT[:, j * CHUNK:(j + 1) * CHUNK], start=(part == 0), stop=(part == 1))
                last.then_inc(m["t_h_ps"].sem, 1)

            def outp(j):
                g = j // 2
                pe.wait_ge(*m["t_hs"](j + 1))
                if j % 2 == 0:
                    if g >= 2:
                        pe.wait_ge(*m["t_o"](g - 1))
                    else:
                        pe.wait_ge(*m["c0_cv"](2 * G))
                for t in range(4):
                    o = (j % 2) * 4 + t
                    for part in range(2):
                        last = pe.matmul(ps[:, 4 + g % 2, o * C:(o + 1) * C], HS[j % 2][:, t * P:(t + 1) * P],
                                         t2[:, part, :], start=(part == 0), stop=(part == 1))
                last.then_inc(m["t_o_ps"].sem, 1)
            hidden(0)
            for j in range(NCHUNK):
                if j + 1 < NCHUNK:
                    hidden(j + 1)
                outp(j)

        def t_scalar(act):
            act.wait_ge(*m["u_vd"](1))
            for j in range(NCHUNK):
                act.wait_ge(*m["t_h_ps"](j + 1))
                if j >= 2:
                    act.wait_ge(*m["t_hs"](j - 1))
                for r in range(2):
                    b = 2 * j + r
                    src = ps[:, 2 + j % 2, :].rearrange("p (h r s) -> p h r s", h=2, r=2)[:, :, r, :]
                    dst = HR[j % 2][:, :].rearrange("p (h r s) -> p h r s", h=2, r=2)[:, :, r, :]
                    last = act.activation(dst, src, ACT.Relu, bias=V[:, b:b + 1])
                last.then_inc(m["t_h"].sem, 1)

        def t_vector(dve):
            wwait(dve, "b_t2")

            def hs(j):
                dve.wait_ge(*m["t_h"](j + 1))
                if j >= 2:
                    dve.wait_ge(*m["t_o_ps"](j - 1))
                vlink(dve.tensor_copy(HS[j % 2][:, :], HR[j % 2][:, :]))
                dve.tensor_tensor(HS[j % 2][C:P, :], HR[j % 2][C:P, :], HS[j % 2][C:P, :].bitcast(F32),
                                  ALU.subtract).then_inc(m["t_hs"].sem, 1)

            def fin(g):
                sl = slice(g * TG, (g + 1) * TG)
                dve.wait_ge(*m["t_o_ps"](2 * g + 2))
                if g >= 2:
                    dve.wait_ge(*m["x1"](g - 1))
                dve.tensor_tensor(OT[g % 2][:, :, :], ps[:, 4 + g % 2, :].rearrange("p (t c) -> p t c", c=C),
                                  bcm(b_t2[:, :], TG), ALU.add).then_inc(m["t_o"].sem, 1)
                dve.wait_ge(*m["t_o"](g + 1))
                dve.scalar_tensor_tensor(X[:, sl, :], OT[g % 2][:, :, :], 0.0, X[:, sl, :], ALU.max,
                                         ALU.add).then_inc(m["x1"].sem, 1)
            for j in range(NCHUNK):
                hs(j)
                if j % 2 == 0 and j >= 2:
                    fin(j // 2 - 1)
                if j % 2 == 1 and j >= 3:
                    ln_stats_of(dve, j // 2 - 1, m["x1"], m["f_var"])
            fin(G - 1)
            ln_stats_of(dve, G - 1, m["x1"], m["f_var"])
        sig2 = signals((G, "f_var f_rstd f_fs f_xu f_wl f_u f_yb x2"), (NCHUNK, "f_ft_ps f_ft f_y_ps f_y f_yt_ps"),
                       (1, "f_tk_ps f_mask f_mt_ps f_wm"), (2 * NCHUNK, "f_h_ps f_h"))
        m.update(sig2)

        def f_sync(sp):
            wdma(sp, "wr0", wr0[:, :], a["L0_ffn_wr"].rearrange("d o -> o d").to_broadcast([P, C]))
            wdma(sp, "wr0", br0[:, :], a["L0_ffn_br"].unsqueeze(0).to_broadcast([P, 1]))
            for h in range(2):
                wdma(sp, "f1", f1_raw[h * C:(h + 1) * C, :], a["L0_ffn_w1"])
            wdma(sp, "f2", b_f1[:, :], a["L0_ffn_b1"].rearrange("(h p) -> p h", p=P))
            wdma(sp, "f2", f2[:, :, :], a["L0_ffn_w2"].rearrange("(h p) o -> p h o", p=P))
            wdma(sp, "b_f2", b_f2[:, :], a["L0_ffn_b2"].unsqueeze(0).to_broadcast([P, C]))

        def ln_pool(pool, eps, var_sem, rstd_sem):
            for g in range(G):
                ln_rstd(pool, g, eps, var_sem, rstd_sem)

        def ln_vector(dve, rstd_sem, u_sem, fs_sem, ps_sem, do_split=True, extra=None):
            for g in range(G):
                sl = slice(g * TG, (g + 1) * TG)
                ln_norm_vector(dve, g, rstd_sem, u_sem)
                if do_split:
                    if g >= 2:
                        dve.wait_ge(*ps_sem(2 * (g - 1)))
                    split(dve, US[g % 2], U[:, sl, :], fs_sem)
                if extra:
                    extra(g, sl)

        def ln_tensor(pe, fs_sem, ps_sem, ft_sem, first_wait=(), then=None):
            for g in range(G):
                pe.wait_ge(*fs_sem(g + 1))
                if g >= 1:
                    pe.wait_ge(*ft_sem(2 * g))
                else:
                    for sem_, v in first_wait:
                        pe.wait_ge(*sem_(v))
                transpose_tiles(pe, US[g % 2], (0, 1), ps_sem)
                if g >= 1 and then:
                    then(g - 1)
            if then:
                pe.wait_ge(*ft_sem(2 * G))
                then(G - 1)

        def ln_scalar(act, rstd_sem, u_sem, ps_sem, ft_sem, first_wait=(), sums=None):
            ln_norm(act, 0, rstd_sem, u_sem)
            for g in range(G):
                if g + 1 < G:
                    ln_norm(act, g + 1, rstd_sem, u_sem)
                if g == 0:
                    for sem_, v in first_wait:
                        act.wait_ge(*sem_(v))
                for j in (2 * g, 2 * g + 1):
                    act.wait_ge(*ps_sem(j + 1))
                    if sums is None:
                        act.activation(UT[:, j * CHUNK:(j + 1) * CHUNK], ps[:, j % 2, :], ACT.Copy).then_inc(ft_sem.sem, 1)
                        continue
                    for r in range(2):
                        src, dst = [x.rearrange("p (h r s) -> p r h s", h=2, r=2)[:, r, :, :]
                                    for x in (ps[:, j % 2, :], UT[:, j * CHUNK:(j + 1) * CHUNK])]
                        last = act.activation(dst, src, ACT.Copy, accum_out=sums[:, 2 * j + r:2 * j + r + 1])
                    last.then_inc(ft_sem.sem, 1)

        def f_pool(pool):
            ln_pool(pool, 1e-5, m["f_var"], m["f_rstd"])
            for g in range(G):
                sl = slice(g * TG, (g + 1) * TG)
                pool.wait_ge(*m["f_fs"](g + 1))
                pool.tensor_tensor(X[:, sl, :], X[:, sl, :], U[:, sl, :], ALU.add).then_inc(m["f_u"].sem, 1)

        wl_q = wl[:, :, :].rearrange("p h (q r) -> p q h r", r=2)

        YB = (6, 0, 1, 6)

        def f_vector(dve):
            wwait(dve, "wr0")

            def extra(g, sl):
                vlink(dve.tensor_tensor(XC[g % 2][:, :, :], U[:, sl, :], bcm(wr0[:, :], TG), ALU.mult))
                vlink(dve.tensor_reduce(R8[0][:, :], XC[g % 2][:, :, :], X_AXIS, ALU.add))
                dve.tensor_scalar(wl_q[:, QG * g:QG * (g + 1), :, :], R8[0][:, :].rearrange("p (q h r) -> p q h r", h=2, r=2),
                                  br0[:, :], None, ALU.add).then_inc(m["f_wl"].sem, 1)
                dve.wait_ge(*m["f_wl"](g + 1))
            ln_vector(dve, m["f_rstd"], m["f_xu"], m["f_fs"], m["f_ft_ps"], extra=extra)
            dve.memset(tk[:, PIX:PIX + 1], 3.0e38)
            dve.wait_ge(*m["f_tk_ps"](1))
            vlink(dve.tensor_copy(tk[:, 0:PIX], ps[0:B, 7, 0:PIX]))
            for i in range((TOPK0 + 1) // 8):
                vlink(dve.max(m8[:, :], tk[:, :]))
                vlink(dve.match_replace(tk[:, :], m8[:, :], tk[:, :], -3.0e38))
            dve.tensor_scalar(tk[:, 0:PIX], tk[:, 0:PIX], -2.9e38, None, ALU.is_le).then_inc(m["f_mask"].sem, 1)
            dve.wait_ge(*m["f_mt_ps"](1))
            dve.tensor_tensor(wm[:, :].rearrange("p (q h r) -> p q h r", h=2, r=2),
                              ps[:, 7, 0:2 * B].rearrange("p (h q r) -> p q h r", h=2, r=2), wl_q, ALU.mult).then_inc(m["f_wm"].sem, 1)
            dve.wait_ge(*m["f_wm"](1))
            wwait(dve, "b_f2")
            for g in range(G):
                sl = slice(g * TG, (g + 1) * TG)
                dve.wait_ge(*m["f_yt_ps"](2 * g + 2))
                dve.wait_ge(*m["f_u"](g + 1))
                dve.tensor_tensor(Y[:, sl, :], ps[:, YB[g], :].rearrange("p (t c) -> p t c", c=C), bcm(b_f2[:, :], TG),
                                  ALU.add).then_inc(m["f_yb"].sem, 1)
                dve.wait_ge(*m["f_yb"](g + 1))
                vlink(dve.tensor_tensor(Y[:, sl, :], Y[:, sl, :], bc(wm[:, sl], C), ALU.mult))
                dve.tensor_tensor(X[:, sl, :], X[:, sl, :], Y[:, sl, :], ALU.add).then_inc(m["x2"].sem, 1)
                ln_stats_of(dve, g, m["x2"], m["v_var"])
        x_ready1 = m["x1"]

        def f_weights(dve):
            wwait(dve, "f1")
            vlink(dve.tensor_copy(f1[:, 0, :], f1_raw[:, :]))
            dve.tensor_tensor(f1[:, 1, :], f1_raw[:, :], f1[:, 0, :].bitcast(F32), ALU.subtract).then_inc(s_f1, 1)
        s_f1 = sem("f1_split")

        def f_scalar(act):
            ln_scalar(act, m["f_rstd"], m["f_xu"], m["f_ft_ps"], m["f_ft"], [(m["t_h_ps"], NCHUNK)])
            wwait(act, "f2")

            def gelu(j):
                for hc in range(2):
                    act.wait_ge(*m["f_h_ps"](2 * j + hc + 1))
                    if j >= 2:
                        act.wait_ge(*m["f_y_ps"](j - 1))
                    act.activation(HG[j % 2][:, hc, :], ps[:, 2 + hc, :], ACT.Gelu_apprx_tanh,
                                   bias=b_f1[:, hc:hc + 1]).then_inc(m["f_h"].sem, 1)

            def move(j):
                act.wait_ge(*m["f_y_ps"](j + 1))
                if j >= 2:
                    act.wait_ge(*m["f_yt_ps"](j - 1))
                act.activation(YT[j % 2][:, :], ps[0:C, 4 + j % 2, :], ACT.Copy).then_inc(m["f_y"].sem, 1)
            for j in range(NCHUNK + 1):
                if j < NCHUNK:
                    gelu(j)
                if j >= 1:
                    move(j - 1)

        def f_tensor(pe):
            ln_tensor(pe, m["f_fs"], m["f_ft_ps"], m["f_ft"], [(m["u_vd"], 1)])
            pe.wait_ge(*m["f_wl"](G))
            for half in range(2):
                last = pe.transpose(ps[0:B, 7, half * P:(half + 1) * P], wl[:, half, :], ident[:, :])
            last.then_inc(m["f_tk_ps"].sem, 1)
            wwait(pe, "f2")
            pe.wait_ge(s_f1, 1)
            pe.wait_ge(*m["t_h"](NCHUNK))
            pe.wait_ge(*m["t_o"](G))

            def hidden(j):
                pe.wait_ge(*m["f_ft"](j + 1))
                for hc in range(2):
                    if j >= 1:
                        pe.wait_ge(*m["f_h"](2 * (j - 1) + hc + 1))
                    for part in range(2):
                        last = pe.matmul(ps[:, 2 + hc, :], f1[:, part, hc * P:(hc + 1) * P],
                                         UT[:, j * CHUNK:(j + 1) * CHUNK], start=(part == 0), stop=(part == 1))
                    last.then_inc(m["f_h_ps"].sem, 1)

            def outp(j):
                pe.wait_ge(*m["f_h"](2 * j + 2))
                if j >= 2:
                    pe.wait_ge(*m["f_y"](j - 1))
                for hc in range(2):
                    last = pe.matmul(ps[0:C, 4 + j % 2, :], f2[:, hc, :], HG[j % 2][:, hc, :], start=(hc == 0), stop=(hc == 1))
                last.then_inc(m["f_y_ps"].sem, 1)

            def back(j):
                pe.wait_ge(*m["f_y"](j + 1))
                if j == 6:
                    pe.wait_ge(*m["f_yb"](1))
                for t in range(4):
                    o = (j % 2) * 4 + t
                    last = pe.transpose(ps[:, YB[j // 2], o * C:(o + 1) * C], YT[j % 2][:, t * P:(t + 1) * P], ident[0:C, 0:C])
                last.then_inc(m["f_yt_ps"].sem, 1)
            hidden(0)
            for j in range(NCHUNK + 1):
                if j + 1 < NCHUNK:
                    hidden(j + 1)
                if j < NCHUNK:
                    outp(j)
                if j == 5:
                    pe.wait_ge(*m["f_mask"](1))
                    for half in range(2):
                        last = pe.transpose(ps[:, 7, half * B:(half + 1) * B], tk[:, half * P:(half + 1) * P], ident[0:B, 0:B])
                    last.then_inc(m["f_mt_ps"].sem, 1)
                if j >= 1:
                    back(j - 1)

        retire(sig1)
        sig3 = signals((G, "v_var v_rstd v_u v_norm v_sb_ps x3"), (2, "v_bits v_band"),
                       (1, "v_ori_ps v_ori v_lg_ps v_a v_y v_h_ps v_h v_s_ps v_s v_w_ps v_w"))
        m.update(sig3)

        def v_sync(sp):
            wdma(sp, "wenc", wenc[:, :], a["L1_conv_w_enc"].rearrange("o c -> c o"))
            wdma(sp, "wenc", b_enc[:, :], a["L1_conv_b_enc"].unsqueeze(0).to_broadcast([C, 1]))
            wdma(sp, "l1w", l1w1_raw[:, :], a["L1_conv_w1"])
            wdma(sp, "l1w", l1w2_raw[:, :], a["L1_conv_w2"])

        def v_pool(pool):
            pool.iota(pidx[:, :], pattern=[[0, 1]], base=0, channel_multiplier=1).then_inc(m["v_bits"].sem, 1)
            pool.iota(rev[:, :], pattern=[[-1, 16]], base=16, channel_multiplier=0,
                      allow_small_or_imprecise_dtypes=True).then_inc(m["v_bits"].sem, 1)
            ln_pool(pool, 1e-6, m["v_var"], m["v_rstd"])

        def v_consts(dve):
            dve.wait_ge(*m["v_bits"](2))
            dve.tensor_scalar(pbit[0][:, :], pidx[:, :], 1, None, ALU.bitwise_and)
            vlink(dve.tensor_scalar(pbit[1][:, :], pidx[:, :], 4, None, ALU.logical_shift_right))
            vlink(dve.tensor_scalar(pbit[2][:, :], pbit[1][:, :], 1, None, ALU.bitwise_and))
            scale = 0.5 / (PIX // 4)
            dve.memset(band[:, 0:1], scale)
            dve.tensor_scalar(band[:, 1:2], pbit[0][:, :], 2 * scale, -scale, ALU.mult, ALU.add)
            vlink(dve.tensor_scalar(band[:, 2:3], pbit[2][:, :], 2 * scale, -scale, ALU.mult, ALU.add))
            dve.scalar_tensor_tensor(band[:, 3:4], band[:, 1:2], 1.0 / scale, band[:, 2:3], ALU.mult, ALU.mult).then_inc(m["v_band"].sem, 1)
            wwait(dve, "wenc")
            dve.wait_ge(s["consts"], NCONST)
            dve.tensor_scalar(wencb[:, :], ones[0:C, 0:C], wenc[:, :], None, ALU.mult).then_inc(m["v_band"].sem, 1)

        def v_vector(dve):
            dve.wait_ge(*m["v_w_ps"](1))
            dve.tensor_copy(l1w1T[:, :], ps[0:C, 7, 64:96])
            dve.tensor_copy(l1w2T[:, :], ps[0:C // 2, 7, 128:192]).then_inc(m["v_w"].sem, 1)

            ln_vector(dve, m["v_rstd"], m["v_u"], None, None, do_split=False,
                      extra=lambda g, sl: dve.sem_inc(m["v_norm"].sem, 1))
            o = ori[:, :, :]
            dve.wait_ge(*m["v_ori_ps"](1))
            dve.tensor_copy(o.rearrange("p b k -> p (b k)"), ps[0:C, 0, 0:C]).then_inc(m["v_ori"].sem, 1)
            dve.wait_ge(*m["v_a"](1))
            A = ba[0][:, :, :]
            vlink(dve.tensor_reduce(bs[0][:, :], A, X_AXIS, ALU.max))
            vlink(dve.tensor_tensor(ba[1][:, :, :], A, bc(bs[0][:, :], 4), ALU.is_equal))
            vlink(dve.tensor_tensor(ba[2][:, :, :], ba[1][:, :, :], bcm(rev[0:C, 0:4], B), ALU.mult))
            vlink(dve.tensor_reduce(bs[1][:, :], ba[2][:, :, :], X_AXIS, ALU.max))
            vlink(dve.tensor_tensor(ba[1][:, :, :], ba[2][:, :, :], bc(bs[1][:, :], 4), ALU.is_equal))
            dve.wait_ge(*m["v_ori"](1))
            vlink(dve.tensor_tensor(ba[3][:, :, :], ba[1][:, :, :], o, ALU.mult))
            vlink(dve.tensor_reduce(bs[2][:, :], ba[3][:, :, :], X_AXIS, ALU.add))
            vlink(dve.tensor_tensor(ba[1][:, :, :], o, bc(bs[2][:, :], 4), ALU.subtract))
            vlink(dve.tensor_scalar(ba[2][:, :, :], ba[1][:, :, :], 0.0, None, ALU.max))
            dve.tensor_reduce(bs[3][:, :], ba[2][:, :, :], X_AXIS, ALU.add).then_inc(m["v_y"].sem, 1)
            dve.wait_ge(*m["v_h_ps"](1))
            dve.tensor_scalar(hq[:, :], ps[0:C // 2, 2, 0:B], 0.0, None, ALU.max).then_inc(m["v_h"].sem, 1)
            for g in range(G):
                sl = slice(g * TG, (g + 1) * TG)
                dve.wait_ge(*m["v_sb_ps"](g + 1))
                gate = ps[:, 4 + g, 0:BG * C].rearrange("p (q rc) -> p q rc", q=QG)
                gate = gate.unsqueeze(2).to_broadcast([P, QG, 2, P])
                u4 = U[:, sl, :].rearrange("p (q h r) c -> p q h (r c)", h=2, r=2)
                xc = XC[g % 2][:, :, :]
                vlink(dve.tensor_tensor(xc.rearrange("p (q h r) c -> p q h (r c)", h=2, r=2), u4, gate, ALU.mult))
                dve.tensor_tensor(X[:, sl, :], X[:, sl, :], xc, ALU.add).then_inc(m["x3"].sem, 1)
                ln_stats_of(dve, g, m["x3"], e1["var"])

        def v_scalar(act):
            for g in range(G):
                ln_norm(act, g, m["v_rstd"], m["v_u"])
            act.wait_ge(*m["v_lg_ps"](1))
            wwait(act, "wenc")
            act.activation(ba[0][:, :, :].rearrange("p b k -> p (b k)"), ps[0:C, 1, 0:C], ACT.Sigmoid,
                           bias=b_enc[:, :]).then_inc(m["v_a"].sem, 1)
            act.wait_ge(*m["v_s_ps"](1))
            act.activation(sg[:, :], ps[0:C, 3, 0:B], ACT.Sigmoid).then_inc(m["v_s"].sem, 1)

        def v_tensor(pe):
            wwait(pe, "l1w")
            pe.wait_ge(*m["f_wm"](1))
            pe.transpose(ps[0:C, 7, 64:96], l1w1_raw[:, :], ident[0:C // 2, 0:C // 2])
            pe.transpose(ps[0:C // 2, 7, 128:192], l1w2_raw[:, :], ident[0:C, 0:C]).then_inc(m["v_w_ps"].sem, 1)
            pe.wait_ge(*m["v_band"](2))
            for b in range(B):
                q, r = b // 2, b % 2
                if b % BG == 0:
                    pe.wait_ge(*m["v_norm"](b // BG + 1))
                for half in range(2):
                    last = pe.matmul(ps[0:C, 0, 4 * b:4 * b + 4], U[:, 4 * q + 2 * half + r, :], band[:, :],
                                     start=(half == 0), stop=(half == 1))
            last.then_inc(m["v_ori_ps"].sem, 1)
            pe.wait_ge(*m["v_ori"](1))
            pe.matmul(ps[0:C, 1, 0:C], wencb[:, :], ori[:, :, :].rearrange("p b k -> p (b k)"), start=True,
                      stop=True).then_inc(m["v_lg_ps"].sem, 1)
            pe.wait_ge(*m["v_w"](1))
            pe.wait_ge(*m["v_y"](1))
            pe.wait_ge(*m["f_h"](2 * NCHUNK))
            pe.matmul(ps[0:C // 2, 2, 0:B], l1w1T[:, :], bs[3][:, :], start=True, stop=True).then_inc(m["v_h_ps"].sem, 1)
            pe.wait_ge(*m["v_h"](1))
            pe.matmul(ps[0:C, 3, 0:B], l1w2T[:, :], hq[:, :], start=True, stop=True).then_inc(m["v_s_ps"].sem, 1)
            pe.wait_ge(*m["v_s"](1))
            pe.wait_ge(*m["f_y"](NCHUNK))
            for b in range(B):
                last = pe.matmul(ps[:, 4 + b // BG, (b % BG) * C:(b % BG + 1) * C], sg[:, b:b + 1].to_broadcast([C, P]),
                                 ident[0:C, 0:C], start=True, stop=True)
                if b % BG == BG - 1:
                    last.then_inc(m["v_sb_ps"].sem, 1)
        def router_tensor(pe, g, w2, ne, bank, done):
            for t in range(g * TG, (g + 1) * TG):
                at = t * 2 * ne
                last = pe.matmul(ps[:, bank + at // 512, at % 512:at % 512 + 2 * ne], UT[:, t * P:(t + 1) * P],
                                 w2[:, :, :].rearrange("p h e -> p (h e)"), start=True, stop=True)
            last.then_inc(done.sem, 1)

        def router_transpose(pe, mm):
            for g in range(G):
                pe.wait_ge(*mm["ds"](g + 1))
                for t in range(TG):
                    if t % 4 == 0 and g >= 2:
                        pe.wait_ge(*mm["dt"](2 * g + t // 4 - 3))
                    last = pe.transpose(ps[:, 4 + 2 * (g % 2) + t // 4, (t % 4) * P:(t % 4 + 1) * P],
                                        DS[g % 2][:, t, :].bitcast(F32), ident[:, :])
                    if t % 4 == 3:
                        last.then_inc(mm["dt_ps"].sem, 1)

        def router_logits(dve, mm, ne, bias, bank, rescale=None):
            rt = [x[:, :, 0:ne] for x in RT]
            dve.wait_ge(*mm["lg_ps"](G))
            lp = ps[:, bank:, :].rearrange("p b (t h e) -> p (b t) h e", h=2, e=ne)
            vlink(dve.tensor_copy(rt[3], lp[:, :, 0, :]))
            vlink(dve.tensor_tensor(rt[1], rt[3], lp[:, :, 1, :], ALU.add))
            if rescale is not None:
                rescale(dve, rt[1])
            vlink(dve.tensor_tensor(rt[0], rt[1], bcm(bias, NT), ALU.add))
            vlink(dve.tensor_reduce(r8[0][:, :], rt[0], X_AXIS, ALU.max))
            dve.tensor_tensor(rt[1], rt[0], bc(r8[0][:, :], ne), ALU.subtract).then_inc(mm["sub"].sem, 1)

        def router_top2(dve, mm, ne):
            rt = [x[:, :, 0:ne] for x in RT]
            rv = bcm(rev[:, 0:ne], NT)
            dve.wait_ge(*mm["exp"](1))
            vlink(dve.scalar_tensor_tensor(rt[5], rt[2], 1.0, rv, ALU.is_equal, ALU.mult))
            vlink(dve.tensor_reduce(r8[5][:, :], rt[5], X_AXIS, ALU.max))
            vlink(dve.tensor_tensor(rt[4], rt[5], bc(r8[5][:, :], ne), ALU.is_equal))
            vlink(dve.scalar_tensor_tensor(rt[6], rt[4], -2.0, rt[2], ALU.mult, ALU.add))
            vlink(dve.tensor_reduce(r8[4][:, :], rt[6], X_AXIS, ALU.max))
            dve.tensor_scalar(r8[6][:, :], r8[4][:, :], 1.0, None, ALU.add)
            vlink(dve.tensor_tensor(rt[5], rt[6], bc(r8[4][:, :], ne), ALU.is_equal))
            dve.reciprocal(r8[3][:, :], r8[6][:, :])
            vlink(dve.tensor_tensor(rt[3], rt[5], rv, ALU.mult))
            dve.tensor_tensor(r8[7][:, :], r8[4][:, :], r8[3][:, :], ALU.mult)
            vlink(dve.tensor_reduce(r8[5][:, :], rt[3], X_AXIS, ALU.max))
            vlink(dve.tensor_tensor(rt[7], rt[3], bc(r8[5][:, :], ne), ALU.is_equal))
            dve.tensor_tensor(rt[4], rt[4], bc(r8[3][:, :], ne), ALU.mult)
            vlink(dve.tensor_tensor(rt[7], rt[7], bc(r8[7][:, :], ne), ALU.mult))
            vlink(dve.tensor_tensor(rt[5], rt[4], rt[7], ALU.add))
            for g in range(G):
                d = rt[5][:, g * TG:(g + 1) * TG, :]
                if g >= 2:
                    dve.wait_ge(*mm["dt_ps"](2 * (g - 1)))
                vlink(dve.tensor_copy(DS[g % 2][:, :, 0:ne], d))
                dve.tensor_tensor(DS[g % 2][:, :, 32:32 + ne], d, DS[g % 2][:, :, 0:ne].bitcast(F32),
                                  ALU.subtract).then_inc(mm["ds"].sem, 1)

        def router_scalar(act, mm, ne):
            act.wait_ge(*mm["sub"](1))
            act.activation(RT[2][:, :, 0:ne], RT[1][:, :, 0:ne], ACT.Exp).then_inc(mm["exp"].sem, 1)

        def router_move(act, mm):
            for j in range(NCHUNK):
                act.wait_ge(*mm["dt_ps"](j + 1))
                act.activation(DT[:, j * CHUNK:(j + 1) * CHUNK], ps[:, 4 + j % 4, :], ACT.Copy).then_inc(mm["dt"].sem, 1)

        N1 = NCHUNK * E1
        retire(sig2)
        e1 = signals((G, "var rstd fs xu ds"), (G, "lg_ps"), (1, "sub exp"), (NCHUNK, "ft_ps ft dt_ps dt x"), (N1, "act h_ps h2_ps d_ps"),
                     (2 + N1, "m1 hid"), (8 + N1, "o_ps"), (1 + NCHUNK, "oc t_ps ta"))
        prep = signals((1, "filled emptied bias_ps bias att"), (E2, "hi lo"))
        s_w12 = sem("w12_split")
        s_w12h = sem("w12_hi")
        s_gw = sem("gw_split")
        s_sel = sem("sel_ready")

        def e1_sync(sp):
            for h in range(2):
                wdma(sp, "gw", gw[h * C:(h + 1) * C, :], a["L1_ffn_gate_w"])
            wdma(sp, "gw", b_gw[:, :], a["L1_ffn_gate_b"].unsqueeze(0).to_broadcast([P, E1]))
            for h in range(2):
                for k, nm in enumerate(("L1_ffn_w1", "L1_ffn_w2")):
                    wdma(sp, "w12", w12_raw[h * C:(h + 1) * C, k, :, :], a[nm].rearrange("e d h -> d e h"))
            wdma(sp, "w3", w3[:, :, :], a["L1_ffn_w3"].rearrange("e h o -> h e o"))

        def e1_consts(dve):
            dve.wait_ge(s["consts"], NCONST)
            dve.memset(DS[0][:, :, :].bitcast(F32), 0.0)
            dve.memset(DS[1][:, :, :].bitcast(F32), 0.0)
            vlink(dve.tensor_tensor(self32[:, :], ident[:, 0:E1], ident[:, 32:32 + E1], ALU.add))
            dve.tensor_copy(sel[:, :], self32[:, :]).then_inc(s_sel, 1)
            wwait(dve, "gw")
            vlink(dve.tensor_copy(gw2[:, 0, :], gw[:, :]))
            dve.tensor_tensor(gw2[:, 1, :], gw[:, :], gw2[:, 0, :].bitcast(F32), ALU.subtract).then_inc(s_gw, 1)

        def e1_whi(act):
            wwait(act, "w12")
            for k in range(2):
                for i in range(4):
                    act.activation(w12[:, 0, k, 4 * i:4 * i + 4, :], w12_raw[:, k, 4 * i:4 * i + 4, :], ACT.Copy).then_inc(s_w12h, 1)

        def e1_pool(pool):
            for k in range(2):
                for i in range(4):
                    sl = slice(4 * i, 4 * i + 4)
                    pool.wait_ge(s_w12h, 4 * k + i + 1)
                    pool.tensor_tensor(w12[:, 1, k, sl, :], w12_raw[:, k, sl, :], w12[:, 0, k, sl, :].bitcast(F32),
                                       ALU.subtract).then_inc(s_w12, 1)
            ln_pool(pool, 1e-5, e1["var"], e1["rstd"])
            for e in range(E2):
                pool.wait_ge(*prep["hi"](e + 1))
                pool.tensor_tensor(w1_6[:, 1, e, :], w1_whole[:, 1, e, :], w1_6[:, 0, e, :].bitcast(F32),
                                   ALU.subtract).then_inc(prep["lo"].sem, 1)

        def experts_finish(dve, mm, i):
            dve.wait_ge(*mm["t_ps"](i + 2))
            dve.tensor_reduce(OA[:, :, :], ps[:, 7, :].rearrange("p (t h c) -> p t c h", h=2, c=C), X_AXIS,
                              ALU.add).then_inc(mm["ta"].sem, 1)
            dve.wait_ge(*mm["ta"](i + 2))
            xs = X[:, bass.ts(i, 4), :]
            dve.tensor_tensor(xs, xs, OA[:, :, :], ALU.add).then_inc(mm["x"].sem, 1)
            dve.wait_ge(*mm["x"](i + 1))

        AT_WO, AT_GSUM = 3 * INNER, 3 * INNER + C
        AT_B1, AT_LNG = AT_GSUM + E2, AT_GSUM + 3 * E2
        AT_LNB, AT_BIAS = AT_LNG + E2, AT_LNG + 2 * E2

        def prep_tensor(pe, e):
            if e == 1:
                wwait(pe, "datt")
                wwait(pe, "e2s")
                pe.transpose(ps[0:C, 7, 0:INNER], wq_raw[:, :], ident[:, :])
                for k in range(2):
                    pe.transpose(ps[0:C, 7, (1 + k) * INNER:(2 + k) * INNER], wkv_raw[:, k, :], ident[:, :])
                pe.transpose(ps[:, 7, AT_WO:AT_WO + C], wo_raw[:, :], ident[0:C, 0:C])
                pe.matmul(ps[:, 7, AT_GSUM:AT_GSUM + E2], ones[0:C, :], gw_6[0:C, :], start=True, stop=True)
                pe.transpose(ps[:, 7, AT_B1:AT_B1 + 2 * E2], b1_raw[:, :], ident[0:2 * E2, 0:2 * E2])
                pe.transpose(ps[:, 7, AT_LNG:AT_LNG + E2], lng_raw[:, :], ident[0:E2, 0:E2])
                pe.transpose(ps[0:C, 7, AT_LNB:AT_LNB + E2], lnb_raw[:, :], ident[0:E2, 0:E2]).then_inc(prep["filled"].sem, 1)
            if e == 10:
                pe.wait_ge(*prep["emptied"](1))
                wwait(pe, "e2w1")
                for u in range(2 * E2):
                    last = pe.matmul(ps[:, 7, AT_BIAS + u:AT_BIAS + u + 1], w1_raw[0:C, u // 2, (u % 2) * P:(u % 2 + 1) * P],
                                     lnb[:, u // 2:u // 2 + 1], start=True, stop=True)
                last.then_inc(prep["bias_ps"].sem, 1)
            if e == 15:
                pe.wait_ge(*prep["bias"](1))

        def prep_vector(dve, e):
            if e == 3:
                dve.wait_ge(*prep["filled"](1))
                for h in range(2):
                    dve.tensor_copy(wq_t[h * C:(h + 1) * C, :], ps[0:C, 7, 0:INNER])
                dve.tensor_copy(lnb[:, :], ps[0:C, 7, AT_LNB:AT_LNB + E2])
            if e == 4:
                dve.tensor_copy(gsum[:, :], ps[:, 7, AT_GSUM:AT_GSUM + E2])
                dve.tensor_copy(b1_t[:, :], ps[:, 7, AT_B1:AT_B1 + 2 * E2])
                dve.tensor_copy(lng[:, :], ps[:, 7, AT_LNG:AT_LNG + E2])
                dve.tensor_copy(wo[:, :], ps[:, 7, AT_WO:AT_WO + C])
            if e in (5, 6):
                h = e - 5
                last = dve.tensor_copy(wkv[h * C:(h + 1) * C, :, :].rearrange("p k i -> p (k i)"), ps[0:C, 7, INNER:3 * INNER])
                if h == 1:
                    last.then_inc(prep["emptied"].sem, 1)
            if e == 7:
                for h in range(2):
                    hs = slice(h * C, (h + 1) * C)
                    dve.tensor_copy(ident2[hs, :], ident[hs, hs])
                dve.tensor_copy(dw_hi[:, :], dw_raw[:, :])
                vlink(dve.tensor_copy(wq[:, 0, :], wq_t[:, :]))
            if e == 8:
                dve.tensor_tensor(wq[:, 1, :], wq_t[:, :], wq[:, 0, :].bitcast(F32), ALU.subtract)
                vlink(dve.tensor_tensor(dw_lo[:, :], dw_raw[:, :], dw_hi[:, :].bitcast(F32), ALU.subtract))
            if 9 <= e < 12:
                for t in range(3 * (e - 9), 3 * (e - 8)):
                    dve.tensor_scalar(wdw[:, t, 0, :], ident2[:, :], dw_hi[:, t:t + 1].bitcast(F32), None, ALU.mult)
                    last = dve.tensor_scalar(wdw[:, t, 1, :], ident2[:, :], dw_lo[:, t:t + 1], None, ALU.mult)
                if e == 11:
                    last.then_inc(prep["att"].sem, 1)
            if e == 13:
                dve.wait_ge(*prep["bias_ps"](1))
                dve.tensor_tensor(b1_6[:, :], b1_t[:, :], ps[:, 7, AT_BIAS:AT_BIAS + 2 * E2], ALU.add).then_inc(prep["bias"].sem, 1)
            if e == 14:
                dve.tensor_copy(b2s[:, 0, :], b2_6[:, :])
                vlink(dve.tensor_copy(gw2_6[:, 0, :], gw_6[:, :]))
                dve.tensor_tensor(b2s[:, 1, :], b2_6[:, :], b2s[:, 0, :].bitcast(F32), ALU.subtract)
                dve.tensor_tensor(gw2_6[:, 1, :], gw_6[:, :], gw2_6[:, 0, :].bitcast(F32), ALU.subtract)

        def prep_scalar(act, e):
            if e >= 8:
                f = e - 8
                if f == 0:
                    act.wait_ge(*prep["emptied"](1))
                    wwait(act, "e2w1")
                act.activation(w1_whole[:, 1, f, :], w1_raw[:, f, :], ACT.Copy, scale=lng[:, f:f + 1])
                act.activation(w1_6[:, 0, f, :], w1_raw[:, f, :], ACT.Copy, scale=lng[:, f:f + 1]).then_inc(prep["hi"].sem, 1)

        def e1_vector(dve):
            mm = e1
            ln_vector(dve, mm["rstd"], mm["xu"], mm["fs"], mm["ft_ps"])
            dve.sem_inc(mm["m1"].sem, 2)
            router_logits(dve, mm, E1, b_gw[:, :], 6)
            router_top2(dve, mm, E1)
            dve.sem_inc(mm["hid"].sem, 2)
            dve.sem_inc(mm["ta"].sem, 1)

            def gate(i, e):
                dve.wait_ge(*mm["act"](i * E1 + (e + 1)))
                dve.wait_ge(*mm["h2_ps"](i * E1 + (e + 1)))
                dve.wait_ge(*mm["o_ps"](i * E1 + (e + 1)))
                dve.tensor_tensor(HID[e % 8][:, :], SB[e % 2][:, :], ps[:, 2 + e % 2, :], ALU.mult).then_inc(mm["m1"].sem, 1)

            def weigh(i, e):
                dve.wait_ge(*mm["m1"](i * E1 + (e + 3)))
                dve.wait_ge(*mm["d_ps"](i * E1 + (e + 1)))
                dve.tensor_tensor(HID[e % 8][:, :], HID[e % 8][:, :], ps[:, 4 + e % 2, :], ALU.mult).then_inc(mm["hid"].sem, 1)

            def chunk(i, prev):
                for e in range(E1):
                    gate(i, e)
                    if e >= 1:
                        weigh(i, e - 1)
                    elif prev is not None:
                        weigh(prev, E1 - 1)
                    if prev is None:
                        prep_vector(dve, e)
                    if e == 6 and prev is not None:
                        experts_finish(dve, mm, prev)
                    if 6 < e <= 6 + STEPS and prev is not None:
                        chunk_stats(dve, prev, X, m["d_var"], e - 7)
            chunk(0, None)
            with vchain.loop(1, NCHUNK, 3) as i:
                chunk(i, i - 1)
            weigh(NCHUNK - 1, E1 - 1)
            dve.wait_ge(*mm["o_ps"](N1 + 8))
            chunk_splits(dve, m["d_u"], m["d_fs"], m["d_ft_ps"], (0, 1))
            experts_finish(dve, mm, NCHUNK - 1)
            for step in range(STEPS):
                chunk_stats(dve, NCHUNK - 1, X, m["d_var"], step)

        def e1_scalar2(act):
            mm = e1
            ln_scalar(act, mm["rstd"], mm["xu"], mm["ft_ps"], mm["ft"])
            router_scalar(act, mm, E1)
            router_move(act, mm)
            act.sem_inc(mm["oc"].sem, 1)

            def chunk(i, prev):
                for e in range(E1):
                    act.wait_ge(*mm["h_ps"](i * E1 + (e + 1)))
                    act.wait_ge(*mm["m1"](i * E1 + (e + 1)))
                    act.activation(SB[e % 2][:, :], ps[:, e % 2, :], ACT.Silu).then_inc(mm["act"].sem, 1)
                    if prev is None:
                        prep_scalar(act, e)
                    if e == 3 and prev is not None:
                        move(prev)
                    if e == 15 and prev is not None:
                        chunk_norm(act, prev, m["d_rstd"], m["d_u"])

            def move(i):
                act.wait_ge(*mm["o_ps"](i * E1 + (E1 + 8)))
                act.wait_ge(*mm["t_ps"](i + 1))
                act.activation(OS[:, :], ps[:, 6, :], ACT.Copy).then_inc(mm["oc"].sem, 1)
            chunk(0, None)
            with act.Fori(1, NCHUNK) as i:
                chunk(i, i - 1)
            move(NCHUNK - 1)
            chunk_norm(act, NCHUNK - 1, m["d_rstd"], m["d_u"])

        def e1_tensor(pe):
            mm = e1
            pe.wait_ge(s_gw, 1)
            pe.wait_ge(*m["x3"](G))
            ln_tensor(pe, mm["fs"], mm["ft_ps"], mm["ft"], then=lambda g: router_tensor(pe, g, gw2, E1, 6, mm["lg_ps"]))
            def hidden(i, e):
                pe.wait_ge(*mm["m1"](i * E1 + (e + 1)))
                for k in range(2):
                    for part in range(2):
                        last = pe.matmul(ps[:, 2 * k + e % 2, :], w12[:, part, k, e, :], UT[:, bass.ts(i, CHUNK)],
                                         start=(part == 0), stop=(part == 1))
                    last.then_inc(mm[("h_ps", "h2_ps")[k]].sem, 1)

            pe.wait_ge(s_w12, 8)
            hidden(0, 0)
            hidden(0, 1)
            router_transpose(pe, mm)
            pe.wait_ge(s_sel, 1)
            wwait(pe, "w3")
            pe.wait_ge(*mm["dt"](NCHUNK))
            pe.sem_inc(mm["o_ps"].sem, 8)
            pe.sem_inc(mm["t_ps"].sem, 1)

            def spread(i, e):
                pe.wait_ge(*mm["hid"](i * E1 + (e + 1)))
                pe.matmul(ps[:, 4 + e % 2, :], sel[:, e:e + 1].to_broadcast([P, P]), DT[:, bass.ts(i, CHUNK)], start=True,
                          stop=True).then_inc(mm["d_ps"].sem, 1)

            def outp(i, e):
                pe.wait_ge(*mm["hid"](i * E1 + (e + 4)))
                for f in (e, e + 1):
                    o = C * (f % 2)
                    pe.matmul(ps[o:o + C, 6, :], w3[:, f, :], HID[f % 8][:, :], start=(f < 2),
                              stop=(f >= E1 - 2)).then_inc(mm["o_ps"].sem, 1)

            def chunk(i, prev):
                for e in range(E1):
                    if prev is not None or e >= 2:
                        hidden(i, e)
                    if e >= 1:
                        spread(i, e - 1)
                    elif prev is not None:
                        spread(prev, E1 - 1)
                    if e in (0, 2) and prev is not None:
                        outp(prev, E1 - 4 + e)
                    if e == 4:
                        pe.wait_ge(*mm["oc"](i + 1))
                    if e % 2 == 0 and e >= 4:
                        outp(i, e - 4)
                    if prev is None:
                        prep_tensor(pe, e)
                    if e == 5 and prev is not None:
                        back(prev)

            def back(i):
                pe.wait_ge(*mm["oc"](i + 2))
                pe.wait_ge(*mm["ta"](i + 1))
                for t in range(4):
                    last = pe.transpose(ps[:, 7, t * P:(t + 1) * P], OS[:, t * P:(t + 1) * P], ident[:, :])
                last.then_inc(mm["t_ps"].sem, 1)
            chunk(0, None)
            with pe.Fori(1, NCHUNK) as i:
                chunk(i, i - 1)
            spread(NCHUNK - 1, E1 - 1)
            outp(NCHUNK - 1, E1 - 4)
            outp(NCHUNK - 1, E1 - 2)
            back(NCHUNK - 1)
        retire(sig3)
        sig5 = signals((G, "d_fs d_qe d_qn d_y x5"), (3, "d_hm"), (1, "d_cw"),
                       (NCHUNK, "d_var d_rstd d_u d_ft_ps d_xp d_ql_ps d_ql d_qt_ps d_qt d_cv_ps d_kd d_k_ps d_km d_ke d_v_ps d_v d_kt_ps d_kt"),
                       (NCHUNK, "d_c_ps d_c d_o_ps d_g d_y_ps"))
        m.update(sig5)

        def d_sync(sp):
            wdma(sp, "datt", wq_raw[:, :], a["L2_conv_wq"])
            wdma(sp, "datt", wkv_raw[:, :, :], a["L2_conv_wpw"].rearrange("(k p) c -> p k c", p=INNER))
            wdma(sp, "datt", wo_raw[:, :], a["L2_conv_wout"])
            for h in range(2):
                wdma(sp, "datt", dw_raw[h * C:(h + 1) * C, :], a["L2_conv_wdw"].rearrange("c i h w -> c (i h w)"))
            wdma(sp, "datt", b_o[:, :], a["L2_conv_bout"].unsqueeze(0).to_broadcast([P, C]))

        def d_pool(pool):
            pool.memset(hmask[:, :], 1.0).then_inc(m["d_hm"].sem, 1)
            hv = hmask[:, :].rearrange("p (h e) -> p h e", e=DH)
            pool.wait_ge(*m["d_hm"](1))
            pool.affine_select(out=hv, in_=hv, compare_op=ALU.is_ge, fill=0.0, base=0, pattern=[[-DH, HEADS], [0, DH]],
                               channel_multiplier=1).then_inc(m["d_hm"].sem, 1)
            pool.wait_ge(*m["d_hm"](2))
            pool.affine_select(out=hv, in_=hv, compare_op=ALU.is_ge, fill=0.0, base=DH - 1, pattern=[[DH, HEADS], [0, DH]],
                               channel_multiplier=-1).then_inc(m["d_hm"].sem, 1)
            chunk_rstd(pool, eps_c, m["d_var"], m["d_rstd"])

        ROUND = 1.5 * 2 ** 23

        def quantise(dve, step):
            if step == 0:
                wwait(dve, "cw")
                dve.tensor_reduce(amax[0][:, :], cw_raw, X_AXIS, ALU.max)
                vlink(dve.tensor_reduce(amax[2][:, :], cw_raw, X_AXIS, ALU.min, negate=True))
                vlink(dve.tensor_tensor(amax[1][:, :], amax[0][:, :], amax[2][:, :], ALU.max))
            if step == 1:
                vlink(dve.tensor_scalar(amax[2][:, :], amax[1][:, :], 1.0 / 7.0, None, ALU.mult))
                vlink(dve.scalar_tensor_tensor(amax[0][:, :], amax[2][:, :], -8.0, amax[1][:, :], ALU.mult, ALU.add))
                vlink(dve.tensor_tensor(amax[0][:, :], amax[0][:, :], amax[2][:, :], ALU.add))
                vlink(dve.scalar_tensor_tensor(amax[2][:, :], amax[0][:, :], 1.0 / 7.0, amax[2][:, :], ALU.mult, ALU.add))
                vlink(dve.tensor_scalar(amax[3][:, :], amax[2][:, :], 2e-16, None, ALU.max))
            if step == 2:
                vlink(dve.tensor_copy(sc_hi[:, :], amax[3][:, :]))
                dve.tensor_tensor(nsc[1][:, :], sc_hi[:, :].bitcast(F32), amax[3][:, :], ALU.subtract)
                dve.tensor_scalar(nsc[0][:, :], sc_hi[:, :].bitcast(F32), -1.0, None, ALU.mult)
                vlink(dve.reciprocal(amax[0][:, :], amax[3][:, :]))
            if step == 3:
                vlink(dve.tensor_scalar(cw_q[:, :], cw_raw, amax[0][:, :], None, ALU.mult))
                vlink(dve.tensor_copy(cq_hi, cw_q[:, :]))
                vlink(dve.tensor_tensor(cq_lo, cw_q[:, :], cq_hi.bitcast(F32), ALU.subtract))
            if step == 4:
                vlink(dve.scalar_tensor_tensor(cw_q1, cq_hi.bitcast(F32), nsc[0][:, :], cw_raw, ALU.mult, ALU.add))
                for q, sc in ((cq_hi.bitcast(F32), 1), (cq_lo, 0), (cq_lo, 1)):
                    vlink(dve.scalar_tensor_tensor(cw_q1, q, nsc[sc][:, :], cw_q1, ALU.mult, ALU.add))
            if step == 5:
                vlink(dve.scalar_tensor_tensor(cw_q[:, :], cw_q1, amax[0][:, :], cw_q[:, :], ALU.mult, ALU.add))
                vlink(dve.tensor_scalar(cw_q1, cw_q[:, :], ROUND, None, ALU.add))
                vlink(dve.tensor_scalar(cw_q[:, :], cw_q1, -ROUND, None, ALU.add))
            if step == 6:
                vlink(dve.tensor_scalar(cw_q1, cw_q[:, :], 7.0, -7.0, ALU.min, ALU.max))
                vlink(dve.tensor_scalar(cw_q[:, :], cw_q1, amax[3][:, :], None, ALU.mult))
            if step == 7:
                vlink(dve.tensor_tensor(cw_q1, cw_q[:, :], cw_raw, ALU.subtract))
                dve.tensor_tensor(cw_q[:, :], cw_raw, cw_q1, ALU.add).then_inc(m["d_cw"].sem, 1)

        def second_stats(dve, g):
            ln_norm_vector(dve, g, e2["rstd"], e2["xu"])
            ln_stats(dve, g, U[:, g * TG:(g + 1) * TG, :], e2["var2"])
            dve.wait_ge(*e2["var2"](g + 1))

        def d_vector(dve):
            dve.wait_ge(*m["d_hm"](3))

            def q_center(g):
                for j in range(2):
                    dve.wait_ge(*m["d_ql_ps"](2 * g + j + 1))
                    last = dve.tensor_reduce(qr[0][:, j * 32:(j + 1) * 32], ps[:, 2 + j, :].rearrange("p (t d) -> p t d", d=DH),
                                             X_AXIS, ALU.max)
                vlink(last)
                for j in range(2):
                    dve.tensor_tensor(QL[:, 4 * j:4 * j + 4, :].rearrange("p t (h d) -> p (t h) d", d=DH),
                                      ps[:, 2 + j, :].rearrange("p (t d) -> p t d", d=DH),
                                      bc(qr[0][:, j * 32:(j + 1) * 32], DH), ALU.subtract).then_inc(m["d_ql"].sem, 1)

            def q_norm(g):
                dve.wait_ge(*m["d_qe"](g + 1))
                vlink(dve.tensor_reduce(qr[1][:, :], QE[:, :, :].rearrange("p t (h d) -> p (t h) d", d=DH), X_AXIS, ALU.add))
                vlink(dve.reciprocal(qr[2][:, :], qr[1][:, :]))
                vlink(dve.tensor_scalar(qr[1][:, :], qr[2][:, :], DH ** -0.5, None, ALU.mult))
                qe = QE[:, :, :].rearrange("p t (h d) -> p (t h) d", d=DH)
                dve.tensor_tensor(qe, qe, bc(qr[1][:, :], DH), ALU.mult).then_inc(m["d_qn"].sem, 1)

            def kmax(j):
                dve.wait_ge(*m["d_k_ps"](j + 1))
                dve.tensor_reduce(nkm[:, 2 * j:2 * j + 2], ps[:, 5, :].rearrange("p (r s) -> p r s", r=2), X_AXIS, ALU.max,
                                  negate=True).then_inc(m["d_km"].sem, 1)

            def ctx_out(j):
                dve.wait_ge(*m["d_ke"](j + 1))
                vlink(dve.reciprocal(rks[:, 2 * j:2 * j + 2], ksum[:, 2 * j:2 * j + 2]))
                dve.wait_ge(*m["d_c_ps"](j + 1))
                for r in range(2):
                    b = 2 * j + r
                    last = dve.scalar_tensor_tensor(CTX[:, b, :], ps[:, 7, r * INNER:(r + 1) * INNER], rks[:, b:b + 1],
                                                    hmask[:, :], ALU.mult, ALU.mult)
                last.then_inc(m["d_c"].sem, 1)
            for j in range(NCHUNK):
                g = j // 2
                kmax(j)
                if j >= 1:
                    ctx_out(j - 1)
                if j < 2:
                    chunk_splits(dve, m["d_u"], m["d_fs"], m["d_ft_ps"], (2 + j,))
                if j % 2 == 0:
                    q_center(g)
                else:
                    q_norm(g)
                quantise(dve, j)
            ctx_out(NCHUNK - 1)
            for g in range(G):
                sl = slice(g * TG, (g + 1) * TG)
                dve.wait_ge(*m["d_y_ps"](2 * g + 2))
                dve.tensor_tensor(XC[g % 2][:, :, :], ps[:, 4 + g % 2, :].rearrange("p (t c) -> p t c", c=C), bcm(b_o[:, :], TG),
                                  ALU.add).then_inc(m["d_y"].sem, 1)
                dve.wait_ge(*m["d_y"](g + 1))
                dve.tensor_tensor(X[:, sl, :], X[:, sl, :], XC[g % 2][:, :, :], ALU.add).then_inc(m["x5"].sem, 1)
                ln_stats_of(dve, g, m["x5"], e2["var"])
                if g >= 1:
                    second_stats(dve, g - 1)
            second_stats(dve, G - 1)

        def d_scalar(act):

            def padded(g):
                if g >= 2:
                    act.wait_ge(*m["d_cv_ps"](2 * (g - 1)))
                for j in range(2):
                    act.wait_ge(*m["d_ft_ps"](2 * g + j + 1))
                    act.activation(UT[:, (2 * g + j) * CHUNK:(2 * g + j + 1) * CHUNK], ps[:, j, :], ACT.Copy)
                    to_padded(act, j, XP[g % 2], j, m["d_xp"])

            def q_exp(g):
                act.wait_ge(*m["d_ql"](2 * g + 2))
                if g >= 1:
                    act.wait_ge(*m["d_qt_ps"](2 * g))
                act.activation(QE[:, :, :].rearrange("p t c -> p (t c)"), QL[:, :, :].rearrange("p t c -> p (t c)"),
                               ACT.Exp).then_inc(m["d_qe"].sem, 1)

            def q_move(g):
                for j in range(2):
                    act.wait_ge(*m["d_qt_ps"](2 * g + j + 1))
                    act.activation(QT[:, (2 * g + j) * CHUNK:(2 * g + j + 1) * CHUNK], ps[:, j, :], ACT.Copy).then_inc(m["d_qt"].sem, 1)

            def kd(j):
                act.wait_ge(*m["d_cv_ps"](j + 1))
                if j >= 2:
                    act.wait_ge(*m["d_v_ps"](j - 1))
                act.activation(KD[j % 2][:, :], ps[:, 4, :], ACT.Copy).then_inc(m["d_kd"].sem, 1)

            def kexp(j):
                act.wait_ge(*m["d_v_ps"](j + 1))
                if j >= 2:
                    act.wait_ge(*m["d_c_ps"](j - 1))
                act.activation(VT[j % 2][:, :, :].rearrange("p t c -> p (t c)"), ps[:, 6, :], ACT.Copy).then_inc(m["d_v"].sem, 1)
                act.wait_ge(*m["d_km"](j + 1))
                for r in range(2):
                    b = 2 * j + r
                    last = act.activation(KE[j % 2][:, r * PIX:(r + 1) * PIX], ps[:, 5, r * PIX:(r + 1) * PIX], ACT.Exp,
                                          bias=nkm[:, b:b + 1], accum_out=ksum[:, b:b + 1])
                last.then_inc(m["d_ke"].sem, 1)

            def kt(j):
                act.wait_ge(*m["d_kt_ps"](j + 1))
                act.activation(KT[j % 2][:, :, :].rearrange("p t c -> p (t c)"), ps[:, 7, :], ACT.Copy).then_inc(m["d_kt"].sem, 1)
            padded(0)
            kd(0)
            for j in range(NCHUNK):
                g = j // 2
                kexp(j)
                if j % 2 == 0 and g + 1 < G:
                    padded(g + 1)
                if j + 1 < NCHUNK:
                    kd(j + 1)
                kt(j)
                if j % 2 == 0:
                    q_exp(g)
                else:
                    q_move(g)
            wwait(act, "datt")
            for j in range(NCHUNK):
                act.wait_ge(*m["d_o_ps"](j + 1))
                if j >= 2:
                    act.wait_ge(*m["d_y_ps"](j - 1))
                act.activation(KE[j % 2][:, :], ps[:, 2 + j % 2, :], ACT.Gelu).then_inc(m["d_g"].sem, 1)
                if j % 2 == 1 and j >= 3:
                    ln_norm(act, j // 2 - 1, e2["rstd"], e2["xu"])
            ln_norm(act, G - 1, e2["rstd"], e2["xu"])

        def d_tensor(pe):
            pe.wait_ge(*e1["ta"](NCHUNK + 1))
            pe.wait_ge(*prep["att"](1))

            def tr(g):
                pe.wait_ge(*m["d_fs"](g + 1))
                if g >= 1:
                    pe.wait_ge(*m["d_xp"](2 * g))
                transpose_tiles(pe, US[g % 2], (0, 1), m["d_ft_ps"])

            def qlog(g):
                for j in range(2):
                    pe.wait_ge(*m["d_xp"](2 * g + j + 1))
                    if g >= 1:
                        pe.wait_ge(*m["d_ql"](2 * (g - 1) + j + 1))
                    for t in range(4):
                        lhs = UT[:, (2 * g + j) * CHUNK + t * P:(2 * g + j) * CHUNK + (t + 1) * P]
                        for part in range(2):
                            last = pe.matmul(ps[:, 2 + j, t * P:(t + 1) * P], lhs, wq[:, part, :], start=(part == 0), stop=(part == 1))
                    last.then_inc(m["d_ql_ps"].sem, 1)

            def conv(j):
                g, jj = j // 2, j % 2
                xp = XP[g % 2][:, :, :].rearrange("p b (y x) -> p b y x", x=PADW)
                pe.wait_ge(*m["d_xp"](j + 1))
                if j >= 1:
                    pe.wait_ge(*m["d_kd"](j))
                for t in range(9):
                    dy, dx = t // 3, t % 3
                    last = pe.matmul(ps[:, 4, :], wdw[:, t, :, :].rearrange("p h c -> p (h c)"),
                                     xp[:, 2 * jj:2 * jj + 2, dy:dy + H, dx:dx + W], start=(t == 0), stop=(t == 8))
                last.then_inc(m["d_cv_ps"].sem, 1)

            def kv(j):
                pe.wait_ge(*m["d_kd"](j + 1))
                if j >= 1:
                    pe.wait_ge(*m["d_ke"](j))
                    pe.wait_ge(*m["d_v"](j))
                pe.matmul(ps[:, 5, :], wkv[:, 0, :], KD[j % 2][:, :], start=True, stop=True).then_inc(m["d_k_ps"].sem, 1)
                for t in range(4):
                    last = pe.matmul(ps[:, 6, t * P:(t + 1) * P], KD[j % 2][:, t * P:(t + 1) * P], wkv[:, 1, :], start=True, stop=True)
                last.then_inc(m["d_v_ps"].sem, 1)

            def ktr(j):
                pe.wait_ge(*m["d_ke"](j + 1))
                if j >= 1:
                    pe.wait_ge(*m["d_c"](j))
                for t in range(4):
                    last = pe.transpose(ps[:, 7, t * P:(t + 1) * P], KE[j % 2][:, t * P:(t + 1) * P], ident[:, :])
                last.then_inc(m["d_kt_ps"].sem, 1)

            def ctxm(j):
                pe.wait_ge(*m["d_kt"](j + 1))
                pe.wait_ge(*m["d_v"](j + 1))
                for r in range(2):
                    for half in range(2):
                        t = 2 * r + half
                        last = pe.matmul(ps[:, 7, r * INNER:(r + 1) * INNER], KT[j % 2][:, t, :], VT[j % 2][:, t, :],
                                         start=(half == 0), stop=(half == 1))
                last.then_inc(m["d_c_ps"].sem, 1)

            def qtr(g):
                pe.wait_ge(*m["d_qn"](g + 1))
                for t in range(TG):
                    last = pe.transpose(ps[:, t // 4, (t % 4) * P:(t % 4 + 1) * P], QE[:, t, :], ident[:, :])
                    if t % 4 == 3:
                        last.then_inc(m["d_qt_ps"].sem, 1)
            tr(0)
            conv(0)
            for j in range(NCHUNK):
                g = j // 2
                if j % 2 == 0:
                    qlog(g)
                kv(j)
                if j >= 1:
                    ctxm(j - 1)
                if j % 2 == 0 and g + 1 < G:
                    if g >= 1:
                        pe.wait_ge(*m["d_qt"](2 * g))
                    tr(g + 1)
                if j + 1 < NCHUNK:
                    conv(j + 1)
                ktr(j)
                if j % 2 == 1:
                    qtr(g)
            ctxm(NCHUNK - 1)
            def att(j):
                pe.wait_ge(*m["d_c"](NCHUNK))
                pe.wait_ge(*m["d_qt"](NCHUNK))
                if j >= 2:
                    pe.wait_ge(*m["d_g"](j - 1))
                for r in range(2):
                    b = 2 * j + r
                    image = lambda cols: cols.rearrange("p (h r s) -> p r h s", h=2, r=2)[:, r, :, :]
                    last = pe.matmul(image(ps[:, 2 + j % 2, :]), CTX[:, b, :], image(QT[:, j * CHUNK:(j + 1) * CHUNK]),
                                     start=True, stop=True)
                last.then_inc(m["d_o_ps"].sem, 1)

            def proj(j):
                g = j // 2
                pe.wait_ge(*m["d_g"](j + 1))
                if g >= 2 and j % 2 == 0:
                    pe.wait_ge(*m["d_y"](g - 1))
                for t in range(4):
                    o = (j % 2) * 4 + t
                    last = pe.matmul(ps[:, 4 + g % 2, o * C:(o + 1) * C], KE[j % 2][:, t * P:(t + 1) * P], wo[:, :], start=True, stop=True)
                last.then_inc(m["d_y_ps"].sem, 1)
            att(0)
            for j in range(NCHUNK):
                if j + 1 < NCHUNK:
                    att(j + 1)
                proj(j)
        retire(e1)
        U2 = 2 * E2
        e2 = signals((G, "var rstd xu var2 rstd2 xu2 fs ds"), (G, "lg_ps"), (1, "sub exp"), (NCHUNK, "ft_ps ft dt_ps dt x"),
                     (4 + NCHUNK * U2, "act"), (NCHUNK * U2, "h_ps"), (NCHUNK * E2, "d_ps"), (3 + NCHUNK * U2, "hid"),
                     (8 + NCHUNK * U2, "o_ps"), (1 + NCHUNK, "oc t_ps ta"))

        def e2_sync(sp):
            for h in range(2):
                wdma(sp, "e2s", gw_6[h * C:(h + 1) * C, :], a["L2_ffn_Wr"])
                wdma(sp, "e2s", lng_raw[:, h * C:(h + 1) * C], a["L2_ffn_ln_g"])
            wdma(sp, "e2s", b_gw_6[:, :], a["L2_ffn_br"].unsqueeze(0).to_broadcast([P, E2]))
            wdma(sp, "e2s", lnb_raw[:, :], a["L2_ffn_ln_b"])
            wdma(sp, "e2s", b1_raw[:, :], a["L2_ffn_b1"].rearrange("e (h p) -> (e h) p", p=P))
            sp.wait_ge(*m["x3"](1))
            for r in (0, 32):
                wdma(sp, "e2s", b2_6[r:r + E2, 0:C], a["L2_ffn_b2"])
            for h in range(2):
                wdma(sp, "e2w1", w1_raw[h * C:(h + 1) * C, :, :], a["L2_ffn_W1"].rearrange("e d h -> d e h"))
            sp.wait_ge(*e1["x"](NCHUNK))
            wdma(sp, "e2w2", w2_6[:, :, :, :], a["L2_ffn_W2"].rearrange("e (h p) o -> p e h o", p=P))

        def e2_pool(pool):
            ln_rstd(pool, 0, 1e-5, e2["var"], e2["rstd"])
            for g in range(G):
                if g + 1 < G:
                    ln_rstd(pool, g + 1, 1e-5, e2["var"], e2["rstd"])
                ln_rstd(pool, g, 1e-5, e2["var2"], e2["rstd2"])

        def taps_tensor(pe, u):
            wv = cw_q[:, :].rearrange("o (c t) -> o t c", t=9)
            if u == 1:
                pe.wait_ge(*m["d_cw"](1))
                for t in range(8):
                    last = pe.matmul(ps[0:C, 7, t * C:(t + 1) * C], wv[:, t, :], ident[0:C, 0:C], is_transpose=True)
                last.then_inc(m["q_wps"].sem, 1)
            if u == 9:
                pe.wait_ge(*m["q_tap"](1))
                pe.matmul(ps[0:C, 7, 0:C], wv[:, 8, :], ident[0:C, 0:C], is_transpose=True).then_inc(m["q_wps2"].sem, 1)
            if u == 15:
                pe.wait_ge(*m["q_w"](1))

        def taps_vector(dve, u):
            if u in (4, 6):
                h = (u - 4) // 2
                if h == 0:
                    dve.wait_ge(*m["q_wps"](1))
                last = dve.tensor_copy(cw_t[h * C:(h + 1) * C, 0:8, :], ps[0:C, 7, :].rearrange("p (t o) -> p t o", o=C))
                if h == 1:
                    last.then_inc(m["q_tap"].sem, 1)
            if u == 11:
                dve.wait_ge(*m["q_wps2"](1))
                dve.tensor_copy(cw_t[0:C, 8, :], ps[0:C, 7, 0:C])
                vlink(dve.tensor_copy(cw_t[C:P, 8, :], ps[0:C, 7, 0:C]))
            if u == 12:
                vlink(dve.tensor_copy(cw[:, :, 0, :], cw_t[:, :, :]))
            if u == 13:
                dve.tensor_tensor(cw[:, :, 1, :], cw_t[:, :, :], cw[:, :, 0, :].bitcast(F32), ALU.subtract).then_inc(m["q_w"].sem, 1)

        def e2_vector(dve):
            mm = e2
            for i in range(2):
                for c0 in (E2, 32 + E2):
                    dve.memset(DS[i][:, :, c0:c0 + E1 - E2].bitcast(F32), 0.0)

            for g in range(G):
                ln_norm_vector(dve, g, mm["rstd2"], mm["xu2"], src=U, dst=XC[g % 2])
                if g >= 2:
                    dve.wait_ge(*mm["ft_ps"](2 * (g - 1)))
                split(dve, US[g % 2], XC[g % 2][:, :, :], mm["fs"])

            def rescale(dve, r1):
                r2 = RT[2][:, :, 0:E2]
                dve.tensor_tensor(r8[6][:, :], vpe[:, :], rstd[:, :], ALU.mult)
                vlink(dve.tensor_scalar(r8[7][:, :], S1_[:, :], 0.5, None, ALU.mult))
                dve.tensor_tensor(r2, bc(r8[7][:, :], E2), bcm(gsum[:, :], NT), ALU.mult)
                vlink(dve.tensor_tensor(r1, r1, bc(r8[6][:, :], E2), ALU.mult))
                vlink(dve.tensor_tensor(r1, r1, r2, ALU.add))
            router_logits(dve, mm, E2, b_gw_6[:, :], 7, rescale)
            router_top2(dve, mm, E2)
            dve.sem_inc(mm["hid"].sem, 3)
            dve.sem_inc(mm["ta"].sem, 1)

            def weigh(i, u):
                dve.wait_ge(*mm["act"](i * U2 + (u + 5)))
                if u % 2 == 0:
                    dve.wait_ge(*mm["d_ps"](i * E2 + (u // 2 + 1)))
                dve.tensor_tensor(HID[u % 8][:, :], HID[u % 8][:, :], ps[:, 4 + (u // 2) % 2, :], ALU.mult).then_inc(mm["hid"].sem, 1)

            def chunk(i, prev):
                for u in range(U2):
                    weigh(i, u)
                    if prev is None:
                        taps_vector(dve, u)
                    if u == 6 and prev is not None:
                        experts_finish(dve, mm, prev)
                    if 6 < u <= 6 + STEPS and prev is not None:
                        chunk_stats(dve, prev, X, m["q_var"], u - 7)
            chunk(0, None)
            with vchain.loop(1, NCHUNK, 3) as i:
                chunk(i, i - 1)
            dve.wait_ge(*mm["o_ps"](NCHUNK * U2 + 8))
            chunk_splits(dve, m["q_u"], m["q_fs"], m["q_ft_ps"], (0, 1))
            experts_finish(dve, mm, NCHUNK - 1)
            for step in range(STEPS):
                chunk_stats(dve, NCHUNK - 1, X, m["q_var"], step)

        def e2_scalar(act):
            mm = e2
            for g in range(G + 1):
                if g < G:
                    if g >= 2:
                        act.wait_ge(*mm["fs"](g - 1))
                    ln_norm(act, g, mm["rstd2"], mm["xu2"], src=U, dst=XC[g % 2])
                if g >= 1:
                    for j in (2 * g - 2, 2 * g - 1):
                        act.wait_ge(*mm["ft_ps"](j + 1))
                        act.activation(UT[:, j * CHUNK:(j + 1) * CHUNK], ps[:, j % 2, :], ACT.Copy).then_inc(mm["ft"].sem, 1)
            act.wait_ge(*prep["bias"](1))
            act.sem_inc(mm["act"].sem, 4)
            router_scalar(act, mm, E2)
            router_move(act, mm)
            act.sem_inc(mm["oc"].sem, 1)

            def chunk(i, prev):
                for u in range(U2):
                    act.wait_ge(*mm["h_ps"](i * U2 + (u + 1)))
                    act.wait_ge(*mm["o_ps"](i * U2 + (u + 1)))
                    act.activation(HID[u % 8][:, :], ps[:, u % 4, :], ACT.Gelu, bias=b1_6[:, u:u + 1]).then_inc(mm["act"].sem, 1)
                    if u == 12 and prev is None:
                        wwait(act, "i8")
                        act.activation(w1_8[:, :, 0, :], w1_8raw[:, :, :], ACT.Copy).then_inc(m["q_i8hi"].sem, 1)
                    if u == 2 and prev is not None:
                        move(prev)
                    if u == 15 and prev is not None:
                        chunk_norm(act, prev, m["q_rstd"], m["q_u"])

            def move(i):
                act.wait_ge(*mm["o_ps"](i * U2 + (U2 + 8)))
                act.wait_ge(*mm["t_ps"](i + 1))
                act.activation(OS[:, :], ps[:, 6, :], ACT.Copy).then_inc(mm["oc"].sem, 1)
            chunk(0, None)
            with act.Fori(1, NCHUNK) as i:
                chunk(i, i - 1)
            move(NCHUNK - 1)
            chunk_norm(act, NCHUNK - 1, m["q_rstd"], m["q_u"])

        def e2_tensor(pe):
            mm = e2
            ln_tensor(pe, mm["fs"], mm["ft_ps"], mm["ft"], then=lambda g: router_tensor(pe, g, gw2_6, E2, 7, mm["lg_ps"]))
            def hidden(i, u):
                e, h = u // 2, u % 2
                pe.wait_ge(*mm["act"](i * U2 + (u + 1)))
                for part in range(2):
                    last = pe.matmul(ps[:, u % 4, :], w1_6[:, part, e, h * P:(h + 1) * P], UT[:, bass.ts(i, CHUNK)],
                                     start=(part == 0), stop=(part == 1))
                last.then_inc(mm["h_ps"].sem, 1)

            pe.wait_ge(*prep["lo"](E2))
            for u in range(4):
                hidden(0, u)
            router_transpose(pe, mm)
            wwait(pe, "e2w2")
            pe.wait_ge(*mm["dt"](NCHUNK))
            pe.sem_inc(mm["o_ps"].sem, 8)
            pe.sem_inc(mm["t_ps"].sem, 1)

            def spread(i, e):
                pe.wait_ge(*mm["hid"](i * U2 + (2 * e + 1)))
                pe.matmul(ps[:, 4 + e % 2, :], sel[:, e:e + 1].to_broadcast([P, P]), DT[:, bass.ts(i, CHUNK)], start=True,
                          stop=True).then_inc(mm["d_ps"].sem, 1)

            def outp(i, e):
                if e == 0:
                    pe.wait_ge(*mm["oc"](i + 1))
                    for part in range(2):
                        pe.matmul(ps[:, 6, :], b2s[:, part, :], DT[:, bass.ts(i, CHUNK)], start=(part == 0), stop=False)
                pe.wait_ge(*mm["hid"](i * U2 + (2 * e + 5)))
                for h in range(2):
                    u = 2 * e + h
                    pe.matmul(ps[h * C:(h + 1) * C, 6, :], w2_6[:, e, h, :], HID[u % 8][:, :], start=False,
                              stop=(e == E2 - 1)).then_inc(mm["o_ps"].sem, 1)

            def chunk(i, prev):
                for e in range(E2):
                    if prev is not None or e >= 2:
                        hidden(i, 2 * e)
                        hidden(i, 2 * e + 1)
                    spread(i, e)
                    if e >= 1:
                        outp(i, e - 1)
                    elif prev is not None:
                        outp(prev, E2 - 1)
                    if prev is None:
                        taps_tensor(pe, 2 * e + 1)
                    if e == 2 and prev is not None:
                        back(prev)

            def back(i):
                pe.wait_ge(*mm["oc"](i + 2))
                pe.wait_ge(*mm["ta"](i + 1))
                for t in range(4):
                    last = pe.transpose(ps[:, 7, t * P:(t + 1) * P], OS[:, t * P:(t + 1) * P], ident[:, :])
                last.then_inc(mm["t_ps"].sem, 1)
            chunk(0, None)
            with pe.Fori(1, NCHUNK) as i:
                chunk(i, i - 1)
            outp(NCHUNK - 1, E2 - 1)
            back(NCHUNK - 1)
        retire(sig5)
        sig7 = signals((G, "q_fs"), (NCHUNK, "q_var q_rstd q_u q_ft_ps q_xp q_cv_ps q_cv q_t_ps q_ta x7"),
                       (1, "q_wps q_tap q_wps2 q_w q_i8hi q_i8lo"))
        m.update(sig7)

        def q_sync(sp):
            wdma(sp, "cw", cw_raw, a["L3_conv_w"].rearrange("o c h w -> o (c h w)"))

        def q_pool(pool):
            pool.wait_ge(*m["q_i8hi"](1))
            pool.tensor_tensor(w1_8[:, :, 1, :], w1_8raw[:, :, :], w1_8[:, :, 0, :].bitcast(F32), ALU.subtract).then_inc(m["q_i8lo"].sem, 1)
            chunk_rstd(pool, eps_c, m["q_var"], m["q_rstd"])

        def q_vector(dve):
            chunk_splits(dve, m["q_u"], m["q_fs"], m["q_ft_ps"], (2, 3))
            for j in range(NCHUNK):
                sl = slice(4 * j, 4 * j + 4)
                dve.wait_ge(*m["q_t_ps"](j + 1))
                dve.tensor_reduce(OA[:, :, :], ps[:, 4 + j % 2, :].rearrange("p (t h c) -> p t c h", h=2, c=C), X_AXIS,
                                  ALU.add).then_inc(m["q_ta"].sem, 1)
                dve.wait_ge(*m["q_ta"](j + 1))
                dve.tensor_tensor(X[:, sl, :], X[:, sl, :], OA[:, :, :], ALU.add).then_inc(m["x7"].sem, 1)
                dve.wait_ge(*m["x7"](j + 1))
                if j % 2 == 1:
                    ln_stats_of(dve, j // 2, m["x7"], m["i_var"], per=2)

        def q_scalar(act):
            def padded(g):
                if g >= 2:
                    act.wait_ge(*m["q_cv_ps"](2 * (g - 1)))
                for j in range(2):
                    act.wait_ge(*m["q_ft_ps"](2 * g + j + 1))
                    to_padded(act, j, XP[g % 2], j, m["q_xp"])

            def move(j):
                act.wait_ge(*m["q_cv_ps"](j + 1))
                if j >= 2:
                    act.wait_ge(*m["q_t_ps"](j - 1))
                act.activation(CQ[j % 2][:, :], ps[:, 2 + j % 2, :], ACT.Copy).then_inc(m["q_cv"].sem, 1)
            padded(0)
            for g in range(G):
                if g + 1 < G:
                    padded(g + 1)
                move(2 * g)
                move(2 * g + 1)

        def q_tensor(pe):
            pe.wait_ge(*m["q_w"](1))

            def tr(g):
                pe.wait_ge(*m["q_fs"](g + 1))
                if g >= 1:
                    pe.wait_ge(*m["q_xp"](2 * g))
                transpose_tiles(pe, US[g % 2], (0, 1), m["q_ft_ps"])

            def conv(j):
                g, jj = j // 2, j % 2
                xp = XP[g % 2][:, :, :].rearrange("p b (y x) -> p b y x", x=PADW)
                pe.wait_ge(*m["q_xp"](j + 1))
                if j >= 2:
                    pe.wait_ge(*m["q_cv"](j - 1))
                for t in range(9):
                    dy, dx = t // 3, t % 3
                    last = pe.matmul(ps[:, 2 + jj, :], cw[:, t, :, :].rearrange("p h c -> p (h c)"),
                                     xp[:, 2 * jj:2 * jj + 2, dy:dy + H, dx:dx + W], start=(t == 0), stop=(t == 8))
                last.then_inc(m["q_cv_ps"].sem, 1)

            def back(j):
                pe.wait_ge(*m["q_cv"](j + 1))
                if j >= 2:
                    pe.wait_ge(*m["q_ta"](j - 1))
                for t in range(4):
                    half, r = t // 2, t % 2
                    c0 = r * PIX + half * P
                    last = pe.transpose(ps[:, 4 + j % 2, t * P:(t + 1) * P], CQ[j % 2][:, c0:c0 + P], ident[:, :])
                last.then_inc(m["q_t_ps"].sem, 1)
            tr(0)
            for g in range(G):
                if g + 1 < G:
                    tr(g + 1)
                conv(2 * g)
                if g:
                    back(2 * g - 1)
                conv(2 * g + 1)
                back(2 * g)
            back(NCHUNK - 1)
        retire(e2)
        NU = 2 * B
        sig8 = signals((G, "i_var i_rstd i_fs i_u z_var z_rstd z_u x8"), (NCHUNK, "i_ft_ps i_ft"),
                       (1, "i_mean i_lg_ps i_l i_e i_rw i_ld_ps i_l2 i_e2 i_w i_we i_top i_tr_ps i_tr i_bc_ps i_ready"),
                       (4 + NU, "i_h"), (8 + NU, "i_y_ps"), (NU, "i_h_ps i_ws"), (2 + NCHUNK, "i_yc i_t_ps i_z"))
        m.update(sig8)
        CAP = -(-TOK * 5 // 4 // E3)

        def i_sync(sp):
            sp.wait_ge(*m["x5"](G))
            for h in range(2):
                wdma(sp, "i8", wr_8[h * C:(h + 1) * C, :], a["L3_ffn_Wr"])
            wdma(sp, "i8", br_8[:, :], a["L3_ffn_br"].unsqueeze(0).to_broadcast([B, E3]))
            wdma(sp, "i8", gam[:, :], a["L3_ffn_gamma"].unsqueeze(0).to_broadcast([P, C]))
            wdma(sp, "i8", bet[:, :], a["L3_ffn_beta"].unsqueeze(0).to_broadcast([P, C]))
            for h in range(2):
                wdma(sp, "i8", w1_8raw[h * C:(h + 1) * C, :, :], a["L3_ffn_W1"].rearrange("e d f -> d e f"))
            wdma(sp, "i8", w2_8[:, :, :], a["L3_ffn_W2"].rearrange("e f o -> f e o"))
            wdma(sp, "i8", b1_8[:, :], a["L3_ffn_b1"])
            wdma(sp, "i8", b2_8[:, :], a["L3_ffn_b2"])

        def i_pool(pool):
            ln_pool(pool, 1e-5, m["i_var"], m["i_rstd"])
            ln_pool(pool, 1e-5, m["z_var"], m["z_rstd"])

        HB, SUM, BACK = (2, 3, 4, 5), (6, 1), (7, 0)

        def i_vector(dve):
            wwait(dve, "i8")
            ln_vector(dve, m["i_rstd"], m["i_u"], m["i_fs"], m["i_ft_ps"])

            dve.wait_ge(*m["i_ft"](NCHUNK))
            dve.tensor_scalar(mean8[:, :], tsum[:, :], 1.0 / PIX, None, ALU.mult).then_inc(m["i_mean"].sem, 1)
            dve.wait_ge(*m["i_lg_ps"](1))
            vlink(dve.tensor_tensor(im[0][:, :], ps[0:B, 3, 0:E3], br_8[:, :], ALU.add))
            vlink(dve.tensor_reduce(i1[0][:, :], im[0][:, :], X_AXIS, ALU.max))
            dve.tensor_scalar(im[1][:, :], im[0][:, :], i1[0][:, :], None, ALU.subtract).then_inc(m["i_l"].sem, 1)
            dve.wait_ge(*m["i_e"](1))
            vlink(dve.tensor_reduce(i1[0][:, :], im[2][:, :], X_AXIS, ALU.add))
            vlink(dve.reciprocal(i1[1][:, :], i1[0][:, :]))
            dve.tensor_scalar(im[3][:, :], im[2][:, :], i1[1][:, :], None, ALU.mult).then_inc(m["i_rw"].sem, 1)
            dve.wait_ge(*m["i_ld_ps"](1))
            vlink(dve.tensor_scalar(im[4][:, :], ps[0:B, 3, 0:E3], float(PIX), None, ALU.mult))
            vlink(dve.reciprocal(im[5][:, :], im[4][:, :]))
            vlink(dve.tensor_scalar(im[4][:, :], im[5][:, :], float(CAP), 1.0, ALU.mult, ALU.min))
            vlink(dve.tensor_tensor(im[0][:, :], im[3][:, :], im[4][:, :], ALU.mult))
            vlink(dve.tensor_reduce(i1[0][:, :], im[0][:, :], X_AXIS, ALU.max))
            dve.tensor_scalar(im[1][:, :], im[0][:, :], i1[0][:, :], None, ALU.subtract).then_inc(m["i_l2"].sem, 1)
            dve.wait_ge(*m["i_e2"](1))
            vlink(dve.tensor_reduce(i1[0][:, :], im[2][:, :], X_AXIS, ALU.add))
            vlink(dve.reciprocal(i1[1][:, :], i1[0][:, :]))
            vlink(dve.tensor_scalar(im[3][:, :], im[2][:, :], i1[1][:, :], None, ALU.mult))
            rv = rev[0:B, 0:E3]
            for k in range(2):
                prob = im[3] if k == 0 else im[6]
                vlink(dve.tensor_reduce(i1[2 + k][:, :], prob[:, :], X_AXIS, ALU.max))
                vlink(dve.tensor_scalar(im[4][:, :], prob[:, :], i1[2 + k][:, :], None, ALU.is_equal))
                vlink(dve.tensor_tensor(im[5][:, :], im[4][:, :], rv, ALU.mult))
                vlink(dve.tensor_reduce(i1[1][:, :], im[5][:, :], X_AXIS, ALU.max))
                dve.tensor_scalar(iw[:, k, 0:1], i1[1][:, :], -1.0, 16.0, ALU.mult, ALU.add)
                vlink(dve.tensor_scalar(hot[:, k, :], im[5][:, :], i1[1][:, :], None, ALU.is_equal))
                if k == 0:
                    vlink(dve.scalar_tensor_tensor(im[6][:, :], hot[:, 0, :], -2.0, im[3][:, :], ALU.mult, ALU.add))
            dve.tensor_tensor(i1[0][:, :], i1[3][:, :], i1[2][:, :], ALU.subtract).then_inc(m["i_w"].sem, 1)
            dve.wait_ge(*m["i_we"](1))
            vlink(dve.tensor_scalar(i1[3][:, :], i1[1][:, :], 1.0, None, ALU.add))
            vlink(dve.reciprocal(iw[:, 0, 1:2], i1[3][:, :]))
            vlink(dve.tensor_tensor(iw[:, 1, 1:2], i1[1][:, :], iw[:, 0, 1:2], ALU.mult))
            vlink(dve.tensor_scalar(im[0][:, :], hot[:, 0, :], iw[:, 0, 1:2], None, ALU.mult))
            dve.scalar_tensor_tensor(im[7][:, :], hot[:, 1, :], iw[:, 1, 1:2], im[0][:, :], ALU.mult, ALU.add)
            dve.tensor_tensor(dia[:, :, :, :].rearrange("p b k v -> p b (k v)"), bc(ident[0:B, 0:B], 4),
                              bcm(iw[:, :, :].rearrange("p k v -> p (k v)"), B), ALU.mult).then_inc(m["i_top"].sem, 1)
            dve.wait_ge(*m["i_tr_ps"](1))
            tp = ps[0:E3, 2, :]
            dve.tensor_copy(hotT[:, :, :].rearrange("p k b -> p (k b)"), tp[:, 0:2 * B])
            dve.tensor_copy(dwT[:, :], tp[:, 2 * B:3 * B])
            pairs = ps[:, 2, P:P + 4 * B].rearrange("p (n v) -> p n v", v=2)
            dve.tensor_copy(idx[:, :], pairs[:, :, 0])
            dve.tensor_copy(wsel[:, :], pairs[:, :, 1]).then_inc(m["i_tr"].sem, 1)
            dve.wait_ge(*m["i_bc_ps"](1))
            dve.tensor_copy(b1u[:, :, :].rearrange("p k b -> p (k b)"), ps[:, 3, 0:2 * B])
            dve.tensor_copy(b2u[:, :], ps[:, 3, 2 * B:2 * B + B // 2]).then_inc(m["i_ready"].sem, 1)
            dve.wait_ge(*m["i_ready"](1))
            dve.sem_inc(m["i_z"].sem, 2)
            dve.wait_ge(*m["q_i8lo"](1))

            def finish(two, p):
                i = two * 2 + p
                dve.wait_ge(*m["i_t_ps"](two * 2 + (p + 3)))
                us_ = U[:, bass.ts(i, 4), :]
                dve.tensor_tensor(us_, us_, ps[:, BACK[p], 0:4 * C].rearrange("p (t c) -> p t c", c=C), ALU.add).then_inc(m["i_z"].sem, 1)

            def pick(two, n):
                e = dve.value_load(idx[0:1, bass.ds(two * 8 + n, 1)], min_val=0, max_val=E3 - 1)
                dve.wait_ge(*m["i_y_ps"](two * 8 + (n // 4 * 4 + 4)))
                dve.tensor_copy(W1S[n][:, :, :], w1_8[:, bass.ds(e, 1), :, :].rearrange("p e h f -> p (e h) f"))
                dve.tensor_scalar(W2S[n][:, :], w2_8[:, bass.ds(e, 1), :].rearrange("p e c -> p (e c)"),
                                  wsel[:, bass.ds(two * 8 + n, 1)], None, ALU.mult).then_inc(m["i_ws"].sem, 1)

            def chunks(two, prev):
                for n in range(8):
                    pick(two, n)
                    if n in (5, 7) and prev is not None:
                        finish(prev, (n - 5) // 2)
            chunks(0, None)
            with dve.Fori(1, NCHUNK // 2) as two:
                chunks(two, two - 1)
            for p in range(2):
                finish(NCHUNK // 2 - 1, p)
            dve.wait_ge(*m["i_z"](NCHUNK + 2))

            def zstats(g):
                ln_stats(dve, g, U[:, g * TG:(g + 1) * TG, :], m["z_var"])
                dve.wait_ge(*m["z_var"](g + 1))
            zstats(0)
            for g in range(G):
                sl = slice(g * TG, (g + 1) * TG)
                xc = XC[g % 2][:, :, :]
                if g + 1 < G:
                    zstats(g + 1)
                ln_norm_vector(dve, g, m["z_rstd"], m["z_u"], src=U, dst=XC[g % 2])
                vlink(dve.tensor_tensor(xc, xc, bcm(gam[:, :], TG), ALU.mult))
                vlink(dve.tensor_tensor(xc, xc, bcm(bet[:, :], TG), ALU.add))
                dve.tensor_tensor(X[:, sl, :], X[:, sl, :], xc, ALU.add).then_inc(m["x8"].sem, 1)

        def i_scalar(act):
            ln_scalar(act, m["i_rstd"], m["i_u"], m["i_ft_ps"], m["i_ft"], sums=tsum)
            act.wait_ge(*m["i_l"](1))
            act.activation(im[2][:, :], im[1][:, :], ACT.Exp).then_inc(m["i_e"].sem, 1)
            act.wait_ge(*m["i_l2"](1))
            act.activation(im[2][:, :], im[1][:, :], ACT.Exp).then_inc(m["i_e2"].sem, 1)
            act.wait_ge(*m["i_w"](1))
            act.activation(i1[1][:, :], i1[0][:, :], ACT.Exp).then_inc(m["i_we"].sem, 1)
            act.wait_ge(*m["i_ready"](1))
            act.sem_inc(m["i_yc"].sem, 2)
            act.sem_inc(m["i_h"].sem, 4)

            def gelu(two, p):
                for n in range(4):
                    u = 4 * p + n
                    act.wait_ge(*m["i_h_ps"](two * 8 + (u + 1)))
                    act.wait_ge(*m["i_y_ps"](two * 8 + (4 * p + 4)))
                    act.activation(GH[u], ps[:, HB[n], 0:PIX], ACT.Gelu,
                                   bias=b1u[:, n % 2, bass.ds(two * 4 + (2 * p + n // 2), 1)]).then_inc(m["i_h"].sem, 1)

            def move(two, p):
                act.wait_ge(*m["i_y_ps"](two * 8 + (4 * p + 12)))
                act.wait_ge(*m["i_t_ps"](two * 2 + (p + 1)))
                act.activation(YS[p][:, :], ps[:, SUM[p], 0:PIX], ACT.Identity,
                               bias=b2u[:, bass.ds(two * 2 + p, 1)]).then_inc(m["i_yc"].sem, 1)

            def chunks(two, prev):
                for p in range(2):
                    gelu(two, p)
                    move(two, p)
            chunks(0, None)
            with act.Fori(1, NCHUNK // 2) as two:
                chunks(two, None)
            for g in range(G):
                if g >= 2:
                    act.wait_ge(*m["x8"](g - 1))
                ln_norm(act, g, m["z_rstd"], m["z_u"], src=U, dst=XC[g % 2])

        def i_tensor(pe):
            pe.wait_ge(*m["x7"](NCHUNK))
            ln_tensor(pe, m["i_fs"], m["i_ft_ps"], m["i_ft"])
            pe.wait_ge(*m["i_mean"](1))
            wwait(pe, "i8")
            pe.matmul(ps[0:B, 3, 0:E3], mean8[:, :], wr_8[:, :], start=True, stop=True).then_inc(m["i_lg_ps"].sem, 1)
            pe.wait_ge(*m["i_rw"](1))
            pe.matmul(ps[0:B, 3, 0:E3], ones[0:B, 0:B], im[3][:, :], start=True, stop=True).then_inc(m["i_ld_ps"].sem, 1)
            pe.wait_ge(*m["i_top"](1))
            for k in range(2):
                pe.transpose(ps[0:E3, 2, k * B:(k + 1) * B], hot[:, k, :], ident[0:B, 0:B])
            pe.transpose(ps[0:E3, 2, 2 * B:3 * B], im[7][:, :], ident[0:B, 0:B])
            pe.matmul(ps[:, 2, P:P + 4 * B], ones[0:B, :], dia[:, :, :, :].rearrange("p b k v -> p (b k v)"), start=True,
                      stop=True).then_inc(m["i_tr_ps"].sem, 1)
            pe.wait_ge(*m["i_tr"](1))
            pe.matmul(ps[:, 3, 0:2 * B], b1_8[:, :], hotT[:, :, :].rearrange("p k b -> p (k b)"), start=True, stop=True)
            dv = dwT[:, :].rearrange("p (q r) -> p r q", r=2)
            for r in range(2):
                last = pe.matmul(ps[r * C:(r + 1) * C, 3, 2 * B:2 * B + B // 2], b2_8[:, :], dv[:, r, :], start=True, stop=True)
            last.then_inc(m["i_bc_ps"].sem, 1)
            pe.wait_ge(*m["i_ready"](1))
            pe.wait_ge(*m["i_ft"](NCHUNK))
            pe.sem_inc(m["i_y_ps"].sem, 8)
            pe.sem_inc(m["i_t_ps"].sem, 2)

            def hidden(two, p):
                cols = UT[:, bass.ts(two * 2 + p, CHUNK)].rearrange("p (h r s) -> p r h s", h=2, r=2)
                for n in range(4):
                    u = 4 * p + n
                    pe.wait_ge(*m["i_ws"](two * 8 + (u + 1)))
                    pe.wait_ge(*m["i_h"](two * 8 + (u + 1)))
                    for part in range(2):
                        last = pe.matmul(ps[:, HB[n], 0:PIX], W1S[u][:, part, :], cols[:, n // 2, :, :],
                                         start=(part == 0), stop=(part == 1))
                    last.then_inc(m["i_h_ps"].sem, 1)

            def outp(two, p):
                pe.wait_ge(*m["i_yc"](two * 2 + (p + 1)))
                pe.wait_ge(*m["i_h"](two * 8 + (4 * p + 8)))
                for k in range(2):
                    for r in range(2):
                        u = 4 * p + 2 * r + k
                        pe.matmul(ps[r * C:(r + 1) * C, SUM[p], 0:PIX], W2S[u][:, :], GH[u], start=(k == 0),
                                  stop=(k == 1)).then_inc(m["i_y_ps"].sem, 1)

            def back(two, p):
                pe.wait_ge(*m["i_yc"](two * 2 + (p + 3)))
                pe.wait_ge(*m["i_z"](two * 2 + (p + 1)))
                for h in range(2):
                    last = pe.transpose(ps[:, BACK[p], h * P:(h + 1) * P], YS[p][:, h * P:(h + 1) * P], ident[:, :])
                last.then_inc(m["i_t_ps"].sem, 1)

            def chunks(two, prev):
                for p in range(2):
                    hidden(two, p)
                    if prev is not None:
                        back(prev, p)
                    outp(two, p)
            chunks(0, None)
            with pe.Fori(1, NCHUNK // 2) as two:
                chunks(two, two - 1)
            last_two = NCHUNK // 2 - 1
            back(last_two, 0)
            back(last_two, 1)
        x_ready = {7: m["x7"], 8: m["x8"]}[min(stop, LAST)]

        s_ot = sem("o_ps"); s_oc = sem("o_copied"); s_out = sem("o_stored")
        s_fin = x_ready
        XM = 2 if min(stop, LAST) in (4, 6, 7) else 1

        def o_tensor(pe):
            for g in range(G):
                pe.wait_ge(*s_fin((g + 1) * XM))
                if g >= 2:
                    pe.wait_ge(s_oc, g - 1)
                for i in range(4):
                    t = g * TG + 2 * i
                    last = pe.transpose(ps[:, g % 2, i * P:(i + 1) * P], X[:, t:t + 2, :].rearrange("p t c -> p (t c)"), ident[:, :])
                last.then_inc(s_ot, 1)
        OUTB = XIN

        def o_scalar(act):
            for g in range(G):
                act.wait_ge(s_ot, g + 1)
                act.activation(OUTB[:, 2 * g:2 * g + 2, :].rearrange("p q s -> p (q s)"), ps[:, g % 2, :], ACT.Copy).then_inc(s_oc, 1)

        def o_sync(sp):
            ov = out.rearrange("(q r) c h w -> (r c) q (h w)", r=2)
            for g in range(G):
                sp.wait_ge(s_oc, g + 1)
                sp.dma_start(ov[:, 2 * g:2 * g + 2, :], OUTB[:, 2 * g:2 * g + 2, :]).then_inc(s_out, 16)
            sp.wait_ge(s_out, 16 * G)

        block = ctx.enter_context(nc.Block())
        @block.sync
        def _(sp):
            load_sync(sp)
            f_sync(sp)
            v_sync(sp)
            e1_sync(sp)
            d_sync(sp)
            e2_sync(sp)
            q_sync(sp)
            i_sync(sp)
            o_sync(sp)

        @block.gpsimd
        def _(pool):
            consts_pool(pool)
            c0_pool(pool)
            f_pool(pool)
            v_pool(pool)
            e1_pool(pool)
            d_pool(pool)
            e2_pool(pool)
            q_pool(pool)
            i_pool(pool)

        @block.scalar
        def _(act):
            xt_scalar(act)
            c0_scalar(act)
            u_scalar(act)
            t_scalar(act)
            f_scalar(act)
            v_scalar(act)
            e1_whi(act)
            e1_scalar2(act)
            d_scalar(act)
            e2_scalar(act)
            q_scalar(act)
            i_scalar(act)
            o_scalar(act)

        @block.vector
        def _(dve):
            vlink(dve.memset(b2_6[:, :], 0.0))
            w0_vector(dve)
            c0_vector(dve)
            u_vector(dve)
            t_vector(dve)
            f_weights(dve)
            f_vector(dve)
            v_consts(dve)
            v_vector(dve)
            e1_consts(dve)
            e1_vector(dve)
            d_vector(dve)
            e2_vector(dve)
            q_vector(dve)
            i_vector(dve)

        @block.tensor
        def _(pe):
            w0_tensor(pe)
            xt_tensor(pe)
            c0_tensor(pe)
            u_tensor(pe)
            t_tensor(pe)
            f_tensor(pe)
            v_tensor(pe)
            e1_tensor(pe)
            d_tensor(pe)
            e2_tensor(pe)
            q_tensor(pe)
            i_tensor(pe)
            o_tensor(pe)


_OUT = (B, C, H, W)


def kernel(**inputs):
    import numpy as np
    import concourse.bacc as bacc
    from concourse.bass_utils import run_bass_kernel_spmd as run

    nc = bacc.Bacc("TRN2", target_bir_lowering=False, num_devices=1)
    arrays, aps = {}, {}
    for name, value in inputs.items():
        v = np.ascontiguousarray(value)
        arrays["in_" + name] = v
        aps[name] = nc.dram_tensor("in_" + name, v.shape, mybir.dt.from_np(v.dtype), kind="ExternalInput").ap()
    out = nc.dram_tensor("out", _OUT, F32, kind="ExternalOutput").ap()
    build(nc, aps, out)
    return run(nc, [arrays], core_ids=[0]).results[0]["out"]
```
